# Optimizing a Trainium2 kernel written in Bass

```python
import numpy as np
import jax
import jax.numpy as jnp

def _softmax(x, axis=-1):
    return jax.nn.softmax(x, axis=axis)

def _gelu(x):
    return jax.nn.gelu(x, approximate=True)

def _silu(x):
    return jax.nn.silu(x)

def _sigmoid(x):
    return jax.nn.sigmoid(x)

def _layernorm(x, axis=-1, eps=1e-05):
    m = jnp.mean(x, axis=axis, keepdims=True)
    v = jnp.var(x, axis=axis, keepdims=True)
    return (x - m) / jnp.sqrt(v + eps)

def _scatter_add(tgt, idx, src, axis=0):
    return tgt.at[idx].add(src)

def _segment_sum(src, seg, n):
    return jax.ops.segment_sum(src, seg, n)
kernel_name = 'mk_macaron_d2_jaxref_r8_60dccd'

def setup_inputs(seed: int=0):
    np.random.seed(seed)
    _w = jnp.asarray

    def _L0_attn_setup():
        import jax, jax.numpy as jnp
        import numpy as np
        H = 32
        HKV = 8
        D = 512
        HD = D // H
        S = 128
        MASK_OUT = 0.9
        MIN_REMAIN = 128
        THETA = 10000.0

        def rope_tables(seq_len, hd):
            inv_freq = 1.0 / THETA ** (jnp.arange(0, hd, 2, dtype=jnp.float32) / hd)
            t = jnp.arange(seq_len, dtype=jnp.float32)
            freqs = jnp.outer(t, inv_freq)
            emb = jnp.concatenate([freqs, freqs], axis=-1)
            return (jnp.cos(emb), jnp.sin(emb))

        def rotate_half(x):
            x1, x2 = jnp.split(x, 2, axis=-1)
            return jnp.concatenate([-x2, x1], axis=-1)

        def apply_rope(x, cos, sin):
            return x * cos + rotate_half(x) * sin
        key = jax.random.key(seed)
        k0, k1, k2, k3, k4 = jax.random.split(key, 5)
        hidden_states = jax.random.normal(k0, (1, S, D), jnp.float32)
        Wq = jax.random.normal(k1, (D, D), jnp.float32) * 0.02
        Wk = jax.random.normal(k2, (HKV * HD, D), jnp.float32) * 0.02
        Wv = jax.random.normal(k3, (HKV * HD, D), jnp.float32) * 0.02
        Wo = jax.random.normal(k4, (D, D), jnp.float32) * 0.02
        return {'hidden_states': hidden_states, 'Wq': Wq, 'Wk': Wk, 'Wv': Wv, 'Wo': Wo}
    _L0_attn_in = _L0_attn_setup()

    def _L0_ffn_setup():
        import jax, jax.numpy as jnp
        import numpy as np
        NUM_EXPERTS = 8
        RANK = 32
        ALPHA = 16.0
        TOP_K = 2
        TEMPERATURE = 1.0
        GAMMA = 0.5
        SOFT_TOPK_TEMP = 0.5
        N_GRAM = 2
        EPS = 1e-06
        key = jax.random.key(seed)
        ks = jax.random.split(key, 6)
        d_in, d_out = (512, 512)
        Bsz, T = (4, 256)
        x = jax.random.normal(ks[0], (Bsz, T, d_in), dtype=jnp.float32)
        W = jax.random.normal(ks[1], (d_out, d_in), dtype=jnp.float32) / np.sqrt(d_in)
        b = jax.random.normal(ks[2], (d_out,), dtype=jnp.float32) * 0.01
        A = jax.random.normal(ks[3], (d_in, RANK), dtype=jnp.float32) / np.sqrt(d_in)
        Bmat = jax.random.normal(ks[4], (RANK, d_out), dtype=jnp.float32) * 0.01
        LiMEs = jax.random.normal(ks[5], (NUM_EXPERTS, RANK), dtype=jnp.float32) * 0.1
        return {'x': x, 'W': W, 'b': b, 'A': A, 'Bmat': Bmat, 'LiMEs': LiMEs}
    _L0_ffn_in = _L0_ffn_setup()

    def _L1_attn_setup():
        import math
        import jax, jax.numpy as jnp
        import numpy as np

        def _rope_tables(T, h, dtype):
            pos = jnp.arange(T, dtype=jnp.float32)
            thetas = 1.0 / 10000.0 ** (jnp.arange(0, h, 2, dtype=jnp.float32) / h)
            pt = jnp.outer(pos, thetas)
            pt = jnp.concatenate([pt, pt], axis=-1)
            return (jnp.sin(pt).astype(dtype), jnp.cos(pt).astype(dtype))

        def _apply_rope(x, sin, cos):
            h = x.shape[-1]
            rot = jnp.concatenate([-x[..., h // 2:], x[..., :h // 2]], axis=-1)
            return x * cos + rot * sin
        key = jax.random.key(seed)
        ks = jax.random.split(key, 5)
        B, T, C = (2, 256, 512)
        s = 1.0 / math.sqrt(C)
        return {'x': jax.random.normal(ks[0], (B, T, C), dtype=jnp.float32), 'wq': jax.random.normal(ks[1], (C, C), dtype=jnp.float32) * s, 'wk': jax.random.normal(ks[2], (C, C), dtype=jnp.float32) * s, 'wv': jax.random.normal(ks[3], (C, C), dtype=jnp.float32) * s, 'wo': jax.random.normal(ks[4], (C, C), dtype=jnp.float32) * s}
    _L1_attn_in = _L1_attn_setup()

    def _L1_ffn_setup():
        import jax, jax.numpy as jnp
        import numpy as np
        SCALING = 16.0 / 8.0
        GAMMA = 1.0
        EPS = 1e-12
        key = jax.random.key(seed)
        ks = jax.random.split(key, 8)
        B, T, H, O = (4, 256, 512, 512)
        E_tot, E_act, r = (16, 4, 8)
        return {'x': jax.random.normal(ks[0], (B, T, H), jnp.float32), 'W_base': jax.random.normal(ks[1], (O, H), jnp.float32) * 0.02, 'b_base': jax.random.normal(ks[2], (O,), jnp.float32) * 0.02, 'lora_A': jax.random.normal(ks[3], (E_tot, r, H), jnp.float32) * 0.02, 'lora_B': jax.random.normal(ks[4], (E_tot, O, r), jnp.float32) * 0.02, 'router_W': jax.random.normal(ks[5], (E_tot, H), jnp.float32) * 0.02, 'router_b': jax.random.normal(ks[6], (E_tot,), jnp.float32) * 0.02, 'domain_prior': jax.random.uniform(ks[7], (E_tot,), jnp.float32), 'active': jnp.arange(E_act, dtype=jnp.int32)}
    _L1_ffn_in = _L1_ffn_setup()
    _d = {'L0_attn_hidden_states': _L0_attn_in['hidden_states'], 'L0_attn_Wq': _L0_attn_in['Wq'], 'L0_attn_Wk': _L0_attn_in['Wk'], 'L0_attn_Wv': _L0_attn_in['Wv'], 'L0_attn_Wo': _L0_attn_in['Wo'], 'L0_ffn_W': _L0_ffn_in['W'], 'L0_ffn_b': _L0_ffn_in['b'], 'L0_ffn_A': _L0_ffn_in['A'], 'L0_ffn_Bmat': _L0_ffn_in['Bmat'], 'L0_ffn_LiMEs': _L0_ffn_in['LiMEs'], 'L1_attn_wq': _L1_attn_in['wq'], 'L1_attn_wk': _L1_attn_in['wk'], 'L1_attn_wv': _L1_attn_in['wv'], 'L1_attn_wo': _L1_attn_in['wo'], 'L1_ffn_W_base': _L1_ffn_in['W_base'], 'L1_ffn_b_base': _L1_ffn_in['b_base'], 'L1_ffn_lora_A': _L1_ffn_in['lora_A'], 'L1_ffn_lora_B': _L1_ffn_in['lora_B'], 'L1_ffn_router_W': _L1_ffn_in['router_W'], 'L1_ffn_router_b': _L1_ffn_in['router_b'], 'L1_ffn_domain_prior': _L1_ffn_in['domain_prior'], 'L1_ffn_active': _L1_ffn_in['active']}
    _x0 = _d['L0_attn_hidden_states']
    _d['L0_attn_hidden_states'] = jax.random.normal(jax.random.fold_in(jax.random.key(seed), 1), (4, 512, 512), dtype=_x0.dtype)
    del _x0
    return _d

def reference(L0_attn_hidden_states, L0_attn_Wq, L0_attn_Wk, L0_attn_Wv, L0_attn_Wo, L0_ffn_W, L0_ffn_b, L0_ffn_A, L0_ffn_Bmat, L0_ffn_LiMEs, L1_attn_wq, L1_attn_wk, L1_attn_wv, L1_attn_wo, L1_ffn_W_base, L1_ffn_b_base, L1_ffn_lora_A, L1_ffn_lora_B, L1_ffn_router_W, L1_ffn_router_b, L1_ffn_domain_prior, L1_ffn_active):

    def _L0_attn_ref(hidden_states, Wq, Wk, Wv, Wo):
        import jax, jax.numpy as jnp
        import numpy as np
        H = 32
        HKV = 8
        D = 512
        HD = D // H
        S = 128
        MASK_OUT = 0.9
        MIN_REMAIN = 128
        THETA = 10000.0

        def rope_tables(seq_len, hd):
            inv_freq = 1.0 / THETA ** (jnp.arange(0, hd, 2, dtype=jnp.float32) / hd)
            t = jnp.arange(seq_len, dtype=jnp.float32)
            freqs = jnp.outer(t, inv_freq)
            emb = jnp.concatenate([freqs, freqs], axis=-1)
            return (jnp.cos(emb), jnp.sin(emb))

        def rotate_half(x):
            x1, x2 = jnp.split(x, 2, axis=-1)
            return jnp.concatenate([-x2, x1], axis=-1)

        def apply_rope(x, cos, sin):
            return x * cos + rotate_half(x) * sin
        B, Sq, Dm = hidden_states.shape
        dtype = hidden_states.dtype
        neg = jnp.finfo(dtype).min
        q = (hidden_states @ Wq.T).reshape(B, Sq, H, HD).transpose(0, 2, 1, 3)
        k = (hidden_states @ Wk.T).reshape(B, Sq, HKV, HD).transpose(0, 2, 1, 3)
        v = (hidden_states @ Wv.T).reshape(B, Sq, HKV, HD).transpose(0, 2, 1, 3)
        rep = H // HKV
        k = jnp.repeat(k, rep, axis=1)
        v = jnp.repeat(v, rep, axis=1)
        cos, sin = rope_tables(Sq, HD)
        qr = apply_rope(q, cos, sin)
        kr = apply_rope(k, cos, sin)
        draft = jnp.einsum('bhqd,bhkd->bhqk', qr, kr)
        qi = jnp.arange(Sq)
        ki = jnp.arange(Sq)
        causal_future = qi[:, None] < ki[None, :]
        draft = draft + jnp.where(causal_future, neg, jnp.asarray(0.0, dtype))
        num_remain = max(min(Sq, MIN_REMAIN), Sq - int(Sq * MASK_OUT))
        _, draft_indices = jax.lax.top_k(draft, num_remain)
        mask = jnp.full((B, H, Sq, Sq), neg, dtype)
        b_idx = jnp.arange(B)[:, None, None, None]
        h_idx = jnp.arange(H)[None, :, None, None]
        s_idx = jnp.arange(Sq)[None, None, :, None]
        mask = mask.at[b_idx, h_idx, s_idx, draft_indices].set(0.0)
        mask = jnp.where(causal_future[None, None, :, :], neg, mask)
        scores = jnp.einsum('bhqd,bhkd->bhqk', qr, kr) / np.sqrt(HD).astype(np.float32) + mask
        attn = jax.nn.softmax(scores, axis=-1)
        out = jnp.einsum('bhqk,bhkd->bhqd', attn, v)
        out = out.transpose(0, 2, 1, 3).reshape(B, Sq, Dm)
        return out @ Wo.T

    def _L0_ffn_ref(x, W, b, A, Bmat, LiMEs):
        import jax, jax.numpy as jnp
        import numpy as np
        NUM_EXPERTS = 8
        RANK = 32
        ALPHA = 16.0
        TOP_K = 2
        TEMPERATURE = 1.0
        GAMMA = 0.5
        SOFT_TOPK_TEMP = 0.5
        N_GRAM = 2
        EPS = 1e-06
        Bsz, T, d_in = x.shape
        E = LiMEs.shape[0]
        scaling = ALPHA / RANK
        H = jnp.einsum('btd,od->bto', x, W) + b
        z = jnp.einsum('btd,dr->btr', x, A)
        anchors = jnp.arange(N_GRAM - 1, T, N_GRAM)
        H_slice = H[:, anchors, :E]
        delta_slice = jnp.einsum('bar,er->bae', z[:, anchors], LiMEs)
        H_scale = jnp.maximum(jnp.max(jnp.abs(H_slice)), EPS)
        d_scale = jnp.maximum(jnp.max(jnp.abs(delta_slice)), EPS)
        logits = ((1.0 - GAMMA) * (H_slice / H_scale) + GAMMA * (delta_slice / d_scale)) / TEMPERATURE
        probs = jax.nn.softmax(logits, axis=-1)
        topk_vals, _ = jax.lax.top_k(probs, TOP_K)
        thresh = topk_vals[..., -1:]
        mask = jax.nn.sigmoid((probs - thresh) / SOFT_TOPK_TEMP)
        weights = probs * mask
        weights = weights / (jnp.sum(weights, axis=-1, keepdims=True) + 1e-09)
        weights_full = jnp.repeat(weights, N_GRAM, axis=1)
        p_mix = jnp.einsum('bte,er->btr', weights_full, LiMEs)
        delta = jnp.einsum('btr,ro->bto', z * p_mix, Bmat) * scaling
        return H + delta

    def _L1_attn_ref(x, wq, wk, wv, wo):
        import math
        import jax, jax.numpy as jnp
        import numpy as np

        def _rope_tables(T, h, dtype):
            pos = jnp.arange(T, dtype=jnp.float32)
            thetas = 1.0 / 10000.0 ** (jnp.arange(0, h, 2, dtype=jnp.float32) / h)
            pt = jnp.outer(pos, thetas)
            pt = jnp.concatenate([pt, pt], axis=-1)
            return (jnp.sin(pt).astype(dtype), jnp.cos(pt).astype(dtype))

        def _apply_rope(x, sin, cos):
            h = x.shape[-1]
            rot = jnp.concatenate([-x[..., h // 2:], x[..., :h // 2]], axis=-1)
            return x * cos + rot * sin
        B, T, C = x.shape
        n_head = 32
        h = C // n_head

        def proj(w):
            y = jnp.einsum('btc,dc->btd', x, w)
            return y.reshape(B, T, n_head, h).transpose(0, 2, 1, 3)
        q, k, v = (proj(wq), proj(wk), proj(wv))
        sin, cos = _rope_tables(T, h, x.dtype)
        q = _apply_rope(q, sin, cos)
        k = _apply_rope(k, sin, cos)
        scores = jnp.einsum('bnth,bnsh->bnts', q, k) * (1.0 / math.sqrt(h))
        causal = jnp.tril(jnp.ones((T, T), dtype=bool))
        scores = jnp.where(causal, scores, -jnp.inf)
        attn = jax.nn.softmax(scores, axis=-1)
        out = jnp.einsum('bnts,bnsh->bnth', attn, v)
        out = out.transpose(0, 2, 1, 3).reshape(B, T, C)
        return jnp.einsum('btc,dc->btd', out, wo)

    def _L1_ffn_ref(x, W_base, b_base, lora_A, lora_B, router_W, router_b, domain_prior, active):
        import jax, jax.numpy as jnp
        import numpy as np
        SCALING = 16.0 / 8.0
        GAMMA = 1.0
        EPS = 1e-12
        y = jnp.einsum('bth,oh->bto', x, W_base) + b_base
        A = lora_A[active]
        Bm = lora_B[active]
        z = jnp.einsum('bth,erh->bter', x, A)
        contribs = jnp.einsum('bter,eor->bteo', z, Bm) * SCALING
        logits = jnp.einsum('bth,eh->bte', x, router_W) + router_b
        logits = logits[..., active]
        prior = domain_prior[active]
        alpha = jax.nn.softmax(jnp.log(prior + EPS) + logits / GAMMA, axis=-1)
        return y + jnp.einsum('bteo,bte->bto', contribs, alpha)
    x = L0_attn_hidden_states
    x = x + 0.5 * _L0_ffn_ref(_layernorm(x, axis=-1), L0_ffn_W, L0_ffn_b, L0_ffn_A, L0_ffn_Bmat, L0_ffn_LiMEs)
    x = x + _L0_attn_ref(_layernorm(x, axis=-1), L0_attn_Wq, L0_attn_Wk, L0_attn_Wv, L0_attn_Wo)
    x = x + 0.5 * _L0_ffn_ref(_layernorm(x, axis=-1), L0_ffn_W, L0_ffn_b, L0_ffn_A, L0_ffn_Bmat, L0_ffn_LiMEs)
    x = x + 0.5 * _L1_ffn_ref(_layernorm(x, axis=-1), L1_ffn_W_base, L1_ffn_b_base, L1_ffn_lora_A, L1_ffn_lora_B, L1_ffn_router_W, L1_ffn_router_b, L1_ffn_domain_prior, L1_ffn_active)
    x = x + _L1_attn_ref(_layernorm(x, axis=-1), L1_attn_wq, L1_attn_wk, L1_attn_wv, L1_attn_wo)
    x = x + 0.5 * _L1_ffn_ref(_layernorm(x, axis=-1), L1_ffn_W_base, L1_ffn_b_base, L1_ffn_lora_A, L1_ffn_lora_B, L1_ffn_router_W, L1_ffn_router_b, L1_ffn_domain_prior, L1_ffn_active)
    return x

_drawn_inputs = setup_inputs


def setup_inputs(seed=0):
    import zlib

    import numpy as np

    out = dict(_drawn_inputs(seed))
    spreads = {}
    factors = {'L0_attn_Wq': 5.795,
     'L0_attn_Wk': 5.8,
     'L0_ffn_b': 7.526,
     'L0_ffn_A': 8.0,
     'L0_ffn_Bmat': 8.0,
     'L0_ffn_LiMEs': 8.0,
     'L1_ffn_b_base': 4.8,
     'L1_ffn_lora_A': 3.193,
     'L1_ffn_lora_B': 3.243,
     'L1_ffn_router_W': 8.0,
     'L1_ffn_router_b': 47.826,
     'L1_ffn_domain_prior': 8.0}
    for name, (base, spread) in spreads.items():
        noise = np.random.default_rng([zlib.crc32(name.encode()), seed]).standard_normal(out[name].shape)
        drawn = base * np.exp(spread * noise) if base else spread * noise
        out[name] = jnp.asarray(drawn.astype(out[name].dtype))
    for name, factor in factors.items():
        out[name] = (out[name] * factor).astype(out[name].dtype)
    return out
```

```python
from contextlib import ExitStack

import numpy as np

import concourse.bass as bass
from concourse import mybir

F32 = mybir.dt.float32
F32R = mybir.dt.float32r
I32 = mybir.dt.int32
ACT = mybir.ActivationFunctionType
ALU = mybir.AluOpType
AX = mybir.AxisListType
RMAX = bass.bass_isa.ReduceOp.max

P = 128
B, S, D = 4, 512, 512
TB = S // P
NT = B * TB
KT = D // P
LN_EPS = 1e-5

RANK = 32
E0 = 8
NGRAM = 2
E_TOT, E_ACT, R1 = 16, 4, 8
STACK = 128
ONES_AT = 3 * RANK

H, HD = 32, 16
HKV0 = 8
KEEP = 128
GH = 4
NG = H // GH
VW = HD + 1
QK_ROWS = 96
CAUSAL = TB * (TB + 1) // 2 * P
ROW_AT = [P * (t * (t + 1) // 2) for t in range(TB)]
COL_AT = [sum((TB - j) * P for j in range(k)) for k in range(TB)]
NEG = -1.0e30
BISECT = 24


def prod3(pe, out, lhs, rhs, ks, start=True, stop=True):
    n, last = len(ks), None
    for c, k in enumerate(ks):
        (lh, ll), (rh, rl) = lhs(k), rhs(k)
        pe.matmul(out, lh, rh, start=start and c == 0, stop=False)
        pe.matmul(out, lh, rl, start=False, stop=False)
        last = pe.matmul(out, ll, rh, start=False, stop=stop and c == n - 1)
    return last


def hold(eng, passed, sem, value):
    eng.wait_ge(sem, value)
    eng.sem_inc(passed, 1)


class Stage:

    def __init__(self, nc, ctx, name):
        self.nc, self.ctx, self.name = nc, ctx, name
        self.sems = []
        ctx.callback(self.clear)

    def sb(self, name, shape, dt=F32):
        return self.ctx.enter_context(self.nc.sbuf_tensor(f"{self.name}_{name}", shape, dt))

    def ps(self, name, n=512):
        return self.ctx.enter_context(self.nc.psum_tensor(f"{self.name}_{name}", [P, n], F32))

    def sem(self, name):
        self.sems.append(self.nc.alloc_semaphore(f"{self.name}_{name}"))
        return self.sems[-1]

    def clear(self):
        if self.sems:
            self.nc.clear_and_free_semaphores(self.sems)
            self.nc.all_engine_barrier()


class Ring2:

    def __init__(self, st, name, steps):
        self.bank = [st.ps(f"{name}{b}") for b in range(2)]
        self.ready = st.sem(f"{name}_ready")
        self.free = [st.sem(f"{name}_free{b}") for b in range(2)]
        self.steps = steps
        self.per = [(steps + 1) // 2, steps // 2]

    def prime(self, eng):
        for f in self.free:
            eng.sem_inc(f, 1)

    def at_free(self, i, k):
        return self.free[k % 2], i * self.per[k % 2] + k // 2 + 1

    def at_used(self, i, k):
        return self.free[k % 2], i * self.per[k % 2] + k // 2 + 2

    def at_ready(self, i, k):
        return self.ready, i * self.steps + k + 1


def prepare_weights(nc, name, ident, jobs):
    with ExitStack() as ctx:
        st = Stage(nc, ctx, name)
        raw = st.sb("raw", [P, 2, KT, D])
        t = Ring2(st, "wt", len(jobs) * KT)
        loaded = [st.sem("loaded0"), st.sem("loaded1")]
        raw_used = st.sem("raw_used")
        hi_ready = st.sem("hi_ready")
        block = ctx.enter_context(nc.Block())

        @block.sync
        def _(sp):
            for j, (w, n_out, _, _) in enumerate(jobs):
                if j >= 2:
                    sp.wait_ge(raw_used, j - 1)
                sp.dma_start(raw[:, j % 2, 0:n_out // P, :],
                             w.rearrange("(a p) i -> p a i", p=P)).then_inc(loaded[j % 2], 16)

        @block.tensor
        def _(pe):
            for j, (_, n_out, _, _) in enumerate(jobs):
                pe.wait_ge(loaded[j % 2], 16 * (j // 2 + 1))
                for k in range(KT):
                    step = j * KT + k
                    if step >= 2:
                        pe.wait_ge(t.free[step % 2], step // 2)
                    for a in range(n_out // P):
                        last = pe.transpose(t.bank[step % 2][:, a * P:(a + 1) * P],
                                            raw[:, j % 2, a, k * P:(k + 1) * P], ident[:, :])
                    last.then_inc(t.ready, 1)
                pe.drain().then_inc(raw_used, 1)

        @block.scalar
        def _(act):
            for j, (_, n_out, hi, lo) in enumerate(jobs):
                for k in range(KT):
                    step = j * KT + k
                    act.wait_ge(t.ready, step + 1)
                    ins = act.activation(hi[:, k, :], t.bank[step % 2][:, 0:n_out], ACT.Copy)
                    ins.then_inc(hi_ready if lo is not None else t.free[step % 2], 1)

        @block.vector
        def _(dve):
            n_hi = 0
            for j, (_, n_out, hi, lo) in enumerate(jobs):
                for k in range(KT):
                    step = j * KT + k
                    if lo is not None:
                        n_hi += 1
                        dve.wait_ge(hi_ready, n_hi)
                        dve.tensor_tensor(lo[:, k, :], t.bank[step % 2][:, 0:n_out],
                                          hi[:, k, :].bitcast(F32), ALU.subtract).then_inc(t.free[step % 2], 1)


class Norm:

    def __init__(self, st, x, ident, t, xn):
        self.x, self.ident, self.t, self.xn = x, ident, t, xn
        self.hi = st.sb("xT_hi", [P, KT, S], F32R)
        self.lo = st.sb("xT_lo", [P, KT, S], F32R)
        self.stats = st.sb("stats", [P, TB, 6])
        self.mv = st.sb("mv", [P, TB, 2])
        self.ve = st.sb("ve", [P, TB])
        self.sd = st.sb("sd", [P, TB])
        self.rs = st.sb("rs", [P, TB])
        self.var_ready = st.sem("var_ready")
        self.std_ready = st.sem("std_ready")
        self.xn_ready = st.sem("xn_ready")
        self.xn_free = st.sem("xn_free")
        self.hi_ready = st.sem("xhi_ready")
        self.free = st.sem("xT_free")

    def prime(self, eng):
        eng.sem_inc(self.xn_free, 1)
        eng.sem_inc(self.free, 1)

    def vector_norm(self, dve, i):
        for t in range(TB):
            dve.bn_stats(self.stats[:, t, :], self.x[:, TB * i + t, :])
        dve.drain()
        for t in range(TB):
            dve.bn_aggr(self.mv[:, t, :], self.stats[:, t, :])
        dve.drain()
        dve.tensor_scalar(self.ve[:, :], self.mv[:, :, 1], LN_EPS, None, ALU.add).then_inc(self.var_ready, 1)
        dve.wait_ge(self.std_ready, i + 1)
        dve.reciprocal(self.rs[:, :], self.sd[:, :])
        dve.drain()
        dve.wait_ge(self.xn_free, i + 1)
        for t in range(TB):
            dve.tensor_scalar(self.xn[:, t, :], self.x[:, TB * i + t, :], self.mv[:, t, 0:1],
                              self.rs[:, t:t + 1], ALU.subtract, ALU.mult).then_inc(self.xn_ready, 1)

    def tensor_transpose(self, pe, i):
        for t in range(TB):
            pe.wait_ge(self.xn_ready, i * TB + t + 1)
            pe.wait_ge(*self.t.at_free(i, t))
            for k in range(KT):
                last = pe.transpose(self.t.bank[t % 2][:, k * P:(k + 1) * P],
                                    self.xn[:, t, k * P:(k + 1) * P], self.ident[:, :])
            last.then_inc(self.t.ready, 1)

    def scalar_split(self, act, i):
        act.wait_ge(self.var_ready, i + 1)
        act.activation(self.sd[:, :], self.ve[:, :], ACT.Sqrt).then_inc(self.std_ready, 1)
        act.wait_ge(self.free, i + 1)
        for t in range(TB):
            act.wait_ge(*self.t.at_ready(i, t))
            act.activation(self.hi[:, :, t * P:(t + 1) * P], self.t.bank[t % 2][:, :], ACT.Copy)\
               .then_inc(self.hi_ready, 1)

    def vector_split(self, dve, i):
        for t in range(TB):
            dve.wait_ge(self.hi_ready, i * TB + t + 1)
            dve.tensor_tensor(self.lo[:, :, t * P:(t + 1) * P],
                              self.t.bank[t % 2][:, :].rearrange("p (k c) -> p k c", k=KT),
                              self.hi[:, :, t * P:(t + 1) * P].bitcast(F32), ALU.subtract)\
               .then_inc(self.t.free[t % 2], 1)

    def tile(self, t):
        return lambda k: (self.hi[:, k, t * P:(t + 1) * P], self.lo[:, k, t * P:(t + 1) * P])

    def batch(self):
        return lambda k: (self.hi[:, k, :], self.lo[:, k, :])


def ffn_weights(nc, name, ident, consts, kind, w, w_hi, w_lo, small_hi, small_lo, stack, extra, ins):
    with ExitStack() as ctx:
        st = Stage(nc, ctx, name)
        raw = st.sb("raw", [P, D])
        scaled = st.sb("scaled", [P, D])
        rounded = st.sb("rounded", [P, D], F32R)
        rest = st.sb("rest", [P, D])
        bank = st.ps("bank")
        bank2 = st.ps("bank2")
        small = st.sb("small", [P, KT, 48])
        loaded = st.sem("loaded")
        cleared = st.sem("cleared")
        built = st.sem("built")
        turned = st.sem("turned")
        vec = st.sem("vec")
        bias = ins["b"].rearrange("(a o) -> a o", a=1)

        if kind == 0:
            a_raw = st.sb("a_raw", [P, KT, RANK])
            aT = st.sb("aT", [RANK, D])
            limesT = st.sb("limesT", [RANK, E0])
            limes_rep = st.sb("limes_rep", [P, RANK])
            block = ctx.enter_context(nc.Block())

            @block.sync
            def _(sp):
                sp.wait_ge(cleared, 1)
                for r in range(3):
                    sp.dma_start(raw[RANK * r:RANK * (r + 1), :], ins["Bmat"]).then_inc(loaded, 16)
                for r in range(2):
                    sp.dma_start(raw[ONES_AT + r:ONES_AT + r + 1, :], bias).then_inc(loaded, 16)
                sp.dma_start(a_raw[:, :, :], ins["A"].rearrange("(k p) r -> p k r", p=P)).then_inc(loaded, 16)
                with nc.allow_non_contiguous_dma(reason="256 numbers"):
                    sp.dma_start(limesT[:, :], ins["LiMEs"].rearrange("e r -> r e")).then_inc(loaded, 16)
                for n in range(NT):
                    sp.dma_start(limes_rep[E0 * n:E0 * (n + 1), :], ins["LiMEs"]).then_inc(loaded, 16)
                sp.dma_start(extra["bias8"][:, :], bias[:, 0:E0].broadcast_to([P, E0])).then_inc(loaded, 16)

            @block.tensor
            def _(pe):
                pe.wait_ge(loaded, 16 * (8 + NT))
                for k in range(KT):
                    last = pe.transpose(bank[0:RANK, k * P:(k + 1) * P], a_raw[:, k, :], ident[:, :])
                last.then_inc(turned, 1)
                pe.wait_ge(vec, 1)
                for k in range(KT):
                    last = pe.matmul(bank2[:, k * E0:(k + 1) * E0], aT[:, k * P:(k + 1) * P], limesT[:, :],
                                     start=True, stop=True)
                last.then_inc(turned, 1)

            @block.vector
            def _(dve):
                dve.memset(raw[:, :], 0.0).then_inc(cleared, 1)
                dve.wait_ge(loaded, 16 * (8 + NT))
                dve.wait_ge(turned, 1)
                dve.tensor_copy(aT[:, :], bank[0:RANK, :]).then_inc(vec, 1)
                dve.tensor_scalar(scaled[:, :], raw[:, :], consts[:, 0:1], None, ALU.mult)
                dve.tensor_tensor(extra["limes_bd"][:, :, :],
                                  limes_rep[:, :].unsqueeze(1).broadcast_to([P, NT, RANK]),
                                  extra["tile_mask"][:, :].unsqueeze(2).broadcast_to([P, NT, RANK]), ALU.mult)
                dve.tensor_copy(small[:, :, 0:RANK], a_raw[:, :, :])
                dve.wait_ge(turned, 2)
                dve.tensor_copy(small[:, :, RANK + E0:48],
                                bank2[:, 0:KT * E0].rearrange("p (k e) -> p k e", k=KT))
                dve.drain()
                dve.tensor_copy(small_hi[:, :, 0:RANK], small[:, :, 0:RANK])
                dve.tensor_copy(small_hi[:, :, RANK + E0:48], small[:, :, RANK + E0:48])
                dve.tensor_copy(small_hi[:, :, RANK:RANK + E0], w_hi[:, :, 0:E0].bitcast(F32))
                dve.tensor_copy(small_lo[:, :, RANK:RANK + E0], w_lo[:, :, 0:E0].bitcast(F32))
                dve.drain()
                for a, z in ((0, RANK), (RANK + E0, 48)):
                    dve.tensor_tensor(small_lo[:, :, a:z], small[:, :, a:z], small_hi[:, :, a:z].bitcast(F32),
                                      ALU.subtract)
                split_stack(dve, stack, scaled, rounded, rest, consts)
        else:
            lora_a = st.sb("lora_a", [E_TOT * R1, D])
            lora_b = st.sb("lora_b", [P, KT, E_TOT, R1])
            lora_bT = st.sb("lora_bT", [E_TOT * R1, D])
            router = st.sb("router", [E_TOT, D])
            rows = st.sb("rows", [E_TOT, 2])
            rows_wide = st.sb("rows_wide", [E_TOT, 2, P])
            act_i = st.sb("act_i", [P, E_ACT], I32)
            act_f = st.sb("act_f", [P, E_ACT])
            sel_e = st.sb("sel_e", [P, E_ACT])
            sel = st.sb("sel", [P, E_ACT, R1])
            prior_log = st.sb("prior_log", [P, E_ACT])
            prior = st.sb("prior", [P, E_ACT])
            block = ctx.enter_context(nc.Block())

            @block.sync
            def _(sp):
                sp.wait_ge(cleared, 1)
                for r in range(2):
                    sp.dma_start(raw[ONES_AT + r:ONES_AT + r + 1, :], bias).then_inc(loaded, 16)
                sp.dma_start(lora_a[:, :], ins["lora_A"].rearrange("e r h -> (e r) h")).then_inc(loaded, 16)
                for k in range(KT):
                    sp.dma_start(lora_b[:, k, :, :],
                                 ins["lora_B"][:, k * P:(k + 1) * P, :].rearrange("e o r -> o e r"))\
                      .then_inc(loaded, 16)
                sp.dma_start(router[:, :], ins["router_W"]).then_inc(loaded, 16)
                with nc.allow_non_contiguous_dma(reason="16 numbers each"):
                    sp.dma_start(rows[:, 0:1], ins["router_b"].rearrange("(e a) -> e a", a=1)).then_inc(loaded, 16)
                    sp.dma_start(rows[:, 1:2], ins["domain_prior"].rearrange("(e a) -> e a", a=1))\
                      .then_inc(loaded, 16)
                sp.dma_start(act_i[:, :], ins["active"].rearrange("(a j) -> a j", a=1).broadcast_to([P, E_ACT]))\
                  .then_inc(loaded, 16)

            @block.tensor
            def _(pe):
                pe.wait_ge(loaded, 16 * 11)
                for k in range(KT):
                    last = pe.transpose(bank[:, k * P:(k + 1) * P],
                                        lora_b[:, k, :, :].rearrange("p e r -> p (e r)"), ident[:, :])
                last.then_inc(turned, 1)
                pe.wait_ge(vec, 1)
                for k in range(KT):
                    pe.matmul(bank2[:, k * 40:k * 40 + RANK], lora_a[:, k * P:(k + 1) * P],
                              sel[:, :, :].rearrange("p j r -> p (j r)"), start=True, stop=True)
                    pe.matmul(bank2[:, k * 40 + RANK:k * 40 + RANK + E_ACT], router[:, k * P:(k + 1) * P],
                              sel_e[0:E_TOT, :], start=True, stop=True)
                for c in range(2):
                    last = pe.matmul(bank2[:, 160 + 4 * c:164 + 4 * c], rows_wide[:, c, :], sel_e[0:E_TOT, :],
                                     start=True, stop=True)
                last.then_inc(turned, 1)
                pe.wait_ge(vec, 2)
                pe.matmul(bank[0:RANK, :], sel[:, :, :].rearrange("p j r -> p (j r)"), lora_bT[:, :],
                          start=True, stop=True).then_inc(turned, 1)

            @block.scalar
            def _(act):
                act.wait_ge(vec, 3)
                act.activation(prior_log[:, :], prior[:, :], ACT.Ln).then_inc(built, 1)

            @block.vector
            def _(dve):
                dve.memset(raw[:, :], 0.0).then_inc(cleared, 1)
                dve.wait_ge(loaded, 16 * 11)
                dve.tensor_copy(act_f[:, :], act_i[:, :])
                dve.tensor_copy(rows_wide[:, :, :], rows[:, :].unsqueeze(2).broadcast_to([E_TOT, 2, P]))
                dve.drain()
                dve.tensor_scalar(sel_e[:, :], act_f[:, :], consts[:, 3:4], None, ALU.is_equal)
                dve.tensor_scalar(act_f[:, :], act_f[:, :], consts[:, 4:5], None, ALU.is_equal)
                dve.drain()
                dve.tensor_tensor(sel[:, :, :], act_f[:, :].unsqueeze(2).broadcast_to([P, E_ACT, R1]),
                                  consts[:, 8:8 + R1].unsqueeze(1).broadcast_to([P, E_ACT, R1]), ALU.mult)\
                   .then_inc(vec, 1)
                dve.wait_ge(turned, 1)
                dve.tensor_copy(lora_bT[:, :], bank[:, :]).then_inc(vec, 1)
                dve.wait_ge(turned, 2)
                dve.tensor_scalar(prior[:, :], bank2[:, 164:168], 1e-12, None, ALU.add).then_inc(vec, 1)
                dve.tensor_copy(small[:, :, 0:36], bank2[:, 0:160].rearrange("p (k c) -> p k c", c=40)[:, :, 0:36])
                dve.wait_ge(built, 1)
                dve.tensor_tensor(extra["logit_bias"][:, :], bank2[:, 160:164], prior_log[:, :], ALU.add)
                dve.drain()
                dve.tensor_copy(small_hi[:, :, 0:36], small[:, :, 0:36])
                dve.wait_ge(turned, 3)
                for r in range(3):
                    dve.tensor_copy(raw[RANK * r:RANK * (r + 1), :], bank[0:RANK, :])
                dve.drain()
                dve.tensor_tensor(small_lo[:, :, 0:36], small[:, :, 0:36], small_hi[:, :, 0:36].bitcast(F32),
                                  ALU.subtract)
                dve.tensor_scalar(scaled[:, :], raw[:, :], consts[:, 0:1], None, ALU.mult)
                split_stack(dve, stack, scaled, rounded, rest, consts)


def split_stack(dve, stack, scaled, rounded, rest, consts):
    dve.drain()
    dve.tensor_copy(rounded[:, :], scaled[:, :])
    dve.drain()
    dve.tensor_tensor(rest[:, :], scaled[:, :], rounded[:, :].bitcast(F32), ALU.subtract)
    dve.drain()
    dve.tensor_scalar(rest[:, :], rest[:, :], consts[:, 2:3], None, ALU.mult)
    dve.drain()
    dve.scalar_tensor_tensor(out=stack[:, :], in0=rounded[:, :].bitcast(F32), scalar=consts[:, 1:2],
                             in1=rest[:, :], op0=ALU.mult, op1=ALU.add)


def ffn_loop(nc, name, kind, x, ident, w_hi, w_lo, small_hi, small_lo, stack, extra):
    n_small = 48 if kind == 0 else 36
    turns = TB if kind == 0 else 2 * TB
    with ExitStack() as ctx:
        st = Stage(nc, ctx, name)
        t = Ring2(st, "t", turns)
        xn = st.sb("xn", [P, TB, D])
        norm = Norm(st, x, ident, t, xn)
        h = [st.ps(f"h{k}") for k in range(TB)]
        sm = st.ps("sm")
        smv = sm[:, 0:TB * 64].rearrange("p (t c) -> p t c", c=64)
        h_ready = st.sem("h_ready")
        h_free = st.sem("h_free")
        sm_ready = st.sem("sm_ready")
        sm_free = st.sem("sm_free")
        ready0 = st.sem("consts_ready")
        left = st.sb("left", [P, TB, STACK])
        leftT = st.sb("leftT", [P, TB, P], F32R)
        if kind == 1:
            logit = st.sb("logit", [P, TB, E_ACT])
            top = st.sb("top", [P, TB])
            ex = st.sb("ex", [P, TB, E_ACT])
            total = st.sb("total", [P, TB])
            alpha = st.sb("alpha", [P, TB, E_ACT])
            u = st.sb("u", [P, TB, RANK])
            logit_ready = st.sem("logit_ready")
            ex_ready = st.sem("ex_ready")
            left_ready = st.sem("left_ready")
            left_free = st.sem("left_free")
            out = extra.get("out")
            stored = st.sem("stored")
            passed = st.sem("passed")
        block = ctx.enter_context(nc.Block())

        @block.tensor
        def _(pe):
            t.prime(pe)
            pe.wait_ge(ready0, 1)
            with pe.Fori(0, B) as i:
                norm.tensor_transpose(pe, i)
                pe.wait_ge(sm_free, i + 1)
                for k in range(TB):
                    pe.wait_ge(*t.at_used(i, k))
                    last = prod3(pe, smv[:, k, 0:n_small], norm.tile(k),
                                 lambda c: (small_hi[:, c, 0:n_small], small_lo[:, c, 0:n_small]), range(KT))
                last.then_inc(sm_ready, 1)
                for k in range(TB):
                    pe.wait_ge(h_free, i * TB + k + 1)
                    prod3(pe, h[k][:, :], norm.tile(k), lambda c: (w_hi[:, c, :], w_lo[:, c, :]), range(KT),
                          stop=False)
                    if kind == 0:
                        pe.matmul(h[k][:, :], leftT[:, 0, :], stack[:, :], start=False, stop=True)\
                          .then_inc(h_ready, 1)
                pe.drain().then_inc(norm.free, 1)
                if kind == 1:
                    for k in range(TB):
                        pe.wait_ge(left_ready, i * TB + k + 1)
                        pe.wait_ge(*t.at_free(i, TB + k))
                        pe.transpose(t.bank[k % 2][:, 0:P], left[:, k, :], ident[:, :]).then_inc(t.ready, 1)
                    pe.drain().then_inc(norm.xn_free, 1)
                    for k in range(TB):
                        pe.wait_ge(*t.at_used(i, TB + k))
                        pe.matmul(h[k][:, :], leftT[:, k, :], stack[:, :], start=False, stop=True)\
                          .then_inc(h_ready, 1)
                    pe.drain().then_inc(left_free, 1)
                else:
                    pe.drain().then_inc(norm.xn_free, 1)

        @block.scalar
        def _(act):
            norm.prime(act)
            act.sem_inc(sm_free, 1)
            act.sem_inc(h_free, TB)
            if kind == 1:
                act.sem_inc(left_free, 1)
            with act.Fori(0, B) as i:
                norm.scalar_split(act, i)
                if kind == 0:
                    act.wait_ge(sm_ready, i + 1)
                    act.activation(extra["small"][:, bass.ds(TB * i, TB), :], smv[:, :, 0:n_small], ACT.Copy)\
                       .then_inc(sm_free, 1)
                else:
                    act.wait_ge(logit_ready, i + 1)
                    act.activation(ex[:, :, :], logit[:, :, :], ACT.Exp).then_inc(ex_ready, 1)
                    act.wait_ge(left_free, i + 1)
                    for k in range(TB):
                        act.wait_ge(*t.at_ready(i, TB + k))
                        act.activation(leftT[:, k, :], t.bank[k % 2][:, 0:P], ACT.Copy)\
                           .then_inc(t.free[k % 2], 1)

        @block.vector
        def _(dve):
            dve.memset(left[:, :, :], 0.0)
            dve.drain()
            dve.memset(left[:, :, ONES_AT:ONES_AT + 2], 1.0)
            if kind == 0:
                ones = left[:, 1, :]
                dve.drain()
                dve.memset(ones, 0.0)
                dve.drain()
                dve.memset(left[ONES_AT:P, 1, :], 1.0)
                dve.drain()
                dve.tensor_copy(leftT[:, 0, :], ones).then_inc(ready0, 1)
            else:
                dve.drain().then_inc(ready0, 1)
            with dve.Fori(0, B) as i:
                norm.vector_norm(dve, i)
                norm.vector_split(dve, i)
                if kind == 1:
                    dve.wait_ge(sm_ready, i + 1)
                    dve.tensor_tensor(logit[:, :, :], smv[:, :, RANK:RANK + E_ACT],
                                      extra["logit_bias"][:, :].unsqueeze(1).broadcast_to([P, TB, E_ACT]), ALU.add)
                    dve.drain()
                    dve.tensor_reduce(top[:, :], logit[:, :, :], AX.X, ALU.max)
                    dve.drain()
                    dve.tensor_tensor(logit[:, :, :], logit[:, :, :],
                                      top[:, :].unsqueeze(2).broadcast_to([P, TB, E_ACT]), ALU.subtract)\
                       .then_inc(logit_ready, 1)
                    dve.wait_ge(ex_ready, i + 1)
                    dve.tensor_reduce(total[:, :], ex[:, :, :], AX.X, ALU.add)
                    dve.drain()
                    dve.reciprocal(total[:, :], total[:, :])
                    dve.drain()
                    dve.tensor_tensor(alpha[:, :, :], ex[:, :, :],
                                      total[:, :].unsqueeze(2).broadcast_to([P, TB, E_ACT]), ALU.mult)
                    dve.drain()
                    for k in range(TB):
                        dve.tensor_tensor(u[:, k, :].rearrange("p (e r) -> p e r", e=E_ACT),
                                          smv[:, k, 0:RANK].rearrange("p (e r) -> p e r", e=E_ACT),
                                          alpha[:, k, :].unsqueeze(2).broadcast_to([P, E_ACT, R1]), ALU.mult)
                    dve.drain().then_inc(sm_free, 1)
                    dve.wait_ge(left_free, i + 1)
                    dve.tensor_copy(left[:, :, 0:RANK].bitcast(F32R), u[:, :, :])
                    dve.drain()
                    dve.tensor_copy(left[:, :, 2 * RANK:3 * RANK], left[:, :, 0:RANK])
                    dve.tensor_tensor(left[:, :, RANK:2 * RANK], u[:, :, :], left[:, :, 0:RANK], ALU.subtract)
                    dve.drain().then_inc(left_ready, TB)
                for k in range(TB):
                    dve.wait_ge(h_ready, i * TB + k + 1)
                    dve.scalar_tensor_tensor(out=x[:, TB * i + k, :], in0=h[k][:, :], scalar=0.5,
                                             in1=x[:, TB * i + k, :], op0=ALU.mult, op1=ALU.add)\
                       .then_inc(h_free, 1)

        if kind == 1 and out is not None:
            @block.sync
            def _(sp):
                with sp.Fori(0, B) as i:
                    hold(sp, passed, h_free, (i + 2) * TB)
                    sp.dma_start(out[i, :, :].rearrange("(t p) c -> p t c", p=P),
                                 x[:, bass.ds(TB * i, TB), :]).then_inc(stored, 16)
                sp.wait_ge(stored, 16 * B)


def ffn0_route(nc, name, x, ident, stack, extra):
    with ExitStack() as ctx:
        st = Stage(nc, ctx, name)
        small = extra["small"]
        t = Ring2(st, "t", TB)
        h = Ring2(st, "h", TB)
        pre = st.ps("pre")
        pre2 = st.ps("pre2")
        anchor = st.sb("anchor", [P, NT, 2 * E0])
        peak = st.sb("peak", [P, 2])
        peak_all = st.sb("peak_all", [P, 2])
        probs = st.sb("probs", [P, NT, E0])
        gate = st.sb("gate", [P, NT, E0])
        top8 = st.sb("top8", [P, NT, 8])
        row = st.sb("row", [P, NT])
        wT = st.sb("wT", [P, P])
        u = st.sb("u", [P, NT, RANK])
        left = st.sb("left", [P, TB, STACK])
        leftT = st.sb("leftT", [P, TB, P], F32R)
        copied = st.sem("copied")
        peak_ready = st.sem("peak_ready")
        peak_all_ready = st.sem("peak_all_ready")
        arg_ready = st.sem("arg_ready")
        exp_ready = st.sem("exp_ready")
        w_ready = st.sem("w_ready")
        wT_ready = st.sem("wT_ready")
        mix_ready = st.sem("mix_ready")
        turned = st.sem("turned")
        left_ready = st.sem("left_ready")
        left_free = st.sem("left_free")
        leftT_free = st.sem("leftT_free")
        block = ctx.enter_context(nc.Block())

        @block.gpsimd
        def _(pool):
            pool.wait_ge(peak_ready, 1)
            pool.partition_all_reduce(peak_all[:, :], peak[:, :], P, RMAX).then_inc(peak_all_ready, 1)

        @block.scalar
        def _(act):
            act.sem_inc(left_free, 1)
            act.sem_inc(leftT_free, TB)
            act.wait_ge(arg_ready, 1)
            act.activation(probs[:, :, :], probs[:, :, :], ACT.Exp).then_inc(exp_ready, 1)
            act.wait_ge(arg_ready, 2)
            act.activation(gate[:, :, :], gate[:, :, :], ACT.Exp, scale=-2.0).then_inc(exp_ready, 1)
            act.wait_ge(turned, 1)
            act.activation(wT[:, :], pre[:, 0:P], ACT.Copy).then_inc(wT_ready, 1)
            with act.Fori(0, B) as i:
                for k in range(TB):
                    act.wait_ge(leftT_free, i * TB + k + 1)
                    act.wait_ge(*t.at_ready(i, k))
                    act.activation(leftT[:, k, :], t.bank[k % 2][:, 0:P], ACT.Copy).then_inc(t.free[k % 2], 1)

        @block.tensor
        def _(pe):
            t.prime(pe)
            h.prime(pe)
            pe.wait_ge(w_ready, 1)
            pe.transpose(pre[:, 0:P], probs[:, :, :].rearrange("p n e -> p (n e)"), ident[:, :])\
              .then_inc(turned, 1)
            pe.wait_ge(wT_ready, 1)
            pe.matmul(pre2[:, :], wT[:, :], extra["limes_bd"][:, :, :].rearrange("p n r -> p (n r)"),
                      start=True, stop=True).then_inc(mix_ready, 1)
            with pe.Fori(0, B) as i:
                pe.wait_ge(left_ready, i + 1)
                for k in range(TB):
                    pe.wait_ge(*t.at_free(i, k))
                    pe.transpose(t.bank[k % 2][:, 0:P], left[:, k, :], ident[:, :]).then_inc(t.ready, 1)
                pe.drain().then_inc(left_free, 1)
                for k in range(TB):
                    pe.wait_ge(*t.at_used(i, k))
                    pe.wait_ge(*h.at_free(i, k))
                    pe.matmul(h.bank[k % 2][:, :], leftT[:, k, :], stack[:, :], start=True, stop=True)\
                      .then_inc(h.ready, 1)
                pe.drain().then_inc(leftT_free, TB)

        @block.vector
        def _(dve):
            dve.memset(left[:, :, :], 0.0)
            dve.stream_shuffle(anchor[:, :, :], small[:, :, RANK:48], [q | (NGRAM - 1) for q in range(32)])
            dve.drain()
            dve.tensor_tensor(anchor[:, :, 0:E0], anchor[:, :, 0:E0],
                              extra["bias8"][:, :].unsqueeze(1).broadcast_to([P, NT, E0]), ALU.add)
            dve.drain()
            for c in range(2):
                dve.tensor_reduce(peak[:, c:c + 1], anchor[:, :, c * E0:(c + 1) * E0], AX.XY, ALU.max,
                                  apply_absolute_value=True)
            dve.drain().then_inc(peak_ready, 1)
            dve.wait_ge(peak_all_ready, 1)
            dve.tensor_scalar(peak[:, :], peak_all[:, :], 1e-6, None, ALU.max)
            dve.drain()
            dve.reciprocal(peak[:, :], peak[:, :])
            dve.drain()
            dve.tensor_scalar(peak[:, :], peak[:, :], 0.5, None, ALU.mult)
            dve.drain()
            dve.tensor_scalar(probs[:, :, :], anchor[:, :, 0:E0], peak[:, 0:1], None, ALU.mult)
            dve.drain()
            dve.scalar_tensor_tensor(out=probs[:, :, :], in0=anchor[:, :, E0:2 * E0], scalar=peak[:, 1:2],
                                     in1=probs[:, :, :], op0=ALU.mult, op1=ALU.add)
            dve.drain()
            dve.tensor_reduce(row[:, :], probs[:, :, :], AX.X, ALU.max)
            dve.drain()
            wide = row[:, :].unsqueeze(2).broadcast_to([P, NT, E0])
            dve.tensor_tensor(probs[:, :, :], probs[:, :, :], wide, ALU.subtract).then_inc(arg_ready, 1)
            dve.wait_ge(exp_ready, 1)
            dve.tensor_reduce(row[:, :], probs[:, :, :], AX.X, ALU.add)
            dve.drain()
            dve.reciprocal(row[:, :], row[:, :])
            dve.drain()
            dve.tensor_tensor(probs[:, :, :], probs[:, :, :], wide, ALU.mult)
            dve.drain()
            for n in range(NT):
                dve.max(top8[:, n, :], probs[:, n, :])
            dve.drain()
            dve.tensor_tensor(gate[:, :, :], probs[:, :, :], top8[:, :, 1:2].broadcast_to([P, NT, E0]),
                              ALU.subtract).then_inc(arg_ready, 1)
            dve.wait_ge(exp_ready, 2)
            dve.tensor_scalar(gate[:, :, :], gate[:, :, :], 1.0, None, ALU.add)
            dve.drain()
            dve.reciprocal(gate[:, :, :], gate[:, :, :])
            dve.drain()
            dve.tensor_tensor(probs[:, :, :], probs[:, :, :], gate[:, :, :], ALU.mult)
            dve.drain()
            dve.tensor_reduce(row[:, :], probs[:, :, :], AX.X, ALU.add)
            dve.drain()
            dve.tensor_scalar(row[:, :], row[:, :], 1e-9, None, ALU.add)
            dve.drain()
            dve.reciprocal(row[:, :], row[:, :])
            dve.drain()
            dve.tensor_tensor(probs[:, :, :], probs[:, :, :], wide, ALU.mult).then_inc(w_ready, 1)
            dve.wait_ge(mix_ready, 1)
            dve.tensor_tensor(u[:, :, :], small[:, :, 0:RANK],
                              pre2[:, :].rearrange("p (n r) -> p n r", n=NT), ALU.mult)
            dve.drain()
            with dve.Fori(0, B) as i:
                dve.wait_ge(left_free, i + 1)
                now = u[:, bass.ds(TB * i, TB), :]
                dve.tensor_copy(left[:, :, 0:RANK].bitcast(F32R), now)
                dve.drain()
                dve.tensor_copy(left[:, :, 2 * RANK:3 * RANK], left[:, :, 0:RANK])
                dve.tensor_tensor(left[:, :, RANK:2 * RANK], now, left[:, :, 0:RANK], ALU.subtract)\
                   .then_inc(left_ready, 1)
                for k in range(TB):
                    dve.wait_ge(*h.at_ready(i, k))
                    dve.scalar_tensor_tensor(out=x[:, TB * i + k, :], in0=h.bank[k % 2][:, :], scalar=0.5,
                                             in1=x[:, TB * i + k, :], op0=ALU.mult, op1=ALU.add)\
                       .then_inc(h.free[k % 2], 1)


def attention(nc, name, kind, x, ident, a):
    pre = f"L{kind}_attn_"
    names = ("Wq", "Wk", "Wv", "Wo") if kind == 0 else ("wq", "wk", "wv", "wo")
    wq, wk, wv, wo = (a[pre + n] for n in names)
    nkv = HKV0 if kind == 0 else H
    kvd = nkv * HD
    with ExitStack() as ctx:
        st = Stage(nc, ctx, name)
        wq_s = (st.sb("wq_hi", [P, KT, D], F32R), st.sb("wq_lo", [P, KT, D], F32R))
        wk_s = (st.sb("wk_hi", [P, KT, kvd], F32R), st.sb("wk_lo", [P, KT, kvd], F32R))
        wv_s = (st.sb("wv_hi", [P, KT, kvd], F32R), st.sb("wv_lo", [P, KT, kvd], F32R))
        wo_s = st.sb("wo", [P, KT, D])
        prepare_weights(nc, name + "w", ident, [(wq, D, *wq_s), (wk, kvd, *wk_s), (wv, kvd, *wv_s),
                                                (wo, D, wo_s, None)])
        attention_loop(nc, name + "l", kind, x, ident, a, wq_s, wk_s, wv_s, wo_s)


def attention_loop(nc, name, kind, x, ident, a, wq, wk, wv, wo):
    nkv = HKV0 if kind == 0 else H
    kvd = nkv * HD
    lag = 4 if kind == 0 else 2
    T_STEPS = TB + NG * (GH * TB + 1) + TB
    t_prob = lambda n, k: TB + (n // GH) * (GH * TB + 1) + (n % GH) * TB + k
    t_out = lambda g: TB + g * (GH * TB + 1) + GH * TB
    t_last = lambda k: TB + NG * (GH * TB + 1) + k
    if kind == 0:
        m_k, m_q = (lambda m: TB), (lambda m: TB + 1 + m)
        m_last = lambda k: TB + 1 + KT + k
        M_STEPS = 2 * TB + 1 + KT
    else:
        m_q, m_k = (lambda m: TB + 2 * m), (lambda m: TB + 2 * m + 1)
        m_last = lambda k: TB + 2 * KT + k
        M_STEPS = 2 * TB + 2 * KT
    on_act = (0, 1, 2, 3) if kind == 0 else (1, 2)
    per_group = 16 * 3 * GH * (1 if kind == 0 else 2)

    with ExitStack() as ctx:
        st = Stage(nc, ctx, name)
        t = Ring2(st, "t", T_STEPS)
        m = Ring2(st, "m", M_STEPS)
        s = Ring2(st, "s", H * TB)
        o = Ring2(st, "o", NG)
        xn = st.sb("xn", [P, TB, D])
        norm = Norm(st, x, ident, t, xn)
        cos, sin = st.sb("cos", [P, S]), st.sb("sin", [P, S])
        causal = st.sb("causal", [P, S])
        turned = st.sb("turned", [P, S])
        roped = st.sb("roped", [P, S])
        qk_hi = [st.sb(f"{n}_hi", [P, S], F32R) for n in "qk"]
        qk_lo = [st.sb(f"{n}_lo", [P, S], F32R) for n in "qk"]
        q_stack = st.sb("q_stack", [QK_ROWS, 2, GH, S], F32R)
        k_stack = st.sb("k_stack", [QK_ROWS, 2, GH, S], F32R)
        v_ones = st.sb("v_ones", [P, TB, nkv, VW])
        sc = st.sb("sc", [P, lag, CAUSAL])
        top = st.sb("top", [P, lag, TB])
        shift = st.sb("shift", [P, lag, TB])
        probT = st.sb("probT", [P, GH, CAUSAL])
        osb = st.sb("osb", [P, S])
        recip = st.sb("recip", [P, TB, GH])
        oT = sc[:, :, :].rearrange("p l c -> p (l c)")[:, 0:KT * S].rearrange("p (k c) -> p k c", k=KT)
        tables_loaded = st.sem("tables_loaded")
        loaded = [st.sem("stack_loaded0"), st.sem("stack_loaded1")]
        stack_free = st.sem("stack_free")
        sp_passed, dve_passed = st.sem("sp_passed"), st.sem("dve_passed")
        roped_ready = [st.sem("q_ready"), st.sem("k_ready")]
        shift_ready = st.sem("shift_ready")
        exp_ready = st.sem("exp_ready")
        if kind == 0:
            k_loaded = st.sem("k_loaded")
            k_free = st.sem("k_free")
            ex = st.sb("ex", [P, 2, CAUSAL])
            sel_ready = st.sem("sel_ready")
            low, high, mid, cnt, cond = (st.sb(n, [P, GH, TB - 1]) for n in ("low", "high", "mid", "cnt", "cond"))
            thr = st.sb("thr", [P, GH, TB])
            junk = st.sb("junk", [P, GH * (TB - 1), S], mybir.dt.bfloat16)
        prob_ready = sel_ready if kind == 0 else exp_ready
        block = ctx.enter_context(nc.Block())

        @block.sync
        def _(sp):
            sp.dma_start(cos[:, :], a["c_cos"]).then_inc(tables_loaded, 16)
            sp.dma_start(sin[:, :], a["c_sin"]).then_inc(tables_loaded, 16)
            sp.dma_start(causal[:, :], a["c_causal"]).then_inc(tables_loaded, 16)

            def restack(which, j, rows, dst, sem):
                hi, lo = qk_hi[which], qk_lo[which]
                for r, src in enumerate((hi, lo, hi) if which == 0 else (hi, hi, lo)):
                    sp.dma_start(dst[HD * r:HD * (r + 1), :].bitcast(F32),
                                 src[HD * j:HD * (j + 1), :].bitcast(F32)).then_inc(sem, 16)

            with sp.Fori(0, B) as i:
                if kind == 0:
                    hold(sp, sp_passed, roped_ready[1], i + 1)
                    hold(sp, sp_passed, k_free, i + 1)
                    for j in range(nkv):
                        restack(1, j, None, k_stack[:, j // GH, j % GH, :], k_loaded)
                for c in range(KT):
                    hold(sp, sp_passed, roped_ready[0], i * KT + c + 1)
                    if kind == 1:
                        hold(sp, sp_passed, roped_ready[1], i * KT + c + 1)
                    for g in (2 * c, 2 * c + 1):
                        hold(sp, sp_passed, stack_free, i * NG + g + 1)
                        for j in range(GH):
                            restack(0, (g % 2) * GH + j, None, q_stack[:, g % 2, j, :], loaded[g % 2])
                            if kind == 1:
                                restack(1, (g % 2) * GH + j, None, k_stack[:, g % 2, j, :], loaded[g % 2])

        @block.tensor
        def _(pe):
            t.prime(pe)
            m.prime(pe)
            s.prime(pe)

            def project(i, c, which):
                w = (wq, wk)[which]
                step = (m_q, m_k)[which](c)
                pe.wait_ge(*m.at_free(i, step))
                prod3(pe, m.bank[step % 2][:, :], lambda k: (w[0][:, k, c * P:(c + 1) * P], w[1][:, k, c * P:(c + 1) * P]),
                      norm.batch(), range(KT)).then_inc(m.ready, 1)

            def scores(i, n):
                g, h = n // GH, n % GH
                if h == 0:
                    pe.wait_ge(loaded[g % 2], (i * (NG // 2) + g // 2 + 2) * per_group)
                for q in range(TB):
                    step = n * TB + q
                    pe.wait_ge(*s.at_free(i, step))
                    kk = k_stack[:, g // GH, g % GH, :] if kind == 0 else k_stack[:, g % 2, h, :]
                    pe.matmul(s.bank[step % 2][:, 0:(q + 1) * P], q_stack[:, g % 2, h, q * P:(q + 1) * P],
                              kk[:, 0:(q + 1) * P], start=True, stop=True).then_inc(s.ready, 1)
                if h == GH - 1:
                    pe.drain().then_inc(stack_free, 1)

            def turn_probs(i, n):
                pe.wait_ge(prob_ready, i * H + n + 1)
                for k in range(TB):
                    step = t_prob(n, k)
                    pe.wait_ge(*t.at_free(i, step))
                    for q in range(k, TB):
                        last = pe.transpose(t.bank[step % 2][:, (q - k) * P:(q - k + 1) * P],
                                            sc[:, n % lag, ROW_AT[q] + k * P:ROW_AT[q] + (k + 1) * P], ident[:, :])
                    last.then_inc(t.ready, 1)

            def weigh(i, g):
                for k in (TB - 2, TB - 1):
                    pe.wait_ge(*t.at_used(i, t_prob(GH * g + GH - 1, k)))
                pe.wait_ge(*o.at_free(i, g))
                for k in range(TB):
                    for h in range(GH):
                        kv = g if kind == 0 else GH * g + h
                        last = pe.matmul(o.bank[g % 2][32 * h:32 * h + VW, k * P:S], v_ones[:, k, kv, :],
                                         probT[:, h, COL_AT[k]:COL_AT[k] + (TB - k) * P],
                                         start=k == 0, stop=k == TB - 1, skip_group_check=True)
                last.then_inc(o.ready, 1)

            def turn_out(i, g):
                pe.wait_ge(*o.at_used(i, g))
                pe.wait_ge(*t.at_free(i, t_out(g)))
                for q in range(TB):
                    last = pe.transpose(t.bank[t_out(g) % 2][:, q * P:(q + 1) * P], osb[:, q * P:(q + 1) * P],
                                        ident[:, :])
                last.then_inc(t.ready, 1)

            with pe.Fori(0, B) as i:
                norm.tensor_transpose(pe, i)
                for k in range(TB):
                    pe.wait_ge(*t.at_used(i, k))
                    pe.wait_ge(*m.at_free(i, k))
                    prod3(pe, m.bank[k % 2][:, 0:kvd], norm.tile(k), lambda c: (wv[0][:, c, :], wv[1][:, c, :]),
                          range(KT)).then_inc(m.ready, 1)
                if kind == 0:
                    project(i, 0, 1)
                project(i, 0, 0)
                if kind == 1:
                    project(i, 0, 1)
                else:
                    pe.wait_ge(k_loaded, (i + 1) * 16 * 3 * nkv)
                for n in range(H + lag):
                    done = n - lag
                    if done >= 0:
                        turn_probs(i, done)
                        if done % GH == GH - 1:
                            weigh(i, done // GH)
                    if n < H:
                        scores(i, n)
                    if done >= 0 and done % GH == GH - 1:
                        turn_out(i, done // GH)
                    if n % 8 == 4 and n < H and n // 8 + 1 < KT:
                        project(i, n // 8 + 1, 0)
                        if kind == 1:
                            project(i, n // 8 + 1, 1)
                        if n // 8 + 2 == KT:
                            pe.drain().then_inc(norm.free, 1)
                    if kind == 0 and n == H - 1:
                        pe.drain().then_inc(k_free, 1)
                pe.wait_ge(*t.at_used(i, t_out(NG - 1)))
                for k in range(TB):
                    pe.wait_ge(*t.at_free(i, t_last(k)))
                    for c in range(KT):
                        last = pe.transpose(t.bank[t_last(k) % 2][:, c * P:(c + 1) * P],
                                            xn[:, k, c * P:(c + 1) * P], ident[:, :])
                    last.then_inc(t.ready, 1)
                pe.drain().then_inc(norm.xn_free, 1)
                for k in range(TB):
                    pe.wait_ge(*t.at_used(i, t_last(k)))
                    pe.wait_ge(*m.at_free(i, m_last(k)))
                    for c in range(KT):
                        last = pe.matmul(m.bank[m_last(k) % 2][:, :], oT[:, c, k * P:(k + 1) * P], wo[:, c, :],
                                         start=c == 0, stop=c == KT - 1)
                    last.then_inc(m.ready, 1)

        def move_probs(eng, copy, i, n, tiles):
            g = n // GH
            for k in tiles:
                step = t_prob(n, k)
                if n % GH == 0 and g >= 1:
                    eng.wait_ge(*o.at_ready(i, g - 1))
                eng.wait_ge(*t.at_ready(i, step))
                copy(probT[:, n % GH, COL_AT[k]:COL_AT[k] + (TB - k) * P],
                     t.bank[step % 2][:, 0:(TB - k) * P]).then_inc(t.free[step % 2], 1)

        @block.scalar
        def _(act):
            norm.prime(act)
            if kind == 0:
                act.sem_inc(k_free, 1)
            copy = lambda out, in_: act.activation(out, in_, ACT.Copy)

            def exps(i, n):
                act.wait_ge(shift_ready, i * H + n + 1)
                if kind == 0 and n >= 2:
                    act.wait_ge(sel_ready, i * H + n - 1)
                for q in range(TB):
                    src = sc[:, n % lag, ROW_AT[q]:ROW_AT[q] + (q + 1) * P]
                    dst = src if kind == 1 else ex[:, n % 2, ROW_AT[q]:ROW_AT[q] + (q + 1) * P]
                    last = act.activation(dst, src, ACT.Exp, bias=shift[:, n % lag, q:q + 1], scale=HD ** -0.5)
                last.then_inc(exp_ready, 1)

            with act.Fori(0, B) as i:
                norm.scalar_split(act, i)
                for k in range(TB):
                    act.wait_ge(*m.at_ready(i, k))
                    copy(v_ones[:, k, :, 0:HD], m.bank[k % 2][:, 0:kvd].rearrange("p (h d) -> p h d", d=HD))\
                        .then_inc(m.free[k % 2], 1)
                for n in range(H + lag):
                    done = n - lag
                    if done >= 0:
                        move_probs(act, copy, i, done, on_act)
                        if done % GH == GH - 1:
                            g = done // GH
                            act.wait_ge(*o.at_ready(i, g))
                            if g >= 1:
                                act.wait_ge(*t.at_ready(i, t_out(g - 1)))
                            copy(osb[:, :], o.bank[g % 2][:, :]).then_inc(o.free[g % 2], 1)
                    if kind == 1 and n < H:
                        exps(i, n)
                    if kind == 0 and n < H and n % GH == GH - 1:
                        for nn in range(n - GH + 1, n + 1):
                            exps(i, nn)
                for k in range(TB):
                    act.wait_ge(*t.at_ready(i, t_last(k)))
                    copy(oT[:, :, k * P:(k + 1) * P],
                         t.bank[t_last(k) % 2][:, :].rearrange("p (k c) -> p k c", k=KT))\
                        .then_inc(t.free[t_last(k) % 2], 1)

        @block.vector
        def _(dve):
            dve.memset(q_stack[:, :, :, :].bitcast(F32), 0.0)
            dve.memset(k_stack[:, :, :, :].bitcast(F32), 0.0)
            dve.memset(v_ones[:, :, :, HD:VW], 1.0)
            if kind == 0:
                dve.memset(thr[:, :, :], NEG / 2)
            for b in range(2):
                dve.memset(o.bank[b][:, :], 0.0)
            dve.drain().then_inc(stack_free, 2)
            o.prime(dve)
            for b in range(2):
                dve.sem_inc(loaded[b], per_group)
            dve.wait_ge(tables_loaded, 48)

            def rope(i, c, which):
                step = (m_q, m_k)[which](c)
                bank = m.bank[step % 2]
                dve.drain()
                dve.wait_ge(*m.at_ready(i, step))
                dve.tensor_tensor(roped[:, :], bank[:, :], cos[:, :], ALU.mult)
                dve.stream_shuffle(turned[:, :], bank[:, :], [p ^ (HD // 2) for p in range(32)])\
                   .then_inc(m.free[step % 2], 1)
                dve.drain()
                dve.tensor_tensor(turned[:, :], turned[:, :], sin[:, :], ALU.mult)
                dve.drain()
                dve.tensor_tensor(roped[:, :], roped[:, :], turned[:, :], ALU.add)
                dve.drain()
                if kind == 0 and which == 1:
                    pass
                else:
                    for b in range(2):
                        dve.wait_ge(loaded[b], (i * KT + c + 1) * per_group)
                dve.tensor_copy(qk_hi[which][:, :], roped[:, :])
                dve.drain()
                dve.tensor_tensor(qk_lo[which][:, :], roped[:, :], qk_hi[which][:, :].bitcast(F32), ALU.subtract)\
                   .then_inc(roped_ready[which], 1)

            def row_max(i, n):
                if n >= lag:
                    hold(dve, dve_passed, *t.at_ready(i, t_prob(n - lag, TB - 1)))
                for q in range(TB):
                    step, w = n * TB + q, (q + 1) * P
                    hold(dve, dve_passed, *s.at_ready(i, step))
                    dve.tensor_tensor_reduce(sc[:, n % lag, ROW_AT[q]:ROW_AT[q] + w], s.bank[step % 2][:, 0:w],
                                             causal[:, S - w:S], 1.0, 3 * NEG, ALU.add, ALU.max,
                                             top[:, n % lag, q:q + 1]).then_inc(s.free[step % 2], 1)
                dve.drain()
                dve.tensor_scalar(shift[:, n % lag, :], top[:, n % lag, :], -HD ** -0.5, None, ALU.mult)\
                   .then_inc(shift_ready, 1)

            def select(i, g):
                dve.drain()
                for h in range(GH):
                    for q in range(1, TB):
                        dve.tensor_reduce(low[:, h, q - 1:q], sc[:, h, ROW_AT[q]:ROW_AT[q] + q * P], AX.X, ALU.min)
                dve.tensor_copy(high[:, :, :], top[:, :, 1:TB])
                dve.drain()
                with dve.Fori(0, BISECT):
                    dve.tensor_tensor(mid[:, :, :], low[:, :, :], high[:, :, :], ALU.add)
                    dve.drain()
                    dve.tensor_scalar(mid[:, :, :], mid[:, :, :], 0.5, None, ALU.mult)
                    dve.drain()
                    c = 0
                    for h in range(GH):
                        for q in range(1, TB):
                            w = (q + 1) * P
                            dve.tensor_scalar(junk[:, c, 0:w], sc[:, h, ROW_AT[q]:ROW_AT[q] + w],
                                              mid[:, h, q - 1:q], 0.0, ALU.is_ge, ALU.add,
                                              accum_out=cnt[:, h, q - 1:q])
                            c += 1
                    dve.drain()
                    dve.tensor_scalar(cond[:, :, :], cnt[:, :, :], KEEP - 0.5, None, ALU.is_ge)
                    dve.drain()
                    dve.copy_predicated(low[:, :, :], cond[:, :, :].bitcast(I32), mid[:, :, :])
                    dve.drain()
                    dve.tensor_scalar(cond[:, :, :], cnt[:, :, :], KEEP - 0.5, None, ALU.is_lt)
                    dve.drain()
                    dve.copy_predicated(high[:, :, :], cond[:, :, :].bitcast(I32), mid[:, :, :])
                    dve.drain()
                dve.tensor_copy(thr[:, :, 1:TB], low[:, :, :])
                dve.drain()
                for h in range(GH):
                    n = g * GH + h
                    dve.wait_ge(exp_ready, i * H + n + 1)
                    for q in range(TB):
                        part = slice(ROW_AT[q], ROW_AT[q] + (q + 1) * P)
                        last = dve.scalar_tensor_tensor(out=sc[:, h, part], in0=sc[:, h, part],
                                                        scalar=thr[:, h, q:q + 1], in1=ex[:, n % 2, part],
                                                        op0=ALU.is_ge, op1=ALU.mult)
                    last.then_inc(sel_ready, 1)

            def out_rows(i, g):
                step = t_out(g)
                dve.wait_ge(*t.at_ready(i, step))
                v = t.bank[step % 2][:, :].rearrange("p (q h c) -> p q h c", q=TB, h=GH)
                dve.reciprocal(recip[:, :, :], v[:, :, :, HD])
                dve.drain()
                dve.tensor_tensor(xn[:, :, g * GH * HD:(g + 1) * GH * HD].rearrange("p q (h d) -> p q h d", h=GH),
                                  v[:, :, :, 0:HD], recip[:, :, :].unsqueeze(3).broadcast_to([P, TB, GH, HD]),
                                  ALU.mult).then_inc(t.free[step % 2], 1)

            with dve.Fori(0, B) as i:
                norm.vector_norm(dve, i)
                norm.vector_split(dve, i)
                if kind == 0:
                    rope(i, 0, 1)
                rope(i, 0, 0)
                if kind == 1:
                    rope(i, 0, 1)
                for n in range(H + lag):
                    done = n - lag
                    if done >= 0:
                        move_probs(dve, dve.tensor_copy, i, done, [k for k in range(TB) if k not in on_act])
                    if n < H:
                        row_max(i, n)
                    if done >= 0 and done % GH == GH - 1:
                        out_rows(i, done // GH)
                    if kind == 0 and n < H and n % GH == GH - 1:
                        select(i, n // GH)
                    if n % 8 == 4 and n < H and n // 8 + 1 < KT:
                        rope(i, n // 8 + 1, 0)
                        if kind == 1:
                            rope(i, n // 8 + 1, 1)
                for k in range(TB):
                    dve.wait_ge(*m.at_ready(i, m_last(k)))
                    dve.tensor_tensor(x[:, TB * i + k, :], m.bank[m_last(k) % 2][:, :], x[:, TB * i + k, :], ALU.add)\
                       .then_inc(m.free[m_last(k) % 2], 1)


def build(nc, a, out):
    with ExitStack() as ctx:
        sb = lambda name, shape, dt=F32: ctx.enter_context(nc.sbuf_tensor(name, shape, dt))
        x = sb("x", [P, NT, D])
        ident = sb("ident", [P, P])
        consts = sb("consts", [P, 2, 16])
        with ExitStack() as c0:
            loaded = nc.alloc_semaphore("start_loaded")
            block = c0.enter_context(nc.Block())

            @block.sync
            def _(sp):
                for b in range(B):
                    sp.dma_start(x[:, TB * b:TB * (b + 1), :],
                                 a["L0_attn_hidden_states"][b].rearrange("(t p) c -> p t c", p=P)).then_inc(loaded, 16)
                sp.dma_start(ident[:, :], a["c_ident"]).then_inc(loaded, 16)
                sp.dma_start(consts[:, :, :], a["c_rows"]).then_inc(loaded, 16)
                sp.wait_ge(loaded, 16 * (B + 2))
        f0 = {k: a["L0_ffn_" + k] for k in ("b", "A", "Bmat", "LiMEs")} | {"W": a["L0_ffn_W"]}
        f1 = {k: a["L1_ffn_" + k] for k in ("lora_A", "lora_B", "router_W", "router_b", "domain_prior", "active")} \
            | {"W": a["L1_ffn_W_base"], "b": a["L1_ffn_b_base"]}
        ffn(nc, "f0a", 0, x, ident, consts, f0, a)
        attention(nc, "at0", 0, x, ident, a)
        ffn(nc, "f0b", 0, x, ident, consts, f0, a)
        ffn(nc, "f1a", 1, x, ident, consts, f1, a)
        attention(nc, "at1", 1, x, ident, a)
        ffn(nc, "f1b", 1, x, ident, consts, f1, a, out)


def ffn(nc, name, kind, x, ident, consts, ins, a, out=None):
    with ExitStack() as ctx:
        sb = lambda n, shape, dt=F32: ctx.enter_context(nc.sbuf_tensor(f"{name}_{n}", shape, dt))
        w_hi, w_lo = sb("w_hi", [P, KT, D], F32R), sb("w_lo", [P, KT, D], F32R)
        s_hi, s_lo = sb("s_hi", [P, KT, 48], F32R), sb("s_lo", [P, KT, 48], F32R)
        stack = sb("stack", [P, D], F32R)
        extra = {"out": out}
        if kind == 0:
            extra |= {"bias8": sb("bias8", [P, E0]), "limes_bd": sb("limes_bd", [P, NT, RANK]),
                      "tile_mask": sb("tile_mask", [P, NT]), "small": sb("small", [P, NT, 48])}
            with ExitStack() as c0:
                loaded = nc.alloc_semaphore(f"{name}_mask_loaded")
                block = c0.enter_context(nc.Block())

                @block.sync
                def _(sp):
                    sp.dma_start(extra["tile_mask"][:, :], a["c_tile_mask"]).then_inc(loaded, 16)
                    sp.wait_ge(loaded, 16)
        else:
            extra |= {"logit_bias": sb("logit_bias", [P, E_ACT])}
        prepare_weights(nc, name + "w", ident, [(ins["W"], D, w_hi, w_lo)])
        ffn_weights(nc, name + "s", ident, consts[:, kind, :], kind, ins["W"], w_hi, w_lo, s_hi, s_lo, stack,
                    extra, ins)
        ffn_loop(nc, name + "l", kind, x, ident, w_hi, w_lo, s_hi, s_lo, stack, extra)
        if kind == 0:
            ffn0_route(nc, name + "r", x, ident, stack, extra)


_INS = ["L0_attn_hidden_states", "L0_attn_Wq", "L0_attn_Wk", "L0_attn_Wv", "L0_attn_Wo", "L0_ffn_W", "L0_ffn_b",
        "L0_ffn_A", "L0_ffn_Bmat", "L0_ffn_LiMEs", "L1_attn_wq", "L1_attn_wk", "L1_attn_wv", "L1_attn_wo",
        "L1_ffn_W_base", "L1_ffn_b_base", "L1_ffn_lora_A", "L1_ffn_lora_B", "L1_ffn_router_W", "L1_ffn_router_b",
        "L1_ffn_domain_prior", "L1_ffn_active"]


def shape_constants():
    p = np.arange(P)
    rows = np.zeros((P, 2, 16), np.float32)
    scale = (0.5, 2.0)
    for kind in range(2):
        rows[:, kind, 0] = np.where(p < ONES_AT, scale[kind], 1.0)
        lo = ((p >= 2 * RANK) & (p < ONES_AT)) | (p == ONES_AT + 1)
        rows[:, kind, 1] = ~lo
        rows[:, kind, 2] = lo
        rows[:, kind, 3] = p
        rows[:, kind, 4] = p // R1
        rows[:, kind, 8:16] = p[:, None] % R1 == np.arange(R1)
    half = HD // 2
    inv = (1.0 / 10000.0 ** (np.arange(0, HD, 2, dtype=np.float32) / np.float32(HD))).astype(np.float32)
    freqs = np.outer(np.arange(S, dtype=np.float32), inv).astype(np.float32)
    d = p % HD
    cos = np.cos(freqs).astype(np.float32)[:, d % half].T
    sin = np.sin(freqs).astype(np.float32)[:, d % half].T * np.where(d < half, -1.0, 1.0)[:, None]
    causal = np.zeros((P, S), np.float32)
    causal[:, S - P:] = np.where(p[:, None] < p[None, :], NEG, 0.0)
    return {"c_ident": np.eye(P, dtype=np.float32), "c_rows": rows,
            "c_tile_mask": (p[:, None] // E0 == np.arange(NT)).astype(np.float32),
            "c_cos": np.ascontiguousarray(cos), "c_sin": np.ascontiguousarray(sin.astype(np.float32)),
            "c_causal": causal}


def kernel(**inputs):
    import concourse.bacc as _bacc
    from concourse import mybir as _mybir
    from concourse.bass_utils import run_bass_kernel_spmd as _run

    nc = _bacc.Bacc("TRN2", target_bir_lowering=False, num_devices=1)
    arrays, args = {}, {}
    for name, v in [(n, inputs[n]) for n in _INS] + list(shape_constants().items()):
        v = np.ascontiguousarray(v)
        arrays[f"in_{name}"] = v
        args[name] = nc.dram_tensor(f"in_{name}", v.shape, _mybir.dt.from_np(v.dtype), kind="ExternalInput").ap()
    out = nc.dram_tensor("out_x", (B, S, D), F32, kind="ExternalOutput").ap()
    build(nc, args, out)
    r = _run(nc, [arrays], core_ids=[0])
    return r.results[0]["out_x"]
```

```python
from contextlib import ExitStack

import numpy as np

import concourse.bass as bass
from concourse import mybir

F32 = mybir.dt.float32
F32R = mybir.dt.float32r
I32 = mybir.dt.int32
ACT = mybir.ActivationFunctionType
ALU = mybir.AluOpType
AX = mybir.AxisListType
RMAX = bass.bass_isa.ReduceOp.max

P = 128
B, S, D = 4, 512, 512
TB = S // P
NT = B * TB
KT = D // P
LN_EPS = 1e-5

RANK = 32
E0 = 8
NGRAM = 2
E_TOT, E_ACT, R1 = 16, 4, 8
STACK = 128
ONES_AT = 3 * RANK

H, HD = 32, 16
HKV0 = 8
KEEP = 128
GH = 4
NG = H // GH
VW = HD + 1
QK_ROWS = 96
CAUSAL = TB * (TB + 1) // 2 * P
ROW_AT = [P * (t * (t + 1) // 2) for t in range(TB)]
COL_AT = [sum((TB - j) * P for j in range(k)) for k in range(TB)]
NEG = -1.0e30
AIM = KEEP - 3.5
SHARED = 4
EX = 4
BISECT = 60


def prod3(pe, out, lhs, rhs, ks, start=True, stop=True):
    n, last = len(ks), None
    for c, k in enumerate(ks):
        (lh, ll), (rh, rl) = lhs(k), rhs(k)
        pe.matmul(out, lh, rh, start=start and c == 0, stop=False)
        pe.matmul(out, lh, rl, start=False, stop=False)
        last = pe.matmul(out, ll, rh, start=False, stop=stop and c == n - 1)
    return last


def hold(eng, passed, sem, value):
    eng.wait_ge(sem, value)
    eng.sem_inc(passed, 1)


class Stage:

    def __init__(self, nc, ctx, name):
        self.nc, self.ctx, self.name = nc, ctx, name
        self.sems = []
        ctx.callback(self.clear)

    def sb(self, name, shape, dt=F32):
        return self.ctx.enter_context(self.nc.sbuf_tensor(f"{self.name}_{name}", shape, dt))

    def ps(self, name, n=512):
        return self.ctx.enter_context(self.nc.psum_tensor(f"{self.name}_{name}", [P, n], F32))

    def sem(self, name):
        self.sems.append(self.nc.alloc_semaphore(f"{self.name}_{name}"))
        return self.sems[-1]

    def clear(self):
        if self.sems:
            self.nc.clear_and_free_semaphores(self.sems)
            self.nc.all_engine_barrier()


class Ring2:

    def __init__(self, st, name, steps):
        self.bank = [st.ps(f"{name}{b}") for b in range(2)]
        self.ready = st.sem(f"{name}_ready")
        self.free = [st.sem(f"{name}_free{b}") for b in range(2)]
        self.steps = steps
        self.per = [(steps + 1) // 2, steps // 2]

    def prime(self, eng):
        for f in self.free:
            eng.sem_inc(f, 1)

    def at_free(self, i, k):
        return self.free[k % 2], i * self.per[k % 2] + k // 2 + 1

    def at_used(self, i, k):
        return self.free[k % 2], i * self.per[k % 2] + k // 2 + 2

    def at_ready(self, i, k):
        return self.ready, i * self.steps + k + 1


def prepare_weights(nc, name, ident, jobs):
    with ExitStack() as ctx:
        st = Stage(nc, ctx, name)
        raw = st.sb("raw", [P, 2, KT, D])
        t = Ring2(st, "wt", len(jobs) * KT)
        loaded = [st.sem("loaded0"), st.sem("loaded1")]
        raw_used = st.sem("raw_used")
        hi_ready = st.sem("hi_ready")
        block = ctx.enter_context(nc.Block())

        @block.sync
        def _(sp):
            for j, (w, n_out, _, _) in enumerate(jobs):
                if j >= 2:
                    sp.wait_ge(raw_used, j - 1)
                sp.dma_start(raw[:, j % 2, 0:n_out // P, :],
                             w.rearrange("(a p) i -> p a i", p=P)).then_inc(loaded[j % 2], 16)

        @block.tensor
        def _(pe):
            for j, (_, n_out, _, _) in enumerate(jobs):
                pe.wait_ge(loaded[j % 2], 16 * (j // 2 + 1))
                for k in range(KT):
                    step = j * KT + k
                    if step >= 2:
                        pe.wait_ge(t.free[step % 2], step // 2)
                    for a in range(n_out // P):
                        last = pe.transpose(t.bank[step % 2][:, a * P:(a + 1) * P],
                                            raw[:, j % 2, a, k * P:(k + 1) * P], ident[:, :])
                    last.then_inc(t.ready, 1)
                pe.drain().then_inc(raw_used, 1)

        @block.scalar
        def _(act):
            for j, (_, n_out, hi, lo) in enumerate(jobs):
                for k in range(KT):
                    step = j * KT + k
                    act.wait_ge(t.ready, step + 1)
                    ins = act.activation(hi[:, k, :], t.bank[step % 2][:, 0:n_out], ACT.Copy)
                    ins.then_inc(hi_ready if lo is not None else t.free[step % 2], 1)

        @block.vector
        def _(dve):
            n_hi = 0
            for j, (_, n_out, hi, lo) in enumerate(jobs):
                for k in range(KT):
                    step = j * KT + k
                    if lo is not None:
                        n_hi += 1
                        dve.wait_ge(hi_ready, n_hi)
                        dve.tensor_tensor(lo[:, k, :], t.bank[step % 2][:, 0:n_out],
                                          hi[:, k, :].bitcast(F32), ALU.subtract).then_inc(t.free[step % 2], 1)


class Norm:

    def __init__(self, st, x, ident, t, xn):
        self.x, self.ident, self.t, self.xn = x, ident, t, xn
        self.hi = st.sb("xT_hi", [P, KT, S], F32R)
        self.lo = st.sb("xT_lo", [P, KT, S], F32R)
        self.stats = st.sb("stats", [P, NT, 6])
        self.mv = st.sb("mv", [P, NT, 2])
        self.ve = st.sb("ve", [P, NT])
        self.sd = st.sb("sd", [P, NT])
        self.rs = st.sb("rs", [P, NT])
        self.now = st.sb("now", [P, 2, TB])
        self.var_ready = st.sem("var_ready")
        self.std_ready = st.sem("std_ready")
        self.xn_ready = st.sem("xn_ready")
        self.xn_free = st.sem("xn_free")
        self.hi_ready = st.sem("xhi_ready")
        self.free = st.sem("xT_free")

    def prime(self, eng):
        eng.sem_inc(self.xn_free, 1)
        eng.sem_inc(self.free, 1)

    def vector_stats(self, dve):
        for t in range(NT):
            dve.bn_stats(self.stats[:, t, :], self.x[:, t, :])
        dve.drain()
        for t in range(NT):
            dve.bn_aggr(self.mv[:, t, :], self.stats[:, t, :])
        dve.drain()
        dve.tensor_scalar(self.ve[:, :], self.mv[:, :, 1], LN_EPS, None, ALU.add).then_inc(self.var_ready, 1)
        dve.wait_ge(self.std_ready, 1)
        dve.reciprocal(self.rs[:, :], self.sd[:, :])
        dve.drain()

    def scalar_root(self, act):
        act.wait_ge(self.var_ready, 1)
        act.activation(self.sd[:, :], self.ve[:, :], ACT.Sqrt).then_inc(self.std_ready, 1)

    def vector_norm(self, dve, i):
        dve.tensor_copy(self.now[:, 0, :], self.mv[:, bass.ds(TB * i, TB), 0])
        dve.tensor_copy(self.now[:, 1, :], self.rs[:, bass.ds(TB * i, TB)])
        dve.drain()
        dve.wait_ge(self.xn_free, i + 1)
        for t in range(TB):
            dve.tensor_scalar(self.xn[:, t, :], self.x[:, TB * i + t, :], self.now[:, 0, t:t + 1],
                              self.now[:, 1, t:t + 1], ALU.subtract, ALU.mult).then_inc(self.xn_ready, 1)

    def tensor_transpose(self, pe, i):
        for t in range(TB):
            pe.wait_ge(self.xn_ready, i * TB + t + 1)
            pe.wait_ge(*self.t.at_free(i, t))
            for k in range(KT):
                last = pe.transpose(self.t.bank[t % 2][:, k * P:(k + 1) * P],
                                    self.xn[:, t, k * P:(k + 1) * P], self.ident[:, :])
            last.then_inc(self.t.ready, 1)

    def scalar_split(self, act, i):
        act.wait_ge(self.free, i + 1)
        for t in range(TB):
            act.wait_ge(*self.t.at_ready(i, t))
            act.activation(self.hi[:, :, t * P:(t + 1) * P], self.t.bank[t % 2][:, :], ACT.Copy)\
               .then_inc(self.hi_ready, 1)

    def vector_split(self, dve, i):
        for t in range(TB):
            dve.wait_ge(self.hi_ready, i * TB + t + 1)
            dve.tensor_tensor(self.lo[:, :, t * P:(t + 1) * P],
                              self.t.bank[t % 2][:, :].rearrange("p (k c) -> p k c", k=KT),
                              self.hi[:, :, t * P:(t + 1) * P].bitcast(F32), ALU.subtract)\
               .then_inc(self.t.free[t % 2], 1)

    def tile(self, t):
        return lambda k: (self.hi[:, k, t * P:(t + 1) * P], self.lo[:, k, t * P:(t + 1) * P])

    def batch(self):
        return lambda k: (self.hi[:, k, :], self.lo[:, k, :])


def ffn_weights(nc, name, ident, consts, kind, w, w_hi, w_lo, small_hi, small_lo, stack, extra, ins):
    with ExitStack() as ctx:
        st = Stage(nc, ctx, name)
        raw = st.sb("raw", [P, D])
        scaled = st.sb("scaled", [P, D])
        rounded = st.sb("rounded", [P, D], F32R)
        rest = st.sb("rest", [P, D])
        bank = st.ps("bank")
        bank2 = st.ps("bank2")
        small = st.sb("small", [P, KT, 48])
        loaded = st.sem("loaded")
        cleared = st.sem("cleared")
        built = st.sem("built")
        turned = st.sem("turned")
        vec = st.sem("vec")
        bias = ins["b"].rearrange("(a o) -> a o", a=1)

        if kind == 0:
            a_raw = st.sb("a_raw", [P, KT, RANK])
            aT = st.sb("aT", [RANK, D])
            limesT = st.sb("limesT", [RANK, E0])
            limes_rep = st.sb("limes_rep", [P, RANK])
            block = ctx.enter_context(nc.Block())

            @block.sync
            def _(sp):
                sp.wait_ge(cleared, 1)
                for r in range(3):
                    sp.dma_start(raw[RANK * r:RANK * (r + 1), :], ins["Bmat"]).then_inc(loaded, 16)
                for r in range(2):
                    sp.dma_start(raw[ONES_AT + r:ONES_AT + r + 1, :], bias).then_inc(loaded, 16)
                sp.dma_start(a_raw[:, :, :], ins["A"].rearrange("(k p) r -> p k r", p=P)).then_inc(loaded, 16)
                with nc.allow_non_contiguous_dma(reason="256 numbers"):
                    sp.dma_start(limesT[:, :], ins["LiMEs"].rearrange("e r -> r e")).then_inc(loaded, 16)
                for n in range(NT):
                    sp.dma_start(limes_rep[E0 * n:E0 * (n + 1), :], ins["LiMEs"]).then_inc(loaded, 16)
                sp.dma_start(extra["bias8"][:, :], bias[:, 0:E0].broadcast_to([P, E0])).then_inc(loaded, 16)

            @block.tensor
            def _(pe):
                pe.wait_ge(loaded, 16 * (8 + NT))
                for k in range(KT):
                    last = pe.transpose(bank[0:RANK, k * P:(k + 1) * P], a_raw[:, k, :], ident[:, :])
                last.then_inc(turned, 1)
                pe.wait_ge(vec, 1)
                for k in range(KT):
                    last = pe.matmul(bank2[:, k * E0:(k + 1) * E0], aT[:, k * P:(k + 1) * P], limesT[:, :],
                                     start=True, stop=True)
                last.then_inc(turned, 1)

            @block.vector
            def _(dve):
                dve.memset(raw[:, :], 0.0).then_inc(cleared, 1)
                dve.wait_ge(loaded, 16 * (8 + NT))
                dve.wait_ge(turned, 1)
                dve.tensor_copy(aT[:, :], bank[0:RANK, :]).then_inc(vec, 1)
                dve.tensor_scalar(scaled[:, :], raw[:, :], consts[:, 0:1], None, ALU.mult)
                dve.tensor_tensor(extra["limes_bd"][:, :, :],
                                  limes_rep[:, :].unsqueeze(1).broadcast_to([P, NT, RANK]),
                                  extra["tile_mask"][:, :].unsqueeze(2).broadcast_to([P, NT, RANK]), ALU.mult)
                dve.tensor_copy(small[:, :, 0:RANK], a_raw[:, :, :])
                dve.wait_ge(turned, 2)
                dve.tensor_copy(small[:, :, RANK + E0:48],
                                bank2[:, 0:KT * E0].rearrange("p (k e) -> p k e", k=KT))
                dve.drain()
                dve.tensor_copy(small_hi[:, :, 0:RANK], small[:, :, 0:RANK])
                dve.tensor_copy(small_hi[:, :, RANK + E0:48], small[:, :, RANK + E0:48])
                dve.tensor_copy(small_hi[:, :, RANK:RANK + E0], w_hi[:, :, 0:E0].bitcast(F32))
                dve.tensor_copy(small_lo[:, :, RANK:RANK + E0], w_lo[:, :, 0:E0].bitcast(F32))
                dve.drain()
                for a, z in ((0, RANK), (RANK + E0, 48)):
                    dve.tensor_tensor(small_lo[:, :, a:z], small[:, :, a:z], small_hi[:, :, a:z].bitcast(F32),
                                      ALU.subtract)
                split_stack(dve, stack, scaled, rounded, rest, consts)
        else:
            lora_a = st.sb("lora_a", [E_TOT * R1, D])
            lora_b = st.sb("lora_b", [P, KT, E_TOT, R1])
            lora_bT = st.sb("lora_bT", [E_TOT * R1, D])
            router = st.sb("router", [E_TOT, D])
            rows = st.sb("rows", [E_TOT, 2])
            rows_wide = st.sb("rows_wide", [E_TOT, 2, P])
            act_i = st.sb("act_i", [P, E_ACT], I32)
            act_f = st.sb("act_f", [P, E_ACT])
            sel_e = st.sb("sel_e", [P, E_ACT])
            sel = st.sb("sel", [P, E_ACT, R1])
            prior_log = st.sb("prior_log", [P, E_ACT])
            prior = st.sb("prior", [P, E_ACT])
            block = ctx.enter_context(nc.Block())

            @block.sync
            def _(sp):
                sp.wait_ge(cleared, 1)
                for r in range(2):
                    sp.dma_start(raw[ONES_AT + r:ONES_AT + r + 1, :], bias).then_inc(loaded, 16)
                sp.dma_start(lora_a[:, :], ins["lora_A"].rearrange("e r h -> (e r) h")).then_inc(loaded, 16)
                for k in range(KT):
                    sp.dma_start(lora_b[:, k, :, :],
                                 ins["lora_B"][:, k * P:(k + 1) * P, :].rearrange("e o r -> o e r"))\
                      .then_inc(loaded, 16)
                sp.dma_start(router[:, :], ins["router_W"]).then_inc(loaded, 16)
                with nc.allow_non_contiguous_dma(reason="16 numbers each"):
                    sp.dma_start(rows[:, 0:1], ins["router_b"].rearrange("(e a) -> e a", a=1)).then_inc(loaded, 16)
                    sp.dma_start(rows[:, 1:2], ins["domain_prior"].rearrange("(e a) -> e a", a=1))\
                      .then_inc(loaded, 16)
                sp.dma_start(act_i[:, :], ins["active"].rearrange("(a j) -> a j", a=1).broadcast_to([P, E_ACT]))\
                  .then_inc(loaded, 16)

            @block.tensor
            def _(pe):
                pe.wait_ge(loaded, 16 * 11)
                for k in range(KT):
                    last = pe.transpose(bank[:, k * P:(k + 1) * P],
                                        lora_b[:, k, :, :].rearrange("p e r -> p (e r)"), ident[:, :])
                last.then_inc(turned, 1)
                pe.wait_ge(vec, 1)
                for k in range(KT):
                    pe.matmul(bank2[:, k * 40:k * 40 + RANK], lora_a[:, k * P:(k + 1) * P],
                              sel[:, :, :].rearrange("p j r -> p (j r)"), start=True, stop=True)
                    pe.matmul(bank2[:, k * 40 + RANK:k * 40 + RANK + E_ACT], router[:, k * P:(k + 1) * P],
                              sel_e[0:E_TOT, :], start=True, stop=True)
                for c in range(2):
                    last = pe.matmul(bank2[:, 160 + 4 * c:164 + 4 * c], rows_wide[:, c, :], sel_e[0:E_TOT, :],
                                     start=True, stop=True)
                last.then_inc(turned, 1)
                pe.wait_ge(vec, 2)
                pe.matmul(bank[0:RANK, :], sel[:, :, :].rearrange("p j r -> p (j r)"), lora_bT[:, :],
                          start=True, stop=True).then_inc(turned, 1)

            @block.scalar
            def _(act):
                act.wait_ge(vec, 3)
                act.activation(prior_log[:, :], prior[:, :], ACT.Ln).then_inc(built, 1)

            @block.vector
            def _(dve):
                dve.memset(raw[:, :], 0.0).then_inc(cleared, 1)
                dve.wait_ge(loaded, 16 * 11)
                dve.tensor_copy(act_f[:, :], act_i[:, :])
                dve.tensor_copy(rows_wide[:, :, :], rows[:, :].unsqueeze(2).broadcast_to([E_TOT, 2, P]))
                dve.drain()
                dve.tensor_scalar(sel_e[:, :], act_f[:, :], consts[:, 3:4], None, ALU.is_equal)
                dve.tensor_scalar(act_f[:, :], act_f[:, :], consts[:, 4:5], None, ALU.is_equal)
                dve.drain()
                dve.tensor_tensor(sel[:, :, :], act_f[:, :].unsqueeze(2).broadcast_to([P, E_ACT, R1]),
                                  consts[:, 8:8 + R1].unsqueeze(1).broadcast_to([P, E_ACT, R1]), ALU.mult)\
                   .then_inc(vec, 1)
                dve.wait_ge(turned, 1)
                dve.tensor_copy(lora_bT[:, :], bank[:, :]).then_inc(vec, 1)
                dve.wait_ge(turned, 2)
                dve.tensor_scalar(prior[:, :], bank2[:, 164:168], 1e-12, None, ALU.add).then_inc(vec, 1)
                dve.tensor_copy(small[:, :, 0:36], bank2[:, 0:160].rearrange("p (k c) -> p k c", c=40)[:, :, 0:36])
                dve.wait_ge(built, 1)
                dve.tensor_tensor(extra["logit_bias"][:, :], bank2[:, 160:164], prior_log[:, :], ALU.add)
                dve.drain()
                dve.tensor_copy(small_hi[:, :, 0:36], small[:, :, 0:36])
                dve.wait_ge(turned, 3)
                for r in range(3):
                    dve.tensor_copy(raw[RANK * r:RANK * (r + 1), :], bank[0:RANK, :])
                dve.drain()
                dve.tensor_tensor(small_lo[:, :, 0:36], small[:, :, 0:36], small_hi[:, :, 0:36].bitcast(F32),
                                  ALU.subtract)
                dve.tensor_scalar(scaled[:, :], raw[:, :], consts[:, 0:1], None, ALU.mult)
                split_stack(dve, stack, scaled, rounded, rest, consts)


def split_stack(dve, stack, scaled, rounded, rest, consts):
    dve.drain()
    dve.tensor_copy(rounded[:, :], scaled[:, :])
    dve.drain()
    dve.tensor_tensor(rest[:, :], scaled[:, :], rounded[:, :].bitcast(F32), ALU.subtract)
    dve.drain()
    dve.tensor_scalar(rest[:, :], rest[:, :], consts[:, 2:3], None, ALU.mult)
    dve.drain()
    dve.scalar_tensor_tensor(out=stack[:, :], in0=rounded[:, :].bitcast(F32), scalar=consts[:, 1:2],
                             in1=rest[:, :], op0=ALU.mult, op1=ALU.add)


def ffn_loop(nc, name, kind, x, ident, w_hi, w_lo, small_hi, small_lo, stack, extra):
    n_small = 48 if kind == 0 else 36
    turns = TB if kind == 0 else 2 * TB
    with ExitStack() as ctx:
        st = Stage(nc, ctx, name)
        t = Ring2(st, "t", turns)
        xn = st.sb("xn", [P, TB, D])
        norm = Norm(st, x, ident, t, xn)
        h = [st.ps(f"h{k}") for k in range(TB)]
        sm = st.ps("sm")
        smv = sm[:, 0:TB * 64].rearrange("p (t c) -> p t c", c=64)
        h_ready = st.sem("h_ready")
        h_free = st.sem("h_free")
        sm_ready = st.sem("sm_ready")
        sm_free = st.sem("sm_free")
        ready0 = st.sem("consts_ready")
        left = st.sb("left", [P, TB, STACK])
        leftT = st.sb("leftT", [P, TB, P], F32R)
        if kind == 1:
            logit = st.sb("logit", [P, TB, E_ACT])
            top = st.sb("top", [P, TB])
            ex = st.sb("ex", [P, TB, E_ACT])
            total = st.sb("total", [P, TB])
            alpha = st.sb("alpha", [P, TB, E_ACT])
            u = st.sb("u", [P, TB, RANK])
            logit_ready = st.sem("logit_ready")
            ex_ready = st.sem("ex_ready")
            left_ready = st.sem("left_ready")
            left_free = st.sem("left_free")
            out = extra.get("out")
            stored = st.sem("stored")
            passed = st.sem("passed")
        block = ctx.enter_context(nc.Block())

        @block.tensor
        def _(pe):
            t.prime(pe)
            pe.wait_ge(ready0, 1)
            with pe.Fori(0, B) as i:
                norm.tensor_transpose(pe, i)
                pe.wait_ge(sm_free, i + 1)
                for k in range(TB):
                    pe.wait_ge(*t.at_used(i, k))
                    last = prod3(pe, smv[:, k, 0:n_small], norm.tile(k),
                                 lambda c: (small_hi[:, c, 0:n_small], small_lo[:, c, 0:n_small]), range(KT))
                last.then_inc(sm_ready, 1)
                for k in range(TB):
                    pe.wait_ge(h_free, i * TB + k + 1)
                    prod3(pe, h[k][:, :], norm.tile(k), lambda c: (w_hi[:, c, :], w_lo[:, c, :]), range(KT),
                          stop=False)
                    if kind == 0:
                        pe.matmul(h[k][:, :], leftT[:, 0, :], stack[:, :], start=False, stop=True)\
                          .then_inc(h_ready, 1)
                pe.drain().then_inc(norm.free, 1)
                if kind == 1:
                    for k in range(TB):
                        pe.wait_ge(left_ready, i * TB + k + 1)
                        pe.wait_ge(*t.at_free(i, TB + k))
                        pe.transpose(t.bank[k % 2][:, 0:P], left[:, k, :], ident[:, :]).then_inc(t.ready, 1)
                    pe.drain().then_inc(norm.xn_free, 1)
                    for k in range(TB):
                        pe.wait_ge(*t.at_used(i, TB + k))
                        pe.matmul(h[k][:, :], leftT[:, k, :], stack[:, :], start=False, stop=True)\
                          .then_inc(h_ready, 1)
                    pe.drain().then_inc(left_free, 1)
                else:
                    pe.drain().then_inc(norm.xn_free, 1)

        @block.scalar
        def _(act):
            norm.prime(act)
            act.sem_inc(sm_free, 1)
            act.sem_inc(h_free, TB)
            if kind == 1:
                act.sem_inc(left_free, 1)
            norm.scalar_root(act)
            with act.Fori(0, B) as i:
                norm.scalar_split(act, i)
                if kind == 0:
                    act.wait_ge(sm_ready, i + 1)
                    act.activation(extra["small"][:, bass.ds(TB * i, TB), :], smv[:, :, 0:n_small], ACT.Copy)\
                       .then_inc(sm_free, 1)
                else:
                    act.wait_ge(logit_ready, i + 1)
                    act.activation(ex[:, :, :], logit[:, :, :], ACT.Exp).then_inc(ex_ready, 1)
                    act.wait_ge(left_free, i + 1)
                    for k in range(TB):
                        act.wait_ge(*t.at_ready(i, TB + k))
                        act.activation(leftT[:, k, :], t.bank[k % 2][:, 0:P], ACT.Copy)\
                           .then_inc(t.free[k % 2], 1)

        @block.vector
        def _(dve):
            dve.memset(left[:, :, :], 0.0)
            dve.drain()
            dve.memset(left[:, :, ONES_AT:ONES_AT + 2], 1.0)
            if kind == 0:
                ones = left[:, 1, :]
                dve.drain()
                dve.memset(ones, 0.0)
                dve.drain()
                dve.memset(left[ONES_AT:P, 1, :], 1.0)
                dve.drain()
                dve.tensor_copy(leftT[:, 0, :], ones).then_inc(ready0, 1)
            else:
                dve.drain().then_inc(ready0, 1)
            norm.vector_stats(dve)
            with dve.Fori(0, B) as i:
                norm.vector_norm(dve, i)
                norm.vector_split(dve, i)
                if kind == 1:
                    dve.wait_ge(sm_ready, i + 1)
                    dve.tensor_tensor(logit[:, :, :], smv[:, :, RANK:RANK + E_ACT],
                                      extra["logit_bias"][:, :].unsqueeze(1).broadcast_to([P, TB, E_ACT]), ALU.add)
                    dve.drain()
                    dve.tensor_reduce(top[:, :], logit[:, :, :], AX.X, ALU.max)
                    dve.drain()
                    dve.tensor_tensor(logit[:, :, :], logit[:, :, :],
                                      top[:, :].unsqueeze(2).broadcast_to([P, TB, E_ACT]), ALU.subtract)\
                       .then_inc(logit_ready, 1)
                    dve.wait_ge(ex_ready, i + 1)
                    dve.tensor_reduce(total[:, :], ex[:, :, :], AX.X, ALU.add)
                    dve.drain()
                    dve.reciprocal(total[:, :], total[:, :])
                    dve.drain()
                    dve.tensor_tensor(alpha[:, :, :], ex[:, :, :],
                                      total[:, :].unsqueeze(2).broadcast_to([P, TB, E_ACT]), ALU.mult)
                    dve.drain()
                    for k in range(TB):
                        dve.tensor_tensor(u[:, k, :].rearrange("p (e r) -> p e r", e=E_ACT),
                                          smv[:, k, 0:RANK].rearrange("p (e r) -> p e r", e=E_ACT),
                                          alpha[:, k, :].unsqueeze(2).broadcast_to([P, E_ACT, R1]), ALU.mult)
                    dve.drain().then_inc(sm_free, 1)
                    dve.wait_ge(left_free, i + 1)
                    dve.tensor_copy(left[:, :, 0:RANK].bitcast(F32R), u[:, :, :])
                    dve.drain()
                    dve.tensor_copy(left[:, :, 2 * RANK:3 * RANK], left[:, :, 0:RANK])
                    dve.tensor_tensor(left[:, :, RANK:2 * RANK], u[:, :, :], left[:, :, 0:RANK], ALU.subtract)
                    dve.drain().then_inc(left_ready, TB)
                for k in range(TB):
                    dve.wait_ge(h_ready, i * TB + k + 1)
                    dve.scalar_tensor_tensor(out=x[:, TB * i + k, :], in0=h[k][:, :], scalar=0.5,
                                             in1=x[:, TB * i + k, :], op0=ALU.mult, op1=ALU.add)\
                       .then_inc(h_free, 1)

        if kind == 1 and out is not None:
            @block.sync
            def _(sp):
                with sp.Fori(0, B) as i:
                    hold(sp, passed, h_free, (i + 2) * TB)
                    sp.dma_start(out[i, :, :].rearrange("(t p) c -> p t c", p=P),
                                 x[:, bass.ds(TB * i, TB), :]).then_inc(stored, 16)
                sp.wait_ge(stored, 16 * B)


def ffn0_route(nc, name, x, ident, stack, extra):
    with ExitStack() as ctx:
        st = Stage(nc, ctx, name)
        small = extra["small"]
        t = Ring2(st, "t", TB)
        h = Ring2(st, "h", TB)
        pre = st.ps("pre")
        pre2 = st.ps("pre2")
        anchor = st.sb("anchor", [P, NT, 2 * E0])
        peak = st.sb("peak", [P, 2])
        peak_all = st.sb("peak_all", [P, 2])
        probs = st.sb("probs", [P, NT, E0])
        gate = st.sb("gate", [P, NT, E0])
        top8 = st.sb("top8", [P, NT, 8])
        row = st.sb("row", [P, NT])
        wT = st.sb("wT", [P, P])
        u = st.sb("u", [P, NT, RANK])
        left = st.sb("left", [P, TB, STACK])
        leftT = st.sb("leftT", [P, TB, P], F32R)
        copied = st.sem("copied")
        peak_ready = st.sem("peak_ready")
        peak_all_ready = st.sem("peak_all_ready")
        arg_ready = st.sem("arg_ready")
        exp_ready = st.sem("exp_ready")
        w_ready = st.sem("w_ready")
        wT_ready = st.sem("wT_ready")
        mix_ready = st.sem("mix_ready")
        turned = st.sem("turned")
        left_ready = st.sem("left_ready")
        left_free = st.sem("left_free")
        leftT_free = st.sem("leftT_free")
        block = ctx.enter_context(nc.Block())

        @block.gpsimd
        def _(pool):
            pool.wait_ge(peak_ready, 1)
            pool.partition_all_reduce(peak_all[:, :], peak[:, :], P, RMAX).then_inc(peak_all_ready, 1)

        @block.scalar
        def _(act):
            act.sem_inc(left_free, 1)
            act.sem_inc(leftT_free, TB)
            act.wait_ge(arg_ready, 1)
            act.activation(probs[:, :, :], probs[:, :, :], ACT.Exp).then_inc(exp_ready, 1)
            act.wait_ge(arg_ready, 2)
            act.activation(gate[:, :, :], gate[:, :, :], ACT.Exp, scale=-2.0).then_inc(exp_ready, 1)
            act.wait_ge(turned, 1)
            act.activation(wT[:, :], pre[:, 0:P], ACT.Copy).then_inc(wT_ready, 1)
            with act.Fori(0, B) as i:
                for k in range(TB):
                    act.wait_ge(leftT_free, i * TB + k + 1)
                    act.wait_ge(*t.at_ready(i, k))
                    act.activation(leftT[:, k, :], t.bank[k % 2][:, 0:P], ACT.Copy).then_inc(t.free[k % 2], 1)

        @block.tensor
        def _(pe):
            t.prime(pe)
            h.prime(pe)
            pe.wait_ge(w_ready, 1)
            pe.transpose(pre[:, 0:P], probs[:, :, :].rearrange("p n e -> p (n e)"), ident[:, :])\
              .then_inc(turned, 1)
            pe.wait_ge(wT_ready, 1)
            pe.matmul(pre2[:, :], wT[:, :], extra["limes_bd"][:, :, :].rearrange("p n r -> p (n r)"),
                      start=True, stop=True).then_inc(mix_ready, 1)
            with pe.Fori(0, B) as i:
                pe.wait_ge(left_ready, i + 1)
                for k in range(TB):
                    pe.wait_ge(*t.at_free(i, k))
                    pe.transpose(t.bank[k % 2][:, 0:P], left[:, k, :], ident[:, :]).then_inc(t.ready, 1)
                pe.drain().then_inc(left_free, 1)
                for k in range(TB):
                    pe.wait_ge(*t.at_used(i, k))
                    pe.wait_ge(*h.at_free(i, k))
                    pe.matmul(h.bank[k % 2][:, :], leftT[:, k, :], stack[:, :], start=True, stop=True)\
                      .then_inc(h.ready, 1)
                pe.drain().then_inc(leftT_free, TB)

        @block.vector
        def _(dve):
            dve.memset(left[:, :, :], 0.0)
            dve.stream_shuffle(anchor[:, :, :], small[:, :, RANK:48], [q | (NGRAM - 1) for q in range(32)])
            dve.drain()
            dve.tensor_tensor(anchor[:, :, 0:E0], anchor[:, :, 0:E0],
                              extra["bias8"][:, :].unsqueeze(1).broadcast_to([P, NT, E0]), ALU.add)
            dve.drain()
            for c in range(2):
                dve.tensor_reduce(peak[:, c:c + 1], anchor[:, :, c * E0:(c + 1) * E0], AX.XY, ALU.max,
                                  apply_absolute_value=True)
            dve.drain().then_inc(peak_ready, 1)
            dve.wait_ge(peak_all_ready, 1)
            dve.tensor_scalar(peak[:, :], peak_all[:, :], 1e-6, None, ALU.max)
            dve.drain()
            dve.reciprocal(peak[:, :], peak[:, :])
            dve.drain()
            dve.tensor_scalar(peak[:, :], peak[:, :], 0.5, None, ALU.mult)
            dve.drain()
            dve.tensor_scalar(probs[:, :, :], anchor[:, :, 0:E0], peak[:, 0:1], None, ALU.mult)
            dve.drain()
            dve.scalar_tensor_tensor(out=probs[:, :, :], in0=anchor[:, :, E0:2 * E0], scalar=peak[:, 1:2],
                                     in1=probs[:, :, :], op0=ALU.mult, op1=ALU.add)
            dve.drain()
            dve.tensor_reduce(row[:, :], probs[:, :, :], AX.X, ALU.max)
            dve.drain()
            wide = row[:, :].unsqueeze(2).broadcast_to([P, NT, E0])
            dve.tensor_tensor(probs[:, :, :], probs[:, :, :], wide, ALU.subtract).then_inc(arg_ready, 1)
            dve.wait_ge(exp_ready, 1)
            dve.tensor_reduce(row[:, :], probs[:, :, :], AX.X, ALU.add)
            dve.drain()
            dve.reciprocal(row[:, :], row[:, :])
            dve.drain()
            dve.tensor_tensor(probs[:, :, :], probs[:, :, :], wide, ALU.mult)
            dve.drain()
            for n in range(NT):
                dve.max(top8[:, n, :], probs[:, n, :])
            dve.drain()
            dve.tensor_tensor(gate[:, :, :], probs[:, :, :], top8[:, :, 1:2].broadcast_to([P, NT, E0]),
                              ALU.subtract).then_inc(arg_ready, 1)
            dve.wait_ge(exp_ready, 2)
            dve.tensor_scalar(gate[:, :, :], gate[:, :, :], 1.0, None, ALU.add)
            dve.drain()
            dve.reciprocal(gate[:, :, :], gate[:, :, :])
            dve.drain()
            dve.tensor_tensor(probs[:, :, :], probs[:, :, :], gate[:, :, :], ALU.mult)
            dve.drain()
            dve.tensor_reduce(row[:, :], probs[:, :, :], AX.X, ALU.add)
            dve.drain()
            dve.tensor_scalar(row[:, :], row[:, :], 1e-9, None, ALU.add)
            dve.drain()
            dve.reciprocal(row[:, :], row[:, :])
            dve.drain()
            dve.tensor_tensor(probs[:, :, :], probs[:, :, :], wide, ALU.mult).then_inc(w_ready, 1)
            dve.wait_ge(mix_ready, 1)
            dve.tensor_tensor(u[:, :, :], small[:, :, 0:RANK],
                              pre2[:, :].rearrange("p (n r) -> p n r", n=NT), ALU.mult)
            dve.drain()
            with dve.Fori(0, B) as i:
                dve.wait_ge(left_free, i + 1)
                now = u[:, bass.ds(TB * i, TB), :]
                dve.tensor_copy(left[:, :, 0:RANK].bitcast(F32R), now)
                dve.drain()
                dve.tensor_copy(left[:, :, 2 * RANK:3 * RANK], left[:, :, 0:RANK])
                dve.tensor_tensor(left[:, :, RANK:2 * RANK], now, left[:, :, 0:RANK], ALU.subtract)\
                   .then_inc(left_ready, 1)
                for k in range(TB):
                    dve.wait_ge(*h.at_ready(i, k))
                    dve.scalar_tensor_tensor(out=x[:, TB * i + k, :], in0=h.bank[k % 2][:, :], scalar=0.5,
                                             in1=x[:, TB * i + k, :], op0=ALU.mult, op1=ALU.add)\
                       .then_inc(h.free[k % 2], 1)


def attention(nc, name, kind, x, ident, a):
    pre = f"L{kind}_attn_"
    names = ("Wq", "Wk", "Wv", "Wo") if kind == 0 else ("wq", "wk", "wv", "wo")
    wq, wk, wv, wo = (a[pre + n] for n in names)
    nkv = HKV0 if kind == 0 else H
    kvd = nkv * HD
    with ExitStack() as ctx:
        st = Stage(nc, ctx, name)
        wq_s = (st.sb("wq_hi", [P, KT, D], F32R), st.sb("wq_lo", [P, KT, D], F32R))
        wk_s = (st.sb("wk_hi", [P, KT, kvd], F32R), st.sb("wk_lo", [P, KT, kvd], F32R))
        wv_s = (st.sb("wv_hi", [P, KT, kvd], F32R), st.sb("wv_lo", [P, KT, kvd], F32R))
        wo_s = st.sb("wo", [P, KT, D])
        prepare_weights(nc, name + "w", ident, [(wq, D, *wq_s), (wk, kvd, *wk_s), (wv, kvd, *wv_s),
                                                (wo, D, wo_s, None)])
        attention_loop(nc, name + "l", kind, x, ident, a, wq_s, wk_s, wv_s, wo_s)


def attention_loop(nc, name, kind, x, ident, a, wq, wk, wv, wo):
    nkv = HKV0 if kind == 0 else H
    kvd = nkv * HD
    slots = GH if kind == 0 else 3
    T_STEPS = TB + NG * (GH * TB + 1) + TB
    t_prob = lambda n, k: TB + (n // GH) * (GH * TB + 1) + (n % GH) * TB + k
    t_out = lambda g: TB + g * (GH * TB + 1) + GH * TB
    t_last = lambda k: TB + NG * (GH * TB + 1) + k
    if kind == 0:
        m_k, m_q = (lambda m: 0), (lambda m: 1 if m == 0 else TB + 1 + m)
        m_last = lambda k: TB + 1 + KT + k
        M_STEPS = 2 * TB + 1 + KT
    else:
        m_q, m_k = (lambda m: 0 if m == 0 else TB + 2 * m), (lambda m: 1 if m == 0 else TB + 2 * m + 1)
        m_last = lambda k: TB + 2 * KT + k
        M_STEPS = 2 * TB + 2 * KT
    on_act = (0, 1, 2, 3) if kind == 0 else (1, 2)
    per_group = 16 * 3 * GH * (1 if kind == 0 else 2)

    with ExitStack() as ctx:
        st = Stage(nc, ctx, name)
        t = Ring2(st, "t", T_STEPS)
        m = Ring2(st, "m", M_STEPS)
        s = Ring2(st, "s", H * TB)
        o = Ring2(st, "o", NG)
        xn = st.sb("xn", [P, TB, D])
        norm = Norm(st, x, ident, t, xn)
        cos, sin = st.sb("cos", [P, S]), st.sb("sin", [P, S])
        causal = st.sb("causal", [P, S])
        qk_hi = [st.sb(f"{n}_hi", [P, S], F32R) for n in "qk"]
        qk_lo = [st.sb(f"{n}_lo", [P, S], F32R) for n in "qk"]
        q_stack = st.sb("q_stack", [QK_ROWS, 2, GH, S], F32R)
        k_stack = st.sb("k_stack", [QK_ROWS, 2, GH, S], F32R)
        v_ones = st.sb("v_ones", [P, TB, nkv, VW])
        sc = st.sb("sc", [P, slots, CAUSAL])
        top = st.sb("top", [P, slots, TB])
        shift = st.sb("shift", [P, slots, TB])
        probT = st.sb("probT", [P, GH, CAUSAL])
        osb = st.sb("osb", [P, S])
        recip = st.sb("recip", [P, TB, GH])
        oT = sc[:, :, :].rearrange("p l c -> p (l c)")[:, 0:KT * S].rearrange("p (k c) -> p k c", k=KT)
        tables_loaded = st.sem("tables_loaded")
        loaded = [st.sem("stack_loaded0"), st.sem("stack_loaded1")]
        stack_free = st.sem("stack_free")
        sp_passed, dve_passed = st.sem("sp_passed"), st.sem("dve_passed")
        roped_ready = [st.sem("q_ready"), st.sem("k_ready")]
        shift_ready = st.sem("shift_ready")
        exp_ready = st.sem("exp_ready")
        if kind == 0:
            k_loaded = st.sem("k_loaded")
            k_free = st.sem("k_free")
            ex = st.sb("ex", [P, EX, CAUSAL])
            sel_ready = st.sem("sel_ready")
            NQ = TB - 1
            low, high, mid, cnt, n_low, n_high, is_up, is_down, outside, step_a, step_b, step_c, slope = (
                st.sb(n, [P, GH, NQ]) for n in ("low", "high", "mid", "cnt", "n_low", "n_high", "is_up", "is_down", "outside",
                                                "step_a", "step_b", "step_c", "slope"))
            signs = st.sb("signs", [P, 2, NQ])
            sel_tab = st.sb("sel_tab", [P, NQ, 5])
            sign_tab = st.sb("sign_tab", [P, NQ, 3])
            ranks = st.sb("ranks", [P, 8])
            bn = st.sb("bn", [P, GH, NQ, 6])
            mean_var = st.sb("mean_var", [P, GH, NQ, 2])
            next8 = st.sb("next8", [P, GH * NQ, 8])
            hot8 = st.sb("hot8", [P, GH * NQ, 8])
            after8 = st.sb("after8", [P, GH * NQ, 8])
            flag = st.sb("flag", [P, 32])
            flagT = st.sb("flagT", [P, 32])
            flag4 = st.sb("flag4", [P, 4])
            flag_int = st.sb("flag_int", [P, 1], I32)
            above = st.sb("above", [P, GH, CAUSAL], mybir.dt.int8)
            thr = st.sb("thr", [P, GH, TB])
            mid_ready = st.sem("mid_ready")
            signs_ready = st.sem("signs_ready")
        probs, prob_slots, prob_ready = (ex, EX, sel_ready) if kind == 0 else (sc, slots, exp_ready)
        block = ctx.enter_context(nc.Block())

        @block.sync
        def _(sp):
            sp.dma_start(cos[:, :], a["c_cos"]).then_inc(tables_loaded, 16)
            sp.dma_start(sin[:, :], a["c_sin"]).then_inc(tables_loaded, 16)
            sp.dma_start(causal[:, :], a["c_causal"]).then_inc(tables_loaded, 16)
            if kind == 0:
                sp.dma_start(sel_tab[:, :, :], a["c_select"]).then_inc(tables_loaded, 16)

            def restack(which, j, dst, sem):
                hi, lo = qk_hi[which], qk_lo[which]
                for r, src in enumerate((hi, lo, hi) if which == 0 else (hi, hi, lo)):
                    sp.dma_start(dst[HD * r:HD * (r + 1), :].bitcast(F32),
                                 src[HD * j:HD * (j + 1), :].bitcast(F32)).then_inc(sem, 16)

            with sp.Fori(0, B) as i:
                if kind == 0:
                    hold(sp, sp_passed, roped_ready[1], i + 1)
                    hold(sp, sp_passed, k_free, i + 1)
                    restack(1, 0, k_stack[:, 0, 0, :], k_loaded)
                for c in range(KT):
                    hold(sp, sp_passed, roped_ready[0], i * KT + c + 1)
                    if kind == 1:
                        hold(sp, sp_passed, roped_ready[1], i * KT + c + 1)
                    for g in (2 * c, 2 * c + 1):
                        hold(sp, sp_passed, stack_free, i * NG + g + 1)
                        for j in range(GH):
                            restack(0, (g % 2) * GH + j, q_stack[:, g % 2, j, :], loaded[g % 2])
                            if kind == 1:
                                restack(1, (g % 2) * GH + j, k_stack[:, g % 2, j, :], loaded[g % 2])
                        if kind == 0 and g + 1 < nkv:
                            restack(1, g + 1, k_stack[:, (g + 1) // GH, (g + 1) % GH, :], k_loaded)

        @block.tensor
        def _(pe):
            t.prime(pe)
            m.prime(pe)
            s.prime(pe)

            def project(i, c, which):
                w = (wq, wk)[which]
                step = (m_q, m_k)[which](c)
                pe.wait_ge(*m.at_free(i, step))
                prod3(pe, m.bank[step % 2][:, :], lambda k: (w[0][:, k, c * P:(c + 1) * P], w[1][:, k, c * P:(c + 1) * P]),
                      norm.batch(), range(KT)).then_inc(m.ready, 1)

            def scores(i, n, tiles=range(TB)):
                g, h = n // GH, n % GH
                if h == 0 and 0 in tiles:
                    pe.wait_ge(loaded[g % 2], (i * (NG // 2) + g // 2 + 2) * per_group)
                    if kind == 0:
                        pe.wait_ge(k_loaded, (i * nkv + g + 1) * 16 * 3)
                for q in tiles:
                    step = n * TB + q
                    pe.wait_ge(*s.at_free(i, step))
                    kk = k_stack[:, g // GH, g % GH, :] if kind == 0 else k_stack[:, g % 2, h, :]
                    pe.matmul(s.bank[step % 2][:, 0:(q + 1) * P], q_stack[:, g % 2, h, q * P:(q + 1) * P],
                              kk[:, 0:(q + 1) * P], start=True, stop=True).then_inc(s.ready, 1)
                if h == GH - 1 and TB - 1 in tiles:
                    pe.drain().then_inc(stack_free, 1)

            def turn_probs(i, n):
                pe.wait_ge(prob_ready, i * H + n + 1)
                for k in range(TB):
                    step = t_prob(n, k)
                    pe.wait_ge(*t.at_free(i, step))
                    for q in range(k, TB):
                        last = pe.transpose(t.bank[step % 2][:, (q - k) * P:(q - k + 1) * P],
                                            probs[:, n % prob_slots, ROW_AT[q] + k * P:ROW_AT[q] + (k + 1) * P],
                                            ident[:, :])
                    last.then_inc(t.ready, 1)

            def weigh(i, g):
                for k in (TB - 2, TB - 1):
                    pe.wait_ge(*t.at_used(i, t_prob(GH * g + GH - 1, k)))
                pe.wait_ge(*o.at_free(i, g))
                for k in range(TB):
                    for h in range(GH):
                        kv = g if kind == 0 else GH * g + h
                        last = pe.matmul(o.bank[g % 2][32 * h:32 * h + VW, k * P:S], v_ones[:, k, kv, :],
                                         probT[:, h, COL_AT[k]:COL_AT[k] + (TB - k) * P],
                                         start=k == 0, stop=k == TB - 1, skip_group_check=True)
                last.then_inc(o.ready, 1)

            def turn_out(i, g):
                pe.wait_ge(*o.at_used(i, g))
                pe.wait_ge(*t.at_free(i, t_out(g)))
                for q in range(TB):
                    last = pe.transpose(t.bank[t_out(g) % 2][:, q * P:(q + 1) * P], osb[:, q * P:(q + 1) * P],
                                        ident[:, :])
                last.then_inc(t.ready, 1)

            with pe.Fori(0, B) as i:
                norm.tensor_transpose(pe, i)
                for k in range(TB - 2, TB):
                    pe.wait_ge(*t.at_used(i, k))
                if kind == 0:
                    project(i, 0, 1)
                project(i, 0, 0)
                if kind == 1:
                    project(i, 0, 1)
                for k in range(TB):
                    pe.wait_ge(*m.at_free(i, k + 2))
                    prod3(pe, m.bank[k % 2][:, 0:kvd], norm.tile(k), lambda c: (wv[0][:, c, :], wv[1][:, c, :]),
                          range(KT)).then_inc(m.ready, 1)
                if kind == 0:
                    for g in range(NG):
                        for h in range(g > 0, GH):
                            scores(i, GH * g + h)
                        if g >= 1:
                            weigh(i, g - 1)
                            turn_out(i, g - 1)
                        if g % 2 == 0 and g // 2 + 1 < KT:
                            project(i, g // 2 + 1, 0)
                            if g // 2 + 2 == KT:
                                pe.drain().then_inc(norm.free, 1)
                        if g == NG - 1:
                            pe.drain().then_inc(k_free, 1)
                        else:
                            scores(i, GH * (g + 1), range(2))
                        for h in range(GH):
                            if h == GH - 1 and g + 1 < NG:
                                scores(i, GH * (g + 1), range(2, TB))
                            turn_probs(i, GH * g + h)
                    weigh(i, NG - 1)
                    turn_out(i, NG - 1)
                else:
                    for n in range(H + slots):
                        done = n - slots
                        if done >= 0:
                            turn_probs(i, done)
                            if done % GH == GH - 1:
                                weigh(i, done // GH)
                        if n < H:
                            scores(i, n)
                        if done >= 0 and done % GH == GH - 1:
                            turn_out(i, done // GH)
                        if n % 8 == 4 and n < H and n // 8 + 1 < KT:
                            project(i, n // 8 + 1, 0)
                            project(i, n // 8 + 1, 1)
                            if n // 8 + 2 == KT:
                                pe.drain().then_inc(norm.free, 1)
                pe.wait_ge(*t.at_used(i, t_out(NG - 1)))
                for k in range(TB):
                    pe.wait_ge(*t.at_free(i, t_last(k)))
                    for c in range(KT):
                        last = pe.transpose(t.bank[t_last(k) % 2][:, c * P:(c + 1) * P],
                                            xn[:, k, c * P:(c + 1) * P], ident[:, :])
                    last.then_inc(t.ready, 1)
                pe.drain().then_inc(norm.xn_free, 1)
                for k in range(TB):
                    pe.wait_ge(*t.at_used(i, t_last(k)))
                    pe.wait_ge(*m.at_free(i, m_last(k)))
                    for c in range(KT):
                        last = pe.matmul(m.bank[m_last(k) % 2][:, :], oT[:, c, k * P:(k + 1) * P], wo[:, c, :],
                                         start=c == 0, stop=c == KT - 1)
                    last.then_inc(m.ready, 1)

        def move_probs(eng, copy, i, n, tiles):
            g = n // GH
            for k in tiles:
                step = t_prob(n, k)
                if n % GH == 0 and g >= 1:
                    eng.wait_ge(*o.at_ready(i, g - 1))
                eng.wait_ge(*t.at_ready(i, step))
                copy(probT[:, n % GH, COL_AT[k]:COL_AT[k] + (TB - k) * P],
                     t.bank[step % 2][:, 0:(TB - k) * P]).then_inc(t.free[step % 2], 1)

        @block.scalar
        def _(act):
            norm.prime(act)
            if kind == 0:
                act.sem_inc(k_free, 1)
            copy = lambda out, in_: act.activation(out, in_, ACT.Copy)

            def exps(i, n):
                act.wait_ge(shift_ready, i * H + n + 1)
                if kind == 0 and n >= EX:
                    act.wait_ge(*t.at_ready(i, t_prob(n - EX, TB - 1)))
                for q in range(TB):
                    src = sc[:, n % slots, ROW_AT[q]:ROW_AT[q] + (q + 1) * P]
                    dst = src if kind == 1 else ex[:, n % EX, ROW_AT[q]:ROW_AT[q] + (q + 1) * P]
                    last = act.activation(dst, src, ACT.Exp, bias=shift[:, n % slots, q:q + 1], scale=HD ** -0.5)
                last.then_inc(exp_ready, 1)

            def move_out(i, g):
                act.wait_ge(*o.at_ready(i, g))
                if g >= 1:
                    act.wait_ge(*t.at_ready(i, t_out(g - 1)))
                copy(osb[:, :], o.bank[g % 2][:, :]).then_inc(o.free[g % 2], 1)

            def count_signs(i, g):
                for r in range(SHARED):
                    act.wait_ge(mid_ready, (i * NG + g) * SHARED + r + 1)
                    for h in range(2):
                        for q in range(1, TB):
                            part = slice(ROW_AT[q], ROW_AT[q] + (q + 1) * P)
                            last = act.activation(above[:, 2 + h, part], sc[:, 2 + h, part], ACT.Sign, scale=-1.0,
                                                  bias=mid[:, 2 + h, q - 1:q], accum_out=signs[:, h, q - 1:q])
                    last.then_inc(signs_ready, 1)

            norm.scalar_root(act)
            with act.Fori(0, B) as i:
                norm.scalar_split(act, i)
                for k in range(TB):
                    act.wait_ge(*m.at_ready(i, k + 2))
                    copy(v_ones[:, k, :, 0:HD], m.bank[k % 2][:, 0:kvd].rearrange("p (h d) -> p h d", d=HD))\
                        .then_inc(m.free[k % 2], 1)
                if kind == 0:
                    for g in range(NG):
                        count_signs(i, g)
                        for h in range(EX):
                            exps(i, GH * g + h)
                        for h in range(GH):
                            move_probs(act, copy, i, GH * g + h, on_act)
                            if h + EX < GH:
                                exps(i, GH * g + h + EX)
                        move_out(i, g)
                else:
                    for n in range(H + slots):
                        done = n - slots
                        if done >= 0:
                            move_probs(act, copy, i, done, on_act)
                            if done % GH == GH - 1:
                                move_out(i, done // GH)
                        if n < H:
                            exps(i, n)
                for k in range(TB):
                    act.wait_ge(*t.at_ready(i, t_last(k)))
                    copy(oT[:, :, k * P:(k + 1) * P],
                         t.bank[t_last(k) % 2][:, :].rearrange("p (k c) -> p k c", k=KT))\
                        .then_inc(t.free[t_last(k) % 2], 1)

        @block.vector
        def _(dve):
            dve.memset(q_stack[:, :, :, :].bitcast(F32), 0.0)
            dve.memset(k_stack[:, :, :, :].bitcast(F32), 0.0)
            dve.memset(v_ones[:, :, :, HD:VW], 1.0)
            if kind == 0:
                dve.memset(thr[:, :, :], NEG / 2)
                dve.memset(flag[:, :], 0.0)
                for r in range(8):
                    dve.memset(ranks[:, r:r + 1], float(r))
                for q in range(NQ):
                    w = (q + 2) * P
                    dve.memset(sign_tab[:, q, 0:1], w - 2 * (KEEP + 0.25))
                    dve.memset(sign_tab[:, q, 1:2], w - 2 * (KEEP - 7.25))
                    dve.memset(sign_tab[:, q, 2:3], w / 2)
            for b in range(2):
                dve.memset(o.bank[b][:, :], 0.0)
            dve.drain().then_inc(stack_free, 2)
            o.prime(dve)
            for b in range(2):
                dve.sem_inc(loaded[b], per_group)
            dve.wait_ge(tables_loaded, 48 + 16 * (kind == 0))

            def rope(i, c, which):
                step = (m_q, m_k)[which](c)
                bank = m.bank[step % 2]
                hi, lo = qk_hi[which], qk_lo[which]
                straight, turned = lo[:, :].bitcast(F32), hi[:, :].bitcast(F32)
                if kind == 1 or which == 0:
                    for b in range(2):
                        hold(dve, dve_passed, loaded[b], (i * KT + c + 1) * per_group)
                dve.drain()
                hold(dve, dve_passed, *m.at_ready(i, step))
                dve.tensor_tensor(straight, bank[:, :], cos[:, :], ALU.mult)
                dve.stream_shuffle(turned, bank[:, :], [p ^ (HD // 2) for p in range(32)])\
                   .then_inc(m.free[step % 2], 1)
                dve.drain()
                dve.tensor_tensor(turned, turned, sin[:, :], ALU.mult)
                dve.drain()
                dve.tensor_tensor(straight, straight, turned, ALU.add)
                dve.drain()
                dve.tensor_copy(hi[:, :], straight)
                dve.drain()
                dve.tensor_tensor(lo[:, :], straight, turned, ALU.subtract).then_inc(roped_ready[which], 1)

            def row_max(i, n):
                if kind == 1 and n >= slots:
                    hold(dve, dve_passed, *t.at_ready(i, t_prob(n - slots, TB - 1)))
                for q in range(TB):
                    step, w = n * TB + q, (q + 1) * P
                    hold(dve, dve_passed, *s.at_ready(i, step))
                    dve.tensor_tensor_reduce(sc[:, n % slots, ROW_AT[q]:ROW_AT[q] + w], s.bank[step % 2][:, 0:w],
                                             causal[:, S - w:S], 1.0, 3 * NEG, ALU.add, ALU.max,
                                             top[:, n % slots, q:q + 1]).then_inc(s.free[step % 2], 1)
                dve.drain()
                dve.tensor_scalar(shift[:, n % slots, :], top[:, n % slots, :], -HD ** -0.5, None, ALU.mult)\
                   .then_inc(shift_ready, 1)

            def count(heads):
                for h in heads:
                    for q in range(1, TB):
                        part = slice(ROW_AT[q], ROW_AT[q] + (q + 1) * P)
                        dve.tensor_scalar(above[:, h, part], sc[:, h, part], mid[:, h, q - 1:q], 0.0,
                                          ALU.is_ge, ALU.add, accum_out=cnt[:, h, q - 1:q])

            def narrow(first=False, signed=False, again=False):
                by_count = slice(0, 2 if signed else GH)
                dve.tensor_scalar(is_up[:, by_count, :], cnt[:, by_count, :], KEEP + 0.25, None, ALU.is_gt)
                dve.tensor_scalar(is_down[:, by_count, :], cnt[:, by_count, :], KEEP - 7.25, None, ALU.is_lt)
                if signed:
                    tab = lambda c: sign_tab[:, :, c].unsqueeze(1).broadcast_to([P, 2, NQ])
                    dve.tensor_tensor(is_up[:, 2:GH, :], signs[:, :, :], tab(0), ALU.is_lt)
                    dve.tensor_tensor(is_down[:, 2:GH, :], signs[:, :, :], tab(1), ALU.is_gt)
                    dve.scalar_tensor_tensor(out=cnt[:, 2:GH, :], in0=signs[:, :, :], scalar=-0.5, in1=tab(2),
                                             op0=ALU.mult, op1=ALU.add)
                dve.drain()
                up, down = is_up[:, :, :].bitcast(I32), is_down[:, :, :].bitcast(I32)
                dve.copy_predicated(low[:, :, :], up, mid[:, :, :])
                dve.copy_predicated(high[:, :, :], down, mid[:, :, :])
                dve.copy_predicated(n_low[:, :, :], up, cnt[:, :, :])
                dve.copy_predicated(n_high[:, :, :], down, cnt[:, :, :])
                dve.tensor_tensor(outside[:, :, :], is_up[:, :, :], is_down[:, :, :], ALU.max)
                if first:
                    dve.scalar_tensor_tensor(out=step_a[:, :, :], in0=cnt[:, :, :], scalar=AIM, in1=slope[:, :, :],
                                             op0=ALU.subtract, op1=ALU.mult)
                    dve.drain()
                    dve.tensor_tensor(step_a[:, :, :], step_a[:, :, :], mid[:, :, :], ALU.add)
                else:
                    dve.drain()
                    dve.tensor_tensor(step_b[:, :, :], n_low[:, :, :], n_high[:, :, :], ALU.subtract)
                    dve.tensor_tensor(step_a[:, :, :], high[:, :, :], low[:, :, :], ALU.subtract)
                    dve.drain()
                    dve.reciprocal(step_b[:, :, :], step_b[:, :, :])
                    dve.scalar_tensor_tensor(out=step_a[:, :, :], in0=n_low[:, :, :], scalar=AIM,
                                             in1=step_a[:, :, :], op0=ALU.subtract, op1=ALU.mult)
                    dve.drain()
                    dve.tensor_tensor(step_a[:, :, :], step_a[:, :, :], step_b[:, :, :], ALU.mult)
                    dve.drain()
                    dve.tensor_tensor(step_a[:, :, :], step_a[:, :, :], low[:, :, :], ALU.add)
                dve.drain()
                last = dve.copy_predicated(mid[:, :, :], outside[:, :, :].bitcast(I32), step_a[:, :, :])
                if again:
                    last.then_inc(mid_ready, 1)
                dve.drain()

            def start_search():
                dve.drain()
                for h in range(GH):
                    for q in range(1, TB):
                        dve.bn_stats(bn[:, h, q - 1, :], sc[:, h, ROW_AT[q]:ROW_AT[q] + q * P])
                dve.drain()
                for h in range(GH):
                    for q in range(NQ):
                        dve.bn_aggr(mean_var[:, h, q, :], bn[:, h, q, :])
                dve.tensor_copy(high[:, :, :], top[:, :, 1:TB])
                dve.memset(n_high[:, :, :], 1.0)
                tab = lambda c: sel_tab[:, :, c].unsqueeze(1).broadcast_to([P, GH, NQ])
                dve.tensor_copy(n_low[:, :, :], tab(0))
                dve.drain()
                mean, var = mean_var[:, :, :, 0], mean_var[:, :, :, 1]
                sd = step_a
                dve.tensor_copy(step_b[:, :, :], var)
                dve.scalar_tensor_tensor(out=step_c[:, :, :], in0=mean, scalar=-1.0, in1=mean,
                                         op0=ALU.mult, op1=ALU.max)
                dve.drain()
                dve.tensor_scalar(step_c[:, :, :], step_c[:, :, :], 1e-5, None, ALU.mult)
                dve.tensor_scalar(sd[:, :, :].bitcast(I32), step_b[:, :, :].bitcast(I32), 1, None,
                                  ALU.arith_shift_right)
                dve.drain()
                dve.tensor_scalar(sd[:, :, :].bitcast(I32), sd[:, :, :].bitcast(I32), float(0x1fbd1df5), None, ALU.add)
                dve.drain()
                dve.tensor_tensor(slope[:, :, :], sd[:, :, :], tab(3), ALU.mult)
                dve.tensor_tensor(mid[:, :, :], sd[:, :, :], tab(1), ALU.mult)
                dve.tensor_tensor(low[:, :, :], sd[:, :, :], tab(2), ALU.mult)
                dve.drain()
                dve.tensor_tensor(mid[:, :, :], mid[:, :, :], mean, ALU.add)
                dve.tensor_tensor(low[:, :, :], low[:, :, :], step_c[:, :, :], ALU.add)
                dve.drain()
                dve.tensor_tensor(low[:, :, :], mean, low[:, :, :], ALU.subtract)
                dve.tensor_tensor(mid[:, :, :], mid[:, :, :], high[:, :, :], ALU.min).then_inc(mid_ready, 1)
                dve.drain()

            def still_open():
                return dve.value_load(flag_int[0:1, 0:1], min_val=0, max_val=2)

            def threshold():
                for h in range(GH):
                    for q in range(1, TB):
                        part = slice(ROW_AT[q], ROW_AT[q] + (q + 1) * P)
                        dve.scalar_tensor_tensor(out=probT[:, h, part], in0=above[:, h, part], scalar=2 * NEG,
                                                 in1=sc[:, h, part], op0=ALU.mult, op1=ALU.add)
                cnt_wide = cnt[:, :, :].rearrange("p h q -> p (h q)").unsqueeze(2).broadcast_to([P, GH * NQ, 8])
                ranks_wide = ranks[:, :].unsqueeze(1).broadcast_to([P, GH * NQ, 8])
                dve.tensor_tensor(hot8[:, :, :], cnt_wide, ranks_wide, ALU.add)
                dve.drain()
                for h in range(GH):
                    for q in range(1, TB):
                        part = slice(ROW_AT[q], ROW_AT[q] + (q + 1) * P)
                        dve.max(next8[:, h * NQ + q - 1, :], probT[:, h, part])
                dve.tensor_scalar(after8[:, :, :], hot8[:, :, :], float(KEEP), None, ALU.is_equal)
                dve.tensor_scalar(hot8[:, :, :], hot8[:, :, :], KEEP - 1.0, None, ALU.is_equal)
                dve.drain()
                dve.tensor_tensor(hot8[:, :, :], hot8[:, :, :], next8[:, :, :], ALU.mult)
                dve.tensor_tensor(after8[:, :, :], after8[:, :, :], next8[:, :, :], ALU.mult)
                dve.tensor_scalar(is_up[:, :, :], cnt[:, :, :], float(KEEP), None, ALU.is_equal)
                dve.drain()
                per_row = lambda b: b[:, :, :].rearrange("p (h q) r -> p h q r", h=GH)
                dve.tensor_reduce(thr[:, :, 1:TB], per_row(hot8), AX.X, ALU.add)
                dve.tensor_reduce(step_a[:, :, :], per_row(after8), AX.X, ALU.add)
                dve.drain()
                dve.copy_predicated(thr[:, :, 1:TB], is_up[:, :, :].bitcast(I32), mid[:, :, :])
                dve.drain()
                dve.tensor_tensor(step_a[:, :, :], step_a[:, :, :], thr[:, :, 1:TB], ALU.is_equal)
                dve.tensor_scalar(is_up[:, :, :], cnt[:, :, :], KEEP + 0.25, None, ALU.is_gt)
                dve.tensor_scalar(is_down[:, :, :], cnt[:, :, :], KEEP - 7.25, None, ALU.is_lt)
                dve.drain()
                dve.tensor_tensor(is_up[:, :, :], is_up[:, :, :], is_down[:, :, :], ALU.max)
                dve.drain()
                dve.scalar_tensor_tensor(out=is_up[:, :, :], in0=is_up[:, :, :], scalar=2.0, in1=step_a[:, :, :],
                                         op0=ALU.mult, op1=ALU.max)
                dve.drain()
                dve.tensor_reduce(flag[:, 0:1], is_up[:, :, :], AX.XY, ALU.max)
                dve.drain()
                dve.transpose(flagT[:, :], flag[:, :])
                dve.drain()
                dve.tensor_reduce(flag4[:, 0:1], flagT[:, :], AX.X, ALU.max)
                dve.drain()
                for c in range(1, P // 32):
                    dve.tensor_copy(flag4[0:1, c:c + 1], flag4[32 * c:32 * c + 1, 0:1])
                dve.drain()
                dve.tensor_reduce(flag_int[0:1, :], flag4[0:1, :], AX.X, ALU.max)
                dve.drain()
                return still_open()

            def enclose_thr():
                now = thr[:, :, 1:TB]
                dve.scalar_tensor_tensor(out=step_a[:, :, :], in0=now, scalar=-1.0, in1=now,
                                         op0=ALU.mult, op1=ALU.max)
                dve.tensor_copy(low[:, :, :], now)
                dve.drain()
                dve.tensor_scalar(step_a[:, :, :], step_a[:, :, :], 0.512 * 2.0 ** -23, 1e-30, ALU.mult, ALU.add)
                dve.drain()
                dve.tensor_tensor(high[:, :, :], step_a[:, :, :], now, ALU.add)
                dve.drain()
                dve.tensor_copy(mid[:, :, :], high[:, :, :])
                dve.drain()
                count(range(GH))
                dve.drain()
                dve.tensor_scalar(step_a[:, :, :], cnt[:, :, :], -1.0, float(KEEP), ALU.mult, ALU.add)
                dve.drain()

            def search_slowly():
                most = top[:, :, 1:TB]
                dve.scalar_tensor_tensor(out=step_a[:, :, :], in0=most, scalar=-1.0, in1=most,
                                         op0=ALU.mult, op1=ALU.max)
                dve.memset(n_high[:, :, :], 0.0)
                dve.drain()
                dve.tensor_scalar(step_a[:, :, :], step_a[:, :, :], 1e-6, 1e-30, ALU.mult, ALU.add)
                dve.drain()
                dve.tensor_tensor(high[:, :, :], step_a[:, :, :], most, ALU.add)
                dve.drain()
                with dve.Fori(0, BISECT):
                    dve.tensor_tensor(mid[:, :, :], low[:, :, :], high[:, :, :], ALU.add)
                    dve.drain()
                    dve.tensor_scalar(mid[:, :, :], mid[:, :, :], 0.5, None, ALU.mult)
                    dve.drain()
                    count(range(GH))
                    dve.drain()
                    dve.tensor_scalar(is_up[:, :, :], cnt[:, :, :], KEEP - 0.5, None, ALU.is_gt)
                    dve.tensor_scalar(is_down[:, :, :], cnt[:, :, :], KEEP - 0.5, None, ALU.is_lt)
                    dve.drain()
                    dve.copy_predicated(low[:, :, :], is_up[:, :, :].bitcast(I32), mid[:, :, :])
                    dve.copy_predicated(high[:, :, :], is_down[:, :, :].bitcast(I32), mid[:, :, :])
                    dve.copy_predicated(n_high[:, :, :], is_down[:, :, :].bitcast(I32), cnt[:, :, :])
                    dve.drain()
                dve.tensor_copy(thr[:, :, 1:TB], low[:, :, :])
                dve.tensor_scalar(step_a[:, :, :], n_high[:, :, :], -1.0, float(KEEP), ALU.mult, ALU.add)
                dve.drain()

            def drop_ties(h):
                for q in range(1, TB):
                    w = (q + 1) * P
                    scores = sc[:, h, ROW_AT[q]:ROW_AT[q] + w]
                    beyond, tied = probT[:, h, 0:w], probT[:, h, S:S + w]
                    dve.tensor_scalar(beyond, scores, high[:, h, q - 1:q], None, ALU.is_ge)
                    dve.drain()
                    dve.scalar_tensor_tensor(out=tied, in0=scores, scalar=low[:, h, q - 1:q], in1=beyond,
                                             op0=ALU.is_ge, op1=ALU.subtract)
                    dve.drain()
                    dve.tensor_tensor_scan(beyond, tied, tied, 0.0, ALU.add, ALU.max)
                    dve.drain()
                    dve.scalar_tensor_tensor(out=tied, in0=beyond, scalar=step_a[:, h, q - 1:q], in1=tied,
                                             op0=ALU.is_gt, op1=ALU.mult)
                    dve.drain()
                    dve.scalar_tensor_tensor(out=scores, in0=tied, scalar=2 * NEG, in1=scores,
                                             op0=ALU.mult, op1=ALU.add)
                    dve.drain()

            def keep(g, h):
                slot = (g * GH + h) % EX
                for q in range(TB):
                    part = slice(ROW_AT[q], ROW_AT[q] + (q + 1) * P)
                    last = dve.scalar_tensor_tensor(out=ex[:, slot, part], in0=sc[:, h, part],
                                                    scalar=thr[:, h, q:q + 1], in1=ex[:, slot, part],
                                                    op0=ALU.is_ge, op1=ALU.mult)
                last.then_inc(sel_ready, 1)

            def select(i, g):
                start_search()
                for r in range(SHARED):
                    count(range(2))
                    if r == 0 and g >= 1:
                        out_rows(i, g - 1)
                    if r == 1 and g % 2 == 0 and g // 2 + 1 < KT:
                        rope(i, g // 2 + 1, 0)
                    dve.drain()
                    dve.wait_ge(signs_ready, (i * NG + g) * SHARED + r + 1)
                    narrow(first=r == 0, signed=True, again=r < SHARED - 1)
                count(range(GH))
                dve.drain()
                if g >= 1:
                    dve.wait_ge(*o.at_ready(i, g - 1))
                with dve.If(threshold()):
                    with dve.If(still_open() == 2):
                        for _ in range(2):
                            narrow()
                            count(range(GH))
                            dve.drain()
                        threshold()
                    with dve.If(still_open() == 2):
                        search_slowly()
                    with dve.If(still_open() == 1):
                        enclose_thr()
                    for h in range(GH):
                        hold(dve, dve_passed, exp_ready, i * H + g * GH + h + 1)
                        with dve.If(still_open()):
                            drop_ties(h)
                        keep(g, h)
                with dve.Else():
                    for h in range(GH):
                        dve.wait_ge(exp_ready, i * H + g * GH + h + 1)
                        keep(g, h)
                dve.drain()

            def out_rows(i, g):
                step = t_out(g)
                dve.wait_ge(*t.at_ready(i, step))
                v = t.bank[step % 2][:, :].rearrange("p (q h c) -> p q h c", q=TB, h=GH)
                dve.reciprocal(recip[:, :, :], v[:, :, :, HD])
                dve.drain()
                dve.tensor_tensor(xn[:, :, g * GH * HD:(g + 1) * GH * HD].rearrange("p q (h d) -> p q h d", h=GH),
                                  v[:, :, :, 0:HD], recip[:, :, :].unsqueeze(3).broadcast_to([P, TB, GH, HD]),
                                  ALU.mult).then_inc(t.free[step % 2], 1)

            norm.vector_stats(dve)
            with dve.Fori(0, B) as i:
                norm.vector_norm(dve, i)
                norm.vector_split(dve, i)
                if kind == 0:
                    rope(i, 0, 1)
                rope(i, 0, 0)
                if kind == 1:
                    rope(i, 0, 1)
                if kind == 0:
                    for g in range(NG):
                        for h in range(GH):
                            row_max(i, GH * g + h)
                        select(i, g)
                    out_rows(i, NG - 1)
                else:
                    for n in range(H + slots):
                        done = n - slots
                        if done >= 0:
                            move_probs(dve, dve.tensor_copy, i, done, [k for k in range(TB) if k not in on_act])
                        if n < H:
                            row_max(i, n)
                        if done >= 0 and done % GH == GH - 1:
                            out_rows(i, done // GH)
                        if n % 8 == 4 and n < H and n // 8 + 1 < KT:
                            rope(i, n // 8 + 1, 0)
                            rope(i, n // 8 + 1, 1)
                for k in range(TB):
                    dve.wait_ge(*m.at_ready(i, m_last(k)))
                    dve.tensor_tensor(x[:, TB * i + k, :], m.bank[m_last(k) % 2][:, :], x[:, TB * i + k, :], ALU.add)\
                       .then_inc(m.free[m_last(k) % 2], 1)


def build(nc, a, out):
    with ExitStack() as ctx:
        sb = lambda name, shape, dt=F32: ctx.enter_context(nc.sbuf_tensor(name, shape, dt))
        x = sb("x", [P, NT, D])
        ident = sb("ident", [P, P])
        consts = sb("consts", [P, 2, 16])
        with ExitStack() as c0:
            loaded = nc.alloc_semaphore("start_loaded")
            block = c0.enter_context(nc.Block())

            @block.sync
            def _(sp):
                for b in range(B):
                    sp.dma_start(x[:, TB * b:TB * (b + 1), :],
                                 a["L0_attn_hidden_states"][b].rearrange("(t p) c -> p t c", p=P)).then_inc(loaded, 16)
                sp.dma_start(ident[:, :], a["c_ident"]).then_inc(loaded, 16)
                sp.dma_start(consts[:, :, :], a["c_rows"]).then_inc(loaded, 16)
                sp.wait_ge(loaded, 16 * (B + 2))
        f0 = {k: a["L0_ffn_" + k] for k in ("b", "A", "Bmat", "LiMEs")} | {"W": a["L0_ffn_W"]}
        f1 = {k: a["L1_ffn_" + k] for k in ("lora_A", "lora_B", "router_W", "router_b", "domain_prior", "active")} \
            | {"W": a["L1_ffn_W_base"], "b": a["L1_ffn_b_base"]}
        ffn(nc, "f0a", 0, x, ident, consts, f0, a)
        attention(nc, "at0", 0, x, ident, a)
        ffn(nc, "f0b", 0, x, ident, consts, f0, a)
        ffn(nc, "f1a", 1, x, ident, consts, f1, a)
        attention(nc, "at1", 1, x, ident, a)
        ffn(nc, "f1b", 1, x, ident, consts, f1, a, out)


def ffn(nc, name, kind, x, ident, consts, ins, a, out=None):
    with ExitStack() as ctx:
        sb = lambda n, shape, dt=F32: ctx.enter_context(nc.sbuf_tensor(f"{name}_{n}", shape, dt))
        w_hi, w_lo = sb("w_hi", [P, KT, D], F32R), sb("w_lo", [P, KT, D], F32R)
        s_hi, s_lo = sb("s_hi", [P, KT, 48], F32R), sb("s_lo", [P, KT, 48], F32R)
        stack = sb("stack", [P, D], F32R)
        extra = {"out": out}
        if kind == 0:
            extra |= {"bias8": sb("bias8", [P, E0]), "limes_bd": sb("limes_bd", [P, NT, RANK]),
                      "tile_mask": sb("tile_mask", [P, NT]), "small": sb("small", [P, NT, 48])}
            with ExitStack() as c0:
                loaded = nc.alloc_semaphore(f"{name}_mask_loaded")
                block = c0.enter_context(nc.Block())

                @block.sync
                def _(sp):
                    sp.dma_start(extra["tile_mask"][:, :], a["c_tile_mask"]).then_inc(loaded, 16)
                    sp.wait_ge(loaded, 16)
        else:
            extra |= {"logit_bias": sb("logit_bias", [P, E_ACT])}
        prepare_weights(nc, name + "w", ident, [(ins["W"], D, w_hi, w_lo)])
        ffn_weights(nc, name + "s", ident, consts[:, kind, :], kind, ins["W"], w_hi, w_lo, s_hi, s_lo, stack,
                    extra, ins)
        ffn_loop(nc, name + "l", kind, x, ident, w_hi, w_lo, s_hi, s_lo, stack, extra)
        if kind == 0:
            ffn0_route(nc, name + "r", x, ident, stack, extra)


_INS = ["L0_attn_hidden_states", "L0_attn_Wq", "L0_attn_Wk", "L0_attn_Wv", "L0_attn_Wo", "L0_ffn_W", "L0_ffn_b",
        "L0_ffn_A", "L0_ffn_Bmat", "L0_ffn_LiMEs", "L1_attn_wq", "L1_attn_wk", "L1_attn_wv", "L1_attn_wo",
        "L1_ffn_W_base", "L1_ffn_b_base", "L1_ffn_lora_A", "L1_ffn_lora_B", "L1_ffn_router_W", "L1_ffn_router_b",
        "L1_ffn_domain_prior", "L1_ffn_active"]


def shape_constants():
    p = np.arange(P)
    rows = np.zeros((P, 2, 16), np.float32)
    scale = (0.5, 2.0)
    for kind in range(2):
        rows[:, kind, 0] = np.where(p < ONES_AT, scale[kind], 1.0)
        lo = ((p >= 2 * RANK) & (p < ONES_AT)) | (p == ONES_AT + 1)
        rows[:, kind, 1] = ~lo
        rows[:, kind, 2] = lo
        rows[:, kind, 3] = p
        rows[:, kind, 4] = p // R1
        rows[:, kind, 8:16] = p[:, None] % R1 == np.arange(R1)
    half = HD // 2
    inv = (1.0 / 10000.0 ** (np.arange(0, HD, 2, dtype=np.float32) / np.float32(HD))).astype(np.float32)
    freqs = np.outer(np.arange(S, dtype=np.float32), inv).astype(np.float32)
    d = p % HD
    cos = np.cos(freqs).astype(np.float32)[:, d % half].T
    sin = np.sin(freqs).astype(np.float32)[:, d % half].T * np.where(d < half, -1.0, 1.0)[:, None]
    causal = np.zeros((P, S), np.float32)
    causal[:, S - P:] = np.where(p[:, None] < p[None, :], NEG, 0.0)
    grid = np.linspace(-6, 6, 120001)
    density = np.exp(-grid ** 2 / 2) / (2 * np.pi) ** 0.5
    share_below = np.cumsum(density) * (grid[1] - grid[0])
    select = np.zeros((P, TB - 1, 5), np.float32)
    for q in range(1, TB):
        for r in range(P):
            n = q * P + r + 1
            z = np.interp(1 - AIM / n, share_below, grid)
            select[r, q - 1, :4] = n, z, 1.1 * (q * P) ** 0.5, 1 / (n * np.interp(z, grid, density))
    return {"c_select": select, "c_ident": np.eye(P, dtype=np.float32), "c_rows": rows,
            "c_tile_mask": (p[:, None] // E0 == np.arange(NT)).astype(np.float32),
            "c_cos": np.ascontiguousarray(cos), "c_sin": np.ascontiguousarray(sin.astype(np.float32)),
            "c_causal": causal}


def kernel(**inputs):
    import concourse.bacc as _bacc
    from concourse import mybir as _mybir
    from concourse.bass_utils import run_bass_kernel_spmd as _run

    nc = _bacc.Bacc("TRN2", target_bir_lowering=False, num_devices=1)
    arrays, args = {}, {}
    for name, v in [(n, inputs[n]) for n in _INS] + list(shape_constants().items()):
        v = np.ascontiguousarray(v)
        arrays[f"in_{name}"] = v
        args[name] = nc.dram_tensor(f"in_{name}", v.shape, _mybir.dt.from_np(v.dtype), kind="ExternalInput").ap()
    out = nc.dram_tensor("out_x", (B, S, D), F32, kind="ExternalOutput").ap()
    build(nc, args, out)
    r = _run(nc, [arrays], core_ids=[0])
    return r.results[0]["out_x"]
```

```python
from contextlib import ExitStack

import numpy as np

import concourse.bass as bass
from concourse import mybir

F32 = mybir.dt.float32
F32R = mybir.dt.float32r
I32 = mybir.dt.int32
ACT = mybir.ActivationFunctionType
ALU = mybir.AluOpType
AX = mybir.AxisListType
RMAX = bass.bass_isa.ReduceOp.max

P = 128
B, S, D = 4, 512, 512
TB = S // P
NT = B * TB
KT = D // P
LN_EPS = 1e-5

RANK = 32
E0 = 8
NGRAM = 2
E_TOT, E_ACT, R1 = 16, 4, 8
STACK = 128
ONES_AT = 3 * RANK
SMALL = 96

H, HD = 32, 16
HKV0 = 8
KEEP = 128
GH = 4
NG = H // GH
VW = HD + 1
QK_ROWS = 96
CAUSAL = TB * (TB + 1) // 2 * P
ROW_AT = [P * (t * (t + 1) // 2) for t in range(TB)]
COL_AT = [sum((TB - j) * P for j in range(k)) for k in range(TB)]
NEG = -1.0e30
AIM = KEEP - 3.5
SHARED = 4
EX = 4
BISECT = 60


def prod3(pe, out, lhs, rhs, ks, start=True, stop=True):
    n, last = len(ks), None
    for c, k in enumerate(ks):
        (lh, ll), (rh, rl) = lhs(k), rhs(k)
        pe.matmul(out, lh, rh, start=start and c == 0, stop=False)
        pe.matmul(out, lh, rl, start=False, stop=False)
        last = pe.matmul(out, ll, rh, start=False, stop=stop and c == n - 1)
    return last


def hold(eng, passed, sem, value):
    eng.wait_ge(sem, value)
    eng.sem_inc(passed, 1)


class Stage:

    def __init__(self, nc, ctx, name):
        self.nc, self.ctx, self.name = nc, ctx, name
        self.sems = []
        ctx.callback(self.clear)

    def sb(self, name, shape, dt=F32):
        return self.ctx.enter_context(self.nc.sbuf_tensor(f"{self.name}_{name}", shape, dt))

    def ps(self, name, n=512):
        return self.ctx.enter_context(self.nc.psum_tensor(f"{self.name}_{name}", [P, n], F32))

    def sem(self, name):
        self.sems.append(self.nc.alloc_semaphore(f"{self.name}_{name}"))
        return self.sems[-1]

    def clear(self):
        if self.sems:
            self.nc.clear_and_free_semaphores(self.sems)
            self.nc.all_engine_barrier()


class Ring2:

    def __init__(self, st, name, steps, before=0):
        self.bank = [st.ps(f"{name}{b}") for b in range(2)]
        self.ready = st.sem(f"{name}_ready")
        self.free = [st.sem(f"{name}_free{b}") for b in range(2)]
        self.steps, self.before = steps, before
        self.per = [(steps + 1) // 2, steps // 2]

    def prime(self, eng):
        for f in self.free:
            eng.sem_inc(f, 1)

    def at_free(self, i, k):
        return self.free[k % 2], i * self.per[k % 2] + (k + self.before) // 2 + 1

    def at_used(self, i, k):
        return self.free[k % 2], i * self.per[k % 2] + (k + self.before) // 2 + 2

    def at_ready(self, i, k):
        return self.ready, i * self.steps + k + self.before + 1


def prepare_weights(nc, name, ident, x, ln, jobs):
    mv, rs = ln
    with ExitStack() as ctx:
        st = Stage(nc, ctx, name)
        raw = st.sb("raw", [P, 2, KT, D])
        t = Ring2(st, "wt", len(jobs) * KT)
        loaded = [st.sem("loaded0"), st.sem("loaded1")]
        raw_used = st.sem("raw_used")
        hi_ready = st.sem("hi_ready")
        stats = st.sb("stats", [P, NT, 6])
        ve = st.sb("ve", [P, NT])
        sd = st.sb("sd", [P, NT])
        var_ready = st.sem("var_ready")
        std_ready = st.sem("std_ready")
        block = ctx.enter_context(nc.Block())

        @block.sync
        def _(sp):
            for j, (w, n_out, _, _) in enumerate(jobs):
                if j >= 2:
                    sp.wait_ge(raw_used, j - 1)
                sp.dma_start(raw[:, j % 2, 0:n_out // P, :],
                             w.rearrange("(a p) i -> p a i", p=P)).then_inc(loaded[j % 2], 16)

        @block.tensor
        def _(pe):
            for j, (_, n_out, _, _) in enumerate(jobs):
                pe.wait_ge(loaded[j % 2], 16 * (j // 2 + 1))
                for k in range(KT):
                    step = j * KT + k
                    if step >= 2:
                        pe.wait_ge(t.free[step % 2], step // 2)
                    for a in range(n_out // P):
                        last = pe.transpose(t.bank[step % 2][:, a * P:(a + 1) * P],
                                            raw[:, j % 2, a, k * P:(k + 1) * P], ident[:, :])
                    last.then_inc(t.ready, 1)
                pe.drain().then_inc(raw_used, 1)

        @block.scalar
        def _(act):
            for j, (_, n_out, hi, lo) in enumerate(jobs):
                for k in range(KT):
                    step = j * KT + k
                    act.wait_ge(t.ready, step + 1)
                    ins = act.activation(hi[:, k, :], t.bank[step % 2][:, 0:n_out], ACT.Copy)
                    ins.then_inc(hi_ready if lo is not None else t.free[step % 2], 1)
            act.wait_ge(var_ready, 1)
            act.activation(sd[:, :], ve[:, :], ACT.Sqrt).then_inc(std_ready, 1)

        @block.vector
        def _(dve):
            for n in range(NT):
                dve.bn_stats(stats[:, n, :], x[:, n, :])
            dve.drain()
            for n in range(NT):
                dve.bn_aggr(mv[:, n, :], stats[:, n, :])
            dve.drain()
            dve.tensor_scalar(ve[:, :], mv[:, :, 1], LN_EPS, None, ALU.add).then_inc(var_ready, 1)
            n_hi = 0
            for j, (_, n_out, hi, lo) in enumerate(jobs):
                for k in range(KT):
                    step = j * KT + k
                    if lo is not None:
                        n_hi += 1
                        dve.wait_ge(hi_ready, n_hi)
                        dve.tensor_tensor(lo[:, k, :], t.bank[step % 2][:, 0:n_out],
                                          hi[:, k, :].bitcast(F32), ALU.subtract).then_inc(t.free[step % 2], 1)
            dve.wait_ge(std_ready, 1)
            dve.reciprocal(rs[:, :], sd[:, :])


class Norm:

    def __init__(self, st, x, ln, ident, t, xn):
        self.x, self.ident, self.t, self.xn = x, ident, t, xn
        self.mv, self.rs = ln
        self.hi = st.sb("xT_hi", [P, KT, S], F32R)
        self.lo = st.sb("xT_lo", [P, KT, S], F32R)
        self.now = st.sb("now", [P, 2, TB])
        self.xn_ready = st.sem("xn_ready")
        self.xn_free = st.sem("xn_free")
        self.hi_ready = st.sem("xhi_ready")
        self.free = st.sem("xT_free")

    def prime(self, eng):
        eng.sem_inc(self.xn_free, 1)
        eng.sem_inc(self.free, 1)

    def vector_norm(self, dve, i, ahead=0):
        first = TB * i + TB * ahead
        dve.tensor_copy(self.now[:, 0, :], self.mv[:, bass.ds(first, TB), 0])
        dve.tensor_copy(self.now[:, 1, :], self.rs[:, bass.ds(first, TB)])
        dve.drain()
        dve.wait_ge(self.xn_free, i + 1 + ahead)
        for t in range(TB):
            dve.tensor_scalar(self.xn[:, t, :], self.x[:, first + t, :], self.now[:, 0, t:t + 1],
                              self.now[:, 1, t:t + 1], ALU.subtract, ALU.mult).then_inc(self.xn_ready, 1)

    def tensor_transpose(self, pe, i, ahead=0, step=0):
        for t in range(TB):
            pe.wait_ge(self.xn_ready, i * TB + ahead * TB + t + 1)
            pe.wait_ge(*self.t.at_free(i, step + t))
            for k in range(KT):
                last = pe.transpose(self.t.bank[t % 2][:, k * P:(k + 1) * P],
                                    self.xn[:, t, k * P:(k + 1) * P], self.ident[:, :])
            last.then_inc(self.t.ready, 1)

    def scalar_split(self, act, i, ahead=0, step=0):
        act.wait_ge(self.free, i + ahead + 1)
        for t in range(TB):
            act.wait_ge(*self.t.at_ready(i, step + t))
            act.activation(self.hi[:, :, t * P:(t + 1) * P], self.t.bank[t % 2][:, :], ACT.Copy)\
               .then_inc(self.hi_ready, 1)

    def vector_split(self, dve, i, ahead=0):
        for t in range(TB):
            dve.wait_ge(self.hi_ready, i * TB + ahead * TB + t + 1)
            dve.tensor_tensor(self.lo[:, :, t * P:(t + 1) * P],
                              self.t.bank[t % 2][:, :].rearrange("p (k c) -> p k c", k=KT),
                              self.hi[:, :, t * P:(t + 1) * P].bitcast(F32), ALU.subtract)\
               .then_inc(self.t.free[t % 2], 1)

    def tile(self, t):
        return lambda k: (self.hi[:, k, t * P:(t + 1) * P], self.lo[:, k, t * P:(t + 1) * P])

    def batch(self):
        return lambda k: (self.hi[:, k, :], self.lo[:, k, :])


def ffn_weights(nc, name, ident, consts, kind, w_hi, w_lo, small_hi, small_lo, stack, extra, ins):
    with ExitStack() as ctx:
        st = Stage(nc, ctx, name)
        raw = st.sb("raw", [P, D])
        scaled = st.sb("scaled", [P, D])
        rounded = st.sb("rounded", [P, D], F32R)
        rest = st.sb("rest", [P, D])
        bank = st.ps("bank")
        bank2 = st.ps("bank2")
        small = st.sb("small", [P, KT, SMALL])
        loaded = st.sem("loaded")
        cleared = st.sem("cleared")
        built = st.sem("built")
        turned = st.sem("turned")
        vec = st.sem("vec")
        bias = ins["b"].rearrange("(a o) -> a o", a=1)

        if kind == 0:
            a_raw = st.sb("a_raw", [P, KT, RANK])
            aT = st.sb("aT", [RANK, D])
            limesT = st.sb("limesT", [RANK, E0])
            limes_rep = st.sb("limes_rep", [P, RANK])
            block = ctx.enter_context(nc.Block())

            @block.sync
            def _(sp):
                sp.wait_ge(cleared, 1)
                for r in range(3):
                    sp.dma_start(raw[RANK * r:RANK * (r + 1), :], ins["Bmat"]).then_inc(loaded, 16)
                for r in range(2):
                    sp.dma_start(raw[ONES_AT + r:ONES_AT + r + 1, :], bias).then_inc(loaded, 16)
                sp.dma_start(a_raw[:, :, :], ins["A"].rearrange("(k p) r -> p k r", p=P)).then_inc(loaded, 16)
                with nc.allow_non_contiguous_dma(reason="256 numbers"):
                    sp.dma_start(limesT[:, :], ins["LiMEs"].rearrange("e r -> r e")).then_inc(loaded, 16)
                sp.dma_start(limes_rep[:, :], ins["LiMEs"].unsqueeze(0).broadcast_to([NT, E0, RANK])).then_inc(loaded, 16)
                sp.dma_start(extra["tile_mask"][:, :], extra["mask_table"]).then_inc(loaded, 16)
                sp.dma_start(extra["bias8"][:, :], bias[:, 0:E0].broadcast_to([P, E0])).then_inc(loaded, 16)

            @block.tensor
            def _(pe):
                pe.wait_ge(loaded, 16 * 10)
                for k in range(KT):
                    last = pe.transpose(bank[0:RANK, k * P:(k + 1) * P], a_raw[:, k, :], ident[:, :])
                last.then_inc(turned, 1)
                pe.wait_ge(vec, 1)
                for k in range(KT):
                    last = pe.matmul(bank2[:, k * E0:(k + 1) * E0], aT[:, k * P:(k + 1) * P], limesT[:, :],
                                     start=True, stop=True)
                last.then_inc(turned, 1)

            @block.vector
            def _(dve):
                dve.memset(raw[:, :], 0.0).then_inc(cleared, 1)
                dve.memset(small[:, :, :], 0.0)
                dve.drain()
                dve.wait_ge(loaded, 16 * 10)
                dve.wait_ge(turned, 1)
                dve.tensor_copy(aT[:, :], bank[0:RANK, :]).then_inc(vec, 1)
                dve.tensor_scalar(scaled[:, :], raw[:, :], consts[:, 0:1], None, ALU.mult)
                dve.tensor_tensor(extra["limes_bd"][:, :, :],
                                  limes_rep[:, :].unsqueeze(1).broadcast_to([P, NT, RANK]),
                                  extra["tile_mask"][:, :].unsqueeze(2).broadcast_to([P, NT, RANK]), ALU.mult)
                dve.tensor_copy(small[:, :, 0:RANK], a_raw[:, :, :])
                dve.wait_ge(turned, 2)
                dve.tensor_copy(small[:, :, RANK + E0:48],
                                bank2[:, 0:KT * E0].rearrange("p (k e) -> p k e", k=KT))
                dve.drain()
                dve.tensor_tensor(small[:, :, RANK:RANK + E0], w_hi[:, :, 0:E0].bitcast(F32),
                                  w_lo[:, :, 0:E0].bitcast(F32), ALU.add)
                split_small(dve, small, small_hi, small_lo)
                split_stack(dve, stack, scaled, rounded, rest, consts)
        else:
            lora_a = st.sb("lora_a", [E_TOT * R1, D])
            lora_b = st.sb("lora_b", [P, KT, E_TOT, R1])
            lora_bT = st.sb("lora_bT", [E_TOT * R1, D])
            router = st.sb("router", [E_TOT, D])
            rows = st.sb("rows", [E_TOT, 2])
            rows_wide = st.sb("rows_wide", [E_TOT, 2, P])
            act_i = st.sb("act_i", [P, E_ACT], I32)
            act_f = st.sb("act_f", [P, E_ACT])
            sel_e = st.sb("sel_e", [P, E_ACT])
            sel = st.sb("sel", [P, E_ACT, R1])
            prior_log = st.sb("prior_log", [P, E_ACT])
            prior = st.sb("prior", [P, E_ACT])
            block = ctx.enter_context(nc.Block())

            @block.sync
            def _(sp):
                sp.wait_ge(cleared, 1)
                for r in range(2):
                    sp.dma_start(raw[ONES_AT + r:ONES_AT + r + 1, :], bias).then_inc(loaded, 16)
                sp.dma_start(lora_a[:, :], ins["lora_A"].rearrange("e r h -> (e r) h")).then_inc(loaded, 16)
                for k in range(KT):
                    sp.dma_start(lora_b[:, k, :, :],
                                 ins["lora_B"][:, k * P:(k + 1) * P, :].rearrange("e o r -> o e r"))\
                      .then_inc(loaded, 16)
                sp.dma_start(router[:, :], ins["router_W"]).then_inc(loaded, 16)
                with nc.allow_non_contiguous_dma(reason="16 numbers each"):
                    sp.dma_start(rows[:, 0:1], ins["router_b"].rearrange("(e a) -> e a", a=1)).then_inc(loaded, 16)
                    sp.dma_start(rows[:, 1:2], ins["domain_prior"].rearrange("(e a) -> e a", a=1))\
                      .then_inc(loaded, 16)
                sp.dma_start(act_i[:, :], ins["active"].rearrange("(a j) -> a j", a=1).broadcast_to([P, E_ACT]))\
                  .then_inc(loaded, 16)

            @block.tensor
            def _(pe):
                pe.wait_ge(loaded, 16 * 11)
                for k in range(KT):
                    last = pe.transpose(bank[:, k * P:(k + 1) * P],
                                        lora_b[:, k, :, :].rearrange("p e r -> p (e r)"), ident[:, :])
                last.then_inc(turned, 1)
                pe.wait_ge(vec, 1)
                for k in range(KT):
                    pe.matmul(bank2[:, k * 40:k * 40 + RANK], lora_a[:, k * P:(k + 1) * P],
                              sel[:, :, :].rearrange("p j r -> p (j r)"), start=True, stop=True)
                    pe.matmul(bank2[:, k * 40 + RANK:k * 40 + RANK + E_ACT], router[:, k * P:(k + 1) * P],
                              sel_e[0:E_TOT, :], start=True, stop=True)
                for c in range(2):
                    last = pe.matmul(bank2[:, 160 + 4 * c:164 + 4 * c], rows_wide[:, c, :], sel_e[0:E_TOT, :],
                                     start=True, stop=True)
                last.then_inc(turned, 1)
                pe.wait_ge(vec, 2)
                pe.matmul(bank[0:RANK, :], sel[:, :, :].rearrange("p j r -> p (j r)"), lora_bT[:, :],
                          start=True, stop=True).then_inc(turned, 1)

            @block.scalar
            def _(act):
                act.wait_ge(vec, 3)
                act.activation(prior_log[:, :], prior[:, :], ACT.Ln).then_inc(built, 1)

            @block.vector
            def _(dve):
                dve.memset(raw[:, :], 0.0).then_inc(cleared, 1)
                dve.memset(small[:, :, :], 0.0)
                dve.drain()
                dve.wait_ge(loaded, 16 * 11)
                dve.tensor_copy(act_f[:, :], act_i[:, :])
                dve.tensor_copy(rows_wide[:, :, :], rows[:, :].unsqueeze(2).broadcast_to([E_TOT, 2, P]))
                dve.drain()
                dve.tensor_scalar(sel_e[:, :], act_f[:, :], consts[:, 3:4], None, ALU.is_equal)
                dve.tensor_scalar(act_f[:, :], act_f[:, :], consts[:, 4:5], None, ALU.is_equal)
                dve.drain()
                dve.tensor_tensor(sel[:, :, :], act_f[:, :].unsqueeze(2).broadcast_to([P, E_ACT, R1]),
                                  consts[:, 8:8 + R1].unsqueeze(1).broadcast_to([P, E_ACT, R1]), ALU.mult)\
                   .then_inc(vec, 1)
                dve.wait_ge(turned, 1)
                dve.tensor_copy(lora_bT[:, :], bank[:, :]).then_inc(vec, 1)
                dve.wait_ge(turned, 2)
                dve.tensor_scalar(prior[:, :], bank2[:, 164:168], 1e-12, None, ALU.add).then_inc(vec, 1)
                dve.tensor_copy(small[:, :, 0:36], bank2[:, 0:160].rearrange("p (k c) -> p k c", c=40)[:, :, 0:36])
                dve.wait_ge(built, 1)
                dve.tensor_tensor(extra["logit_bias"][:, :], bank2[:, 160:164], prior_log[:, :], ALU.add)
                dve.drain()
                dve.wait_ge(turned, 3)
                for r in range(3):
                    dve.tensor_copy(raw[RANK * r:RANK * (r + 1), :], bank[0:RANK, :])
                dve.drain()
                dve.tensor_scalar(scaled[:, :], raw[:, :], consts[:, 0:1], None, ALU.mult)
                split_small(dve, small, small_hi, small_lo)
                split_stack(dve, stack, scaled, rounded, rest, consts)


def split_small(dve, small, small_hi, small_lo):
    dve.drain()
    dve.tensor_copy(small_hi[:, :, :], small[:, :, :])
    dve.drain()
    dve.tensor_tensor(small_lo[:, :, :], small[:, :, :], small_hi[:, :, :].bitcast(F32), ALU.subtract)


def split_stack(dve, stack, scaled, rounded, rest, consts):
    dve.drain()
    dve.tensor_copy(rounded[:, :], scaled[:, :])
    dve.drain()
    dve.tensor_tensor(rest[:, :], scaled[:, :], rounded[:, :].bitcast(F32), ALU.subtract)
    dve.drain()
    dve.tensor_scalar(rest[:, :], rest[:, :], consts[:, 2:3], None, ALU.mult)
    dve.drain()
    dve.scalar_tensor_tensor(out=stack[:, :], in0=rounded[:, :].bitcast(F32), scalar=consts[:, 1:2],
                             in1=rest[:, :], op0=ALU.mult, op1=ALU.add)


def ffn_loop(nc, name, kind, x, ln, ident, w_hi, w_lo, small_hi, small_lo, stack, extra):
    n_small = 48 if kind == 0 else 36
    turns = TB if kind == 0 else 2 * TB
    with ExitStack() as ctx:
        st = Stage(nc, ctx, name)
        t = Ring2(st, "t", turns)
        xn = st.sb("xn", [P, TB, D])
        norm = Norm(st, x, ln, ident, t, xn)
        h = [st.ps(f"h{k}") for k in range(TB)]
        sm = st.ps("sm")
        sm_wide = st.ps("sm_wide")
        smT = st.sb("smT", [P, S])
        wide_ready = st.sem("wide_ready")
        smT_ready = st.sem("smT_ready")
        smv = sm[:, :].rearrange("p (t c) -> p t c", c=P)
        h_ready = st.sem("h_ready")
        h_free = st.sem("h_free")
        sm_ready = st.sem("sm_ready")
        sm_free = st.sem("sm_free")
        ready0 = st.sem("consts_ready")
        left = st.sb("left", [P, TB, STACK])
        leftT = st.sb("leftT", [P, TB, P], F32R)
        if kind == 1:
            logit = st.sb("logit", [P, TB, E_ACT])
            top = st.sb("top", [P, TB])
            ex = st.sb("ex", [P, TB, E_ACT])
            total = st.sb("total", [P, TB])
            alpha = st.sb("alpha", [P, TB, E_ACT])
            u = st.sb("u", [P, TB, RANK])
            logit_ready = st.sem("logit_ready")
            ex_ready = st.sem("ex_ready")
            left_ready = st.sem("left_ready")
            left_free = st.sem("left_free")
            out = extra.get("out")
            stored = st.sem("stored")
            passed = st.sem("passed")
        block = ctx.enter_context(nc.Block())

        @block.tensor
        def _(pe):
            t.prime(pe)
            pe.wait_ge(ready0, 1)
            with pe.Fori(0, B) as i:
                norm.tensor_transpose(pe, i)
                pe.drain().then_inc(norm.xn_free, 1)
                for k in range(TB - 2, TB):
                    pe.wait_ge(*t.at_used(i, k))
                prod3(pe, sm_wide[0:SMALL, :], lambda c: (small_hi[:, c, :], small_lo[:, c, :]), norm.batch(),
                      range(KT)).then_inc(wide_ready, 1)
                for k in range(TB):
                    pe.wait_ge(h_free, i * TB + k + 1)
                    prod3(pe, h[k][:, :], norm.tile(k), lambda c: (w_hi[:, c, :], w_lo[:, c, :]), range(KT),
                          stop=False)
                    if kind == 0:
                        pe.matmul(h[k][:, :], leftT[:, 0, :], stack[:, :], start=False, stop=True)\
                          .then_inc(h_ready, 1)
                    if k == 0:
                        pe.wait_ge(smT_ready, i + 1)
                        pe.wait_ge(sm_free, i + 1)
                        for q in range(TB):
                            last = pe.transpose(smv[:, q, :], smT[:, q * P:(q + 1) * P], ident[:, :])
                        last.then_inc(sm_ready, 1)
                pe.drain().then_inc(norm.free, 1)
                if kind == 1:
                    for k in range(TB):
                        pe.wait_ge(left_ready, i * TB + k + 1)
                        pe.wait_ge(*t.at_free(i, TB + k))
                        pe.transpose(t.bank[k % 2][:, 0:P], left[:, k, :], ident[:, :]).then_inc(t.ready, 1)
                    for k in range(TB):
                        pe.wait_ge(*t.at_used(i, TB + k))
                        pe.matmul(h[k][:, :], leftT[:, k, :], stack[:, :], start=False, stop=True)\
                          .then_inc(h_ready, 1)
                    pe.drain().then_inc(left_free, 1)

        @block.scalar
        def _(act):
            norm.prime(act)
            act.sem_inc(sm_free, 1)
            act.sem_inc(h_free, TB)
            if kind == 1:
                act.sem_inc(left_free, 1)
            with act.Fori(0, B) as i:
                norm.scalar_split(act, i)
                act.wait_ge(wide_ready, i + 1)
                act.activation(smT[0:SMALL, :], sm_wide[0:SMALL, :], ACT.Copy).then_inc(smT_ready, 1)
                if kind == 0:
                    act.wait_ge(sm_ready, i + 1)
                    act.activation(extra["small"][:, bass.ds(TB * i, TB), :], smv[:, :, 0:n_small], ACT.Copy)\
                       .then_inc(sm_free, 1)
                else:
                    act.wait_ge(logit_ready, i + 1)
                    act.activation(ex[:, :, :], logit[:, :, :], ACT.Exp).then_inc(ex_ready, 1)
                    act.wait_ge(left_free, i + 1)
                    for k in range(TB):
                        act.wait_ge(*t.at_ready(i, TB + k))
                        act.activation(leftT[:, k, :], t.bank[k % 2][:, 0:P], ACT.Copy)\
                           .then_inc(t.free[k % 2], 1)

        @block.vector
        def _(dve):
            dve.memset(left[:, :, :], 0.0)
            dve.memset(smT[:, :], 0.0)
            dve.drain()
            dve.memset(left[:, :, ONES_AT:ONES_AT + 2], 1.0)
            if kind == 0:
                ones = left[:, 1, :]
                dve.drain()
                dve.memset(ones, 0.0)
                dve.drain()
                dve.memset(left[ONES_AT:P, 1, :], 1.0)
                dve.drain()
                dve.tensor_copy(leftT[:, 0, :], ones).then_inc(ready0, 1)
            else:
                dve.drain().then_inc(ready0, 1)
            norm.vector_norm(dve, 0)
            def batch(i, last):
                norm.vector_split(dve, i)
                if kind == 1:
                    dve.wait_ge(sm_ready, i + 1)
                    dve.tensor_tensor(logit[:, :, :], smv[:, :, RANK:RANK + E_ACT],
                                      extra["logit_bias"][:, :].unsqueeze(1).broadcast_to([P, TB, E_ACT]), ALU.add)
                    dve.drain()
                    dve.tensor_reduce(top[:, :], logit[:, :, :], AX.X, ALU.max)
                    dve.drain()
                    dve.tensor_tensor(logit[:, :, :], logit[:, :, :],
                                      top[:, :].unsqueeze(2).broadcast_to([P, TB, E_ACT]), ALU.subtract)\
                       .then_inc(logit_ready, 1)
                    dve.wait_ge(ex_ready, i + 1)
                    dve.tensor_reduce(total[:, :], ex[:, :, :], AX.X, ALU.add)
                    dve.drain()
                    dve.reciprocal(total[:, :], total[:, :])
                    dve.drain()
                    dve.tensor_tensor(alpha[:, :, :], ex[:, :, :],
                                      total[:, :].unsqueeze(2).broadcast_to([P, TB, E_ACT]), ALU.mult)
                    dve.drain()
                    for k in range(TB):
                        dve.tensor_tensor(u[:, k, :].rearrange("p (e r) -> p e r", e=E_ACT),
                                          smv[:, k, 0:RANK].rearrange("p (e r) -> p e r", e=E_ACT),
                                          alpha[:, k, :].unsqueeze(2).broadcast_to([P, E_ACT, R1]), ALU.mult)
                    dve.drain().then_inc(sm_free, 1)
                    dve.wait_ge(left_free, i + 1)
                    dve.tensor_copy(left[:, :, 0:RANK].bitcast(F32R), u[:, :, :])
                    dve.drain()
                    dve.tensor_copy(left[:, :, 2 * RANK:3 * RANK], left[:, :, 0:RANK])
                    dve.tensor_tensor(left[:, :, RANK:2 * RANK], u[:, :, :], left[:, :, 0:RANK], ALU.subtract)
                    dve.drain().then_inc(left_ready, TB)
                if not last:
                    norm.vector_norm(dve, i, 1)
                for k in range(TB):
                    dve.wait_ge(h_ready, i * TB + k + 1)
                    dve.scalar_tensor_tensor(out=x[:, TB * i + k, :], in0=h[k][:, :], scalar=0.5,
                                             in1=x[:, TB * i + k, :], op0=ALU.mult, op1=ALU.add)\
                       .then_inc(h_free, 1)

            with dve.Fori(0, B - 1) as i:
                batch(i, last=False)
            batch(B - 1, last=True)

        if kind == 1 and out is not None:
            @block.sync
            def _(sp):
                with sp.Fori(0, B) as i:
                    hold(sp, passed, h_free, (i + 2) * TB)
                    sp.dma_start(out[i, :, :].rearrange("(t p) c -> p t c", p=P),
                                 x[:, bass.ds(TB * i, TB), :]).then_inc(stored, 16)
                sp.wait_ge(stored, 16 * B)


def ffn0_route(nc, name, x, ident, stack, extra):
    with ExitStack() as ctx:
        st = Stage(nc, ctx, name)
        small = extra["small"]
        t = Ring2(st, "t", NT)
        h = Ring2(st, "h", NT)
        pre = st.ps("pre")
        pre2 = st.ps("pre2")
        anchor = st.sb("anchor", [P, NT, 2 * E0])
        peak = st.sb("peak", [P, 2])
        peak_all = st.sb("peak_all", [P, 2])
        probs = st.sb("probs", [P, NT, E0])
        gate = st.sb("gate", [P, NT, E0])
        top8 = st.sb("top8", [P, NT, 8])
        row = st.sb("row", [P, NT])
        wT = st.sb("wT", [P, P])
        u = st.sb("u", [P, NT, RANK])
        left = st.sb("left", [P, NT, STACK])
        leftT = st.sb("leftT", [P, TB, P], F32R)
        copied = st.sem("copied")
        peak_ready = st.sem("peak_ready")
        peak_all_ready = st.sem("peak_all_ready")
        arg_ready = st.sem("arg_ready")
        exp_ready = st.sem("exp_ready")
        w_ready = st.sem("w_ready")
        wT_ready = st.sem("wT_ready")
        mix_ready = st.sem("mix_ready")
        turned = st.sem("turned")
        left_ready = st.sem("left_ready")
        leftT_free = st.sem("leftT_free")
        block = ctx.enter_context(nc.Block())

        @block.gpsimd
        def _(pool):
            pool.wait_ge(peak_ready, 1)
            pool.partition_all_reduce(peak_all[:, :], peak[:, :], P, RMAX).then_inc(peak_all_ready, 1)

        @block.scalar
        def _(act):
            act.wait_ge(arg_ready, 1)
            act.activation(probs[:, :, :], probs[:, :, :], ACT.Exp).then_inc(exp_ready, 1)
            act.wait_ge(arg_ready, 2)
            act.activation(gate[:, :, :], gate[:, :, :], ACT.Exp, scale=-2.0).then_inc(exp_ready, 1)
            act.wait_ge(turned, 1)
            act.activation(wT[:, :], pre[:, 0:P], ACT.Copy).then_inc(wT_ready, 1)
            for n in range(NT):
                if n >= TB:
                    act.wait_ge(leftT_free, n - TB + 1)
                act.wait_ge(*t.at_ready(0, n))
                act.activation(leftT[:, n % TB, :], t.bank[n % 2][:, 0:P], ACT.Copy).then_inc(t.free[n % 2], 1)

        @block.tensor
        def _(pe):
            t.prime(pe)
            h.prime(pe)
            pe.wait_ge(w_ready, 1)
            pe.transpose(pre[:, 0:P], probs[:, :, :].rearrange("p n e -> p (n e)"), ident[:, :])\
              .then_inc(turned, 1)
            pe.wait_ge(wT_ready, 1)
            pe.matmul(pre2[:, :], wT[:, :], extra["limes_bd"][:, :, :].rearrange("p n r -> p (n r)"),
                      start=True, stop=True).then_inc(mix_ready, 1)
            pe.wait_ge(left_ready, 1)
            for n in range(NT + 1):
                if n < NT:
                    pe.wait_ge(*t.at_free(0, n))
                    pe.transpose(t.bank[n % 2][:, 0:P], left[:, n, :], ident[:, :]).then_inc(t.ready, 1)
                if n >= 1:
                    pe.wait_ge(*t.at_used(0, n - 1))
                    pe.wait_ge(*h.at_free(0, n - 1))
                    pe.matmul(h.bank[(n - 1) % 2][:, :], leftT[:, (n - 1) % TB, :], stack[:, :], start=True,
                              stop=True).then_inc(h.ready, 1)
                    pe.drain().then_inc(leftT_free, 1)

        @block.vector
        def _(dve):
            dve.memset(left[:, :, :], 0.0)
            dve.stream_shuffle(anchor[:, :, :], small[:, :, RANK:48], [q | (NGRAM - 1) for q in range(32)])
            dve.drain()
            dve.tensor_tensor(anchor[:, :, 0:E0], anchor[:, :, 0:E0],
                              extra["bias8"][:, :].unsqueeze(1).broadcast_to([P, NT, E0]), ALU.add)
            dve.drain()
            for c in range(2):
                dve.tensor_reduce(peak[:, c:c + 1], anchor[:, :, c * E0:(c + 1) * E0], AX.XY, ALU.max,
                                  apply_absolute_value=True)
            dve.drain().then_inc(peak_ready, 1)
            dve.wait_ge(peak_all_ready, 1)
            dve.tensor_scalar(peak[:, :], peak_all[:, :], 1e-6, None, ALU.max)
            dve.drain()
            dve.reciprocal(peak[:, :], peak[:, :])
            dve.drain()
            dve.tensor_scalar(peak[:, :], peak[:, :], 0.5, None, ALU.mult)
            dve.drain()
            dve.tensor_scalar(probs[:, :, :], anchor[:, :, 0:E0], peak[:, 0:1], None, ALU.mult)
            dve.drain()
            dve.scalar_tensor_tensor(out=probs[:, :, :], in0=anchor[:, :, E0:2 * E0], scalar=peak[:, 1:2],
                                     in1=probs[:, :, :], op0=ALU.mult, op1=ALU.add)
            dve.drain()
            dve.tensor_reduce(row[:, :], probs[:, :, :], AX.X, ALU.max)
            dve.drain()
            wide = row[:, :].unsqueeze(2).broadcast_to([P, NT, E0])
            dve.tensor_tensor(probs[:, :, :], probs[:, :, :], wide, ALU.subtract).then_inc(arg_ready, 1)
            dve.wait_ge(exp_ready, 1)
            dve.tensor_reduce(row[:, :], probs[:, :, :], AX.X, ALU.add)
            dve.drain()
            dve.reciprocal(row[:, :], row[:, :])
            dve.drain()
            dve.tensor_tensor(probs[:, :, :], probs[:, :, :], wide, ALU.mult)
            dve.drain()
            for n in range(NT):
                dve.max(top8[:, n, :], probs[:, n, :])
            dve.drain()
            dve.tensor_tensor(gate[:, :, :], probs[:, :, :], top8[:, :, 1:2].broadcast_to([P, NT, E0]),
                              ALU.subtract).then_inc(arg_ready, 1)
            dve.wait_ge(exp_ready, 2)
            dve.tensor_scalar(gate[:, :, :], gate[:, :, :], 1.0, None, ALU.add)
            dve.drain()
            dve.reciprocal(gate[:, :, :], gate[:, :, :])
            dve.drain()
            dve.tensor_tensor(probs[:, :, :], probs[:, :, :], gate[:, :, :], ALU.mult)
            dve.drain()
            dve.tensor_reduce(row[:, :], probs[:, :, :], AX.X, ALU.add)
            dve.drain()
            dve.tensor_scalar(row[:, :], row[:, :], 1e-9, None, ALU.add)
            dve.drain()
            dve.reciprocal(row[:, :], row[:, :])
            dve.drain()
            dve.tensor_tensor(probs[:, :, :], probs[:, :, :], wide, ALU.mult).then_inc(w_ready, 1)
            dve.wait_ge(mix_ready, 1)
            dve.tensor_tensor(u[:, :, :], small[:, :, 0:RANK],
                              pre2[:, :].rearrange("p (n r) -> p n r", n=NT), ALU.mult)
            dve.drain()
            dve.tensor_copy(left[:, :, 0:RANK].bitcast(F32R), u[:, :, :])
            dve.drain()
            dve.tensor_copy(left[:, :, 2 * RANK:3 * RANK], left[:, :, 0:RANK])
            dve.tensor_tensor(left[:, :, RANK:2 * RANK], u[:, :, :], left[:, :, 0:RANK], ALU.subtract)
            dve.drain().then_inc(left_ready, 1)
            for n in range(NT):
                dve.wait_ge(*h.at_ready(0, n))
                dve.scalar_tensor_tensor(out=x[:, n, :], in0=h.bank[n % 2][:, :], scalar=0.5, in1=x[:, n, :],
                                         op0=ALU.mult, op1=ALU.add).then_inc(h.free[n % 2], 1)


def attention(nc, name, kind, x, ln, ident, a):
    pre = f"L{kind}_attn_"
    names = ("Wq", "Wk", "Wv", "Wo") if kind == 0 else ("wq", "wk", "wv", "wo")
    wq, wk, wv, wo = (a[pre + n] for n in names)
    nkv = HKV0 if kind == 0 else H
    kvd = nkv * HD
    with ExitStack() as ctx:
        st = Stage(nc, ctx, name)
        wq_s = (st.sb("wq_hi", [P, KT, D], F32R), st.sb("wq_lo", [P, KT, D], F32R))
        wk_s = (st.sb("wk_hi", [P, KT, kvd], F32R), st.sb("wk_lo", [P, KT, kvd], F32R))
        wv_s = (st.sb("wv_hi", [P, KT, kvd], F32R), st.sb("wv_lo", [P, KT, kvd], F32R))
        wo_s = st.sb("wo", [P, KT, D])
        prepare_weights(nc, name + "w", ident, x, ln, [(wq, D, *wq_s), (wk, kvd, *wk_s), (wv, kvd, *wv_s),
                                                       (wo, D, wo_s, None)])
        attention_loop(nc, name + "l", kind, x, ln, ident, a, wq_s, wk_s, wv_s, wo_s)


def attention_loop(nc, name, kind, x, ln, ident, a, wq, wk, wv, wo):
    nkv = HKV0 if kind == 0 else H
    kvd = nkv * HD
    slots = GH if kind == 0 else 3
    t_prob = lambda n, k: (n // GH) * (GH * TB + 1) + (n % GH) * TB + k
    t_out = lambda g: g * (GH * TB + 1) + GH * TB
    t_last = lambda k: NG * (GH * TB + 1) + k
    T_NORM = NG * (GH * TB + 1) + TB
    T_STEPS = T_NORM + TB
    if kind == 0:
        m_q, m_k = (lambda m: 2 + m - 1), None
        M_FIRST = 2 + KT - 1
        firsts = (1, 0)
    else:
        m_q, m_k = (lambda m: TB + 2 * m - 2), (lambda m: TB + 2 * m - 1)
        M_FIRST = TB + 2 * KT - 2
        firsts = (0, 1)
    m_last = lambda k, last_one: M_FIRST + (0 if last_one else 2) + k
    M_STEPS = M_FIRST + 2 + TB
    on_act = (0, 1, 2, 3) if kind == 0 else (1, 2)
    per_group = 16 * 3 * (GH + (1 if kind == 0 else GH))

    with ExitStack() as ctx:
        st = Stage(nc, ctx, name)
        t = Ring2(st, "t", T_STEPS, TB)
        m = Ring2(st, "m", M_STEPS, 2)
        s = Ring2(st, "s", H * TB)
        o = Ring2(st, "o", NG)
        heads = st.sb("heads", [P, TB, D])
        probT = st.sb("probT", [P, GH, CAUSAL])
        norm = Norm(st, x, ln, ident, t, probT[:, :, :].rearrange("p h c -> p (h c)")[:, 0:TB * D]
                    .rearrange("p (t c) -> p t c", t=TB))
        cos, sin = st.sb("cos", [P, S]), st.sb("sin", [P, S])
        causal = st.sb("causal", [P, S])
        qk_hi = [st.sb(f"{n}_hi", [P, S], F32R) for n in "qk"]
        qk_lo = [st.sb(f"{n}_lo", [P, S], F32R) for n in "qk"]
        q_stack = st.sb("q_stack", [QK_ROWS, 2, GH, S], F32R)
        k_stack = st.sb("k_stack", [QK_ROWS, 2, GH, S], F32R)
        v_ones = st.sb("v_ones", [P, TB, nkv, VW])
        sc = st.sb("sc", [P, slots, CAUSAL])
        top = st.sb("top", [P, slots, TB])
        shift = st.sb("shift", [P, slots, TB])
        osb = st.sb("osb", [P, S])
        recip = st.sb("recip", [P, TB, GH])
        oT = sc[:, :, :].rearrange("p l c -> p (l c)")[:, 0:KT * S].rearrange("p (k c) -> p k c", k=KT)
        tables_loaded = st.sem("tables_loaded")
        loaded = [st.sem("stack_loaded0"), st.sem("stack_loaded1")]
        stack_free = st.sem("stack_free")
        sp_passed, dve_passed = st.sem("sp_passed"), st.sem("dve_passed")
        roped_ready = [st.sem("q_ready"), st.sem("k_ready")]
        shift_ready = st.sem("shift_ready")
        exp_ready = st.sem("exp_ready")
        if kind == 0:
            vT_ready = st.sem("vT_ready")
            ex = st.sb("ex", [P, EX, CAUSAL])
            sel_ready = st.sem("sel_ready")
            NQ = TB - 1
            low, high, mid, cnt, n_low, n_high, is_up, is_down, outside, step_a, step_b, step_c, slope = (
                st.sb(n, [P, GH, NQ]) for n in ("low", "high", "mid", "cnt", "n_low", "n_high", "is_up", "is_down",
                                                "outside", "step_a", "step_b", "step_c", "slope"))
            signs = st.sb("signs", [P, 2, NQ])
            sel_tab = st.sb("sel_tab", [P, NQ, 5])
            sign_tab = st.sb("sign_tab", [P, NQ, 3])
            ranks = st.sb("ranks", [P, 8])
            bn = st.sb("bn", [P, GH, NQ, 6])
            mean_var = st.sb("mean_var", [P, GH, NQ, 2])
            next8 = st.sb("next8", [P, GH * NQ, 8])
            hot8 = st.sb("hot8", [P, GH * NQ, 8])
            after8 = st.sb("after8", [P, GH * NQ, 8])
            flag = st.sb("flag", [P, 32])
            flagT = st.sb("flagT", [P, 32])
            flags = st.sb("flags", [P, P])
            flag_int = st.sb("flag_int", [P, 1], I32)
            above = st.sb("above", [P, GH, CAUSAL], mybir.dt.int8)
            thr = st.sb("thr", [P, GH, TB])
            mid_ready = st.sem("mid_ready")
            signs_ready = st.sem("signs_ready")
        probs, prob_slots, prob_ready = (ex, EX, sel_ready) if kind == 0 else (sc, slots, exp_ready)
        block = ctx.enter_context(nc.Block())

        @block.sync
        def _(sp):
            sp.dma_start(cos[:, :], a["c_cos"]).then_inc(tables_loaded, 16)
            sp.dma_start(sin[:, :], a["c_sin"]).then_inc(tables_loaded, 16)
            sp.dma_start(causal[:, :], a["c_causal"]).then_inc(tables_loaded, 16)
            if kind == 0:
                sp.dma_start(sel_tab[:, :, :], a["c_select"]).then_inc(tables_loaded, 16)

            def restack(which, j, dst, sem):
                hi, lo = qk_hi[which], qk_lo[which]
                for r, src in enumerate((hi, lo, hi) if which == 0 else (hi, hi, lo)):
                    sp.dma_start(dst[HD * r:HD * (r + 1), :].bitcast(F32),
                                 src[HD * j:HD * (j + 1), :].bitcast(F32)).then_inc(sem, 16)

            with sp.Fori(0, B) as i:
                if kind == 0:
                    hold(sp, sp_passed, roped_ready[1], i + 1)
                for c in range(KT):
                    hold(sp, sp_passed, roped_ready[0], i * KT + c + 1)
                    if kind == 1:
                        hold(sp, sp_passed, roped_ready[1], i * KT + c + 1)
                    for g in (2 * c, 2 * c + 1):
                        hold(sp, sp_passed, stack_free, i * NG + g + 1)
                        if kind == 0:
                            restack(1, g, k_stack[:, g // GH, g % GH, :], loaded[g % 2])
                        for j in range(GH):
                            restack(0, (g % 2) * GH + j, q_stack[:, g % 2, j, :], loaded[g % 2])
                            if kind == 1:
                                restack(1, (g % 2) * GH + j, k_stack[:, g % 2, j, :], loaded[g % 2])

        @block.tensor
        def _(pe):
            t.prime(pe)
            m.prime(pe)
            s.prime(pe)

            def project(i, step, c, which):
                w = (wq, wk, wv)[which]
                pe.wait_ge(*m.at_free(i, step))
                prod3(pe, m.bank[step % 2][:, :],
                      lambda k: (w[0][:, k, c * P:(c + 1) * P], w[1][:, k, c * P:(c + 1) * P]), norm.batch(), range(KT)).then_inc(m.ready, 1)

            def scores(i, n, tiles=range(TB)):
                g, h = n // GH, n % GH
                if h == 0 and 0 in tiles:
                    pe.wait_ge(loaded[g % 2], (i * (NG // 2) + g // 2 + 2) * per_group)
                for q in tiles:
                    step = n * TB + q
                    pe.wait_ge(*s.at_free(i, step))
                    kk = k_stack[:, g // GH, g % GH, :] if kind == 0 else k_stack[:, g % 2, h, :]
                    pe.matmul(s.bank[step % 2][:, 0:(q + 1) * P], q_stack[:, g % 2, h, q * P:(q + 1) * P],
                              kk[:, 0:(q + 1) * P], start=True, stop=True).then_inc(s.ready, 1)
                if h == GH - 1 and TB - 1 in tiles:
                    pe.drain().then_inc(stack_free, 1)

            def turn_probs(i, n):
                pe.wait_ge(prob_ready, i * H + n + 1)
                for k in range(TB):
                    step = t_prob(n, k)
                    pe.wait_ge(*t.at_free(i, step))
                    for q in range(k, TB):
                        last = pe.transpose(t.bank[step % 2][:, (q - k) * P:(q - k + 1) * P],
                                            probs[:, n % prob_slots, ROW_AT[q] + k * P:ROW_AT[q] + (k + 1) * P],
                                            ident[:, :])
                    last.then_inc(t.ready, 1)

            def weigh(i, g):
                for k in (TB - 2, TB - 1):
                    pe.wait_ge(*t.at_used(i, t_prob(GH * g + GH - 1, k)))
                pe.wait_ge(*o.at_free(i, g))
                for k in range(TB):
                    for h in range(GH):
                        kv = g if kind == 0 else GH * g + h
                        last = pe.matmul(o.bank[g % 2][32 * h:32 * h + VW, k * P:S], v_ones[:, k, kv, :],
                                         probT[:, h, COL_AT[k]:COL_AT[k] + (TB - k) * P],
                                         start=k == 0, stop=k == TB - 1, skip_group_check=True)
                last.then_inc(o.ready, 1)

            def turn_out(i, g):
                pe.wait_ge(*o.at_used(i, g))
                pe.wait_ge(*t.at_free(i, t_out(g)))
                for q in range(TB):
                    last = pe.transpose(t.bank[t_out(g) % 2][:, q * P:(q + 1) * P], osb[:, q * P:(q + 1) * P],
                                        ident[:, :])
                last.then_inc(t.ready, 1)

            def start(i, ahead, t_step, m_step):
                norm.tensor_transpose(pe, i, ahead, t_step)
                for k in range(TB - 2, TB):
                    pe.wait_ge(*t.at_used(i, t_step + k))
                for k in range(2):
                    project(i, m_step + k, 0, firsts[k])

            def batch(i, last_one):
                if kind == 0:
                    project(i, 0, 0, 2)
                    pe.wait_ge(vT_ready, i + 1)
                    pe.wait_ge(*m.at_free(i, 1))
                    for k in range(TB):
                        last = pe.transpose(m.bank[1][:, k * P:(k + 1) * P], osb[:, k * P:(k + 1) * P], ident[:, :])
                    last.then_inc(m.ready, 1)
                else:
                    for k in range(TB):
                        pe.wait_ge(*m.at_free(i, k))
                        prod3(pe, m.bank[k % 2][:, :], norm.tile(k), lambda c: (wv[0][:, c, :], wv[1][:, c, :]),
                              range(KT)).then_inc(m.ready, 1)
                if kind == 0:
                    for g in range(NG):
                        for h in range(g > 0, GH):
                            scores(i, GH * g + h)
                        if g >= 1:
                            weigh(i, g - 1)
                            turn_out(i, g - 1)
                        if g % 2 == 0 and g // 2 + 1 < KT:
                            project(i, m_q(g // 2 + 1), g // 2 + 1, 0)
                            if g // 2 + 2 == KT:
                                pe.drain().then_inc(norm.free, 1)
                        if g + 1 < NG:
                            scores(i, GH * (g + 1), range(2))
                        for h in range(GH):
                            if h == GH - 1 and g + 1 < NG:
                                scores(i, GH * (g + 1), range(2, TB))
                            turn_probs(i, GH * g + h)
                    weigh(i, NG - 1)
                    turn_out(i, NG - 1)
                else:
                    for n in range(H + slots):
                        done = n - slots
                        if done >= 0:
                            turn_probs(i, done)
                            if done % GH == GH - 1:
                                weigh(i, done // GH)
                        if n < H:
                            scores(i, n)
                        if done >= 0 and done % GH == GH - 1:
                            turn_out(i, done // GH)
                        if n % 8 == 4 and n < H and n // 8 + 1 < KT:
                            project(i, m_q(n // 8 + 1), n // 8 + 1, 0)
                            project(i, m_k(n // 8 + 1), n // 8 + 1, 1)
                            if n // 8 + 2 == KT:
                                pe.drain().then_inc(norm.free, 1)
                pe.drain().then_inc(norm.xn_free, 1)
                pe.wait_ge(*t.at_used(i, t_out(NG - 1)))
                for k in range(TB):
                    pe.wait_ge(*t.at_free(i, t_last(k)))
                    for c in range(KT):
                        last = pe.transpose(t.bank[t_last(k) % 2][:, c * P:(c + 1) * P],
                                            heads[:, k, c * P:(c + 1) * P], ident[:, :])
                    last.then_inc(t.ready, 1)
                if not last_one:
                    start(i, 1, T_NORM, M_FIRST)
                for k in range(TB):
                    pe.wait_ge(*t.at_used(i, t_last(k)))
                    pe.wait_ge(*m.at_free(i, m_last(k, last_one)))
                    for c in range(KT):
                        last = pe.matmul(m.bank[m_last(k, last_one) % 2][:, :], oT[:, c, k * P:(k + 1) * P], wo[:, c, :],
                                         start=c == 0, stop=c == KT - 1)
                    last.then_inc(m.ready, 1)

            start(0, 0, -TB, -2)
            with pe.Fori(0, B - 1) as i:
                batch(i, False)
            batch(B - 1, True)

        def move_probs(eng, copy, i, n, tiles):
            g = n // GH
            for k in tiles:
                step = t_prob(n, k)
                if n % GH == 0 and g >= 1:
                    eng.wait_ge(*o.at_ready(i, g - 1))
                eng.wait_ge(*t.at_ready(i, step))
                copy(probT[:, n % GH, COL_AT[k]:COL_AT[k] + (TB - k) * P],
                     t.bank[step % 2][:, 0:(TB - k) * P]).then_inc(t.free[step % 2], 1)

        @block.scalar
        def _(act):
            norm.prime(act)
            copy = lambda out, in_: act.activation(out, in_, ACT.Copy)

            def exps(i, n):
                act.wait_ge(shift_ready, i * H + n + 1)
                if kind == 0 and n >= EX:
                    act.wait_ge(*t.at_ready(i, t_prob(n - EX, TB - 1)))
                for q in range(TB):
                    src = sc[:, n % slots, ROW_AT[q]:ROW_AT[q] + (q + 1) * P]
                    dst = src if kind == 1 else ex[:, n % EX, ROW_AT[q]:ROW_AT[q] + (q + 1) * P]
                    last = act.activation(dst, src, ACT.Exp, bias=shift[:, n % slots, q:q + 1], scale=HD ** -0.5)
                last.then_inc(exp_ready, 1)

            def move_out(i, g):
                act.wait_ge(*o.at_ready(i, g))
                if g >= 1:
                    act.wait_ge(*t.at_ready(i, t_out(g - 1)))
                copy(osb[:, :], o.bank[g % 2][:, :]).then_inc(o.free[g % 2], 1)

            def count_signs(i, g):
                for r in range(SHARED):
                    act.wait_ge(mid_ready, (i * NG + g) * SHARED + r + 1)
                    for h in range(2):
                        for q in range(1, TB):
                            part = slice(ROW_AT[q], ROW_AT[q] + (q + 1) * P)
                            last = act.activation(above[:, 2 + h, part], sc[:, 2 + h, part], ACT.Sign, scale=-1.0,
                                                  bias=mid[:, 2 + h, q - 1:q], accum_out=signs[:, h, q - 1:q])
                    last.then_inc(signs_ready, 1)

            def batch(i, last_one):
                if kind == 0:
                    act.wait_ge(*m.at_ready(i, 0))
                    copy(osb[:, :], m.bank[0][:, :])
                    act.drain().then_inc(vT_ready, 1)
                    act.sem_inc(m.free[0], 1)
                    act.wait_ge(*m.at_ready(i, 1))
                    copy(v_ones[:, :, :, 0:HD], m.bank[1][:, :].rearrange("p (k h d) -> p k h d", k=TB, d=HD))\
                        .then_inc(m.free[1], 1)
                else:
                    for k in range(TB):
                        act.wait_ge(*m.at_ready(i, k))
                        copy(v_ones[:, k, :, 0:HD], m.bank[k % 2][:, :].rearrange("p (h d) -> p h d", d=HD))\
                            .then_inc(m.free[k % 2], 1)
                if kind == 0:
                    for g in range(NG):
                        count_signs(i, g)
                        for h in range(EX):
                            exps(i, GH * g + h)
                        for h in range(GH):
                            move_probs(act, copy, i, GH * g + h, on_act)
                            if h + EX < GH:
                                exps(i, GH * g + h + EX)
                        move_out(i, g)
                else:
                    for n in range(H + slots):
                        done = n - slots
                        if done >= 0:
                            move_probs(act, copy, i, done, on_act)
                            if done % GH == GH - 1:
                                move_out(i, done // GH)
                        if n < H:
                            exps(i, n)
                for k in range(TB):
                    act.wait_ge(*t.at_ready(i, t_last(k)))
                    copy(oT[:, :, k * P:(k + 1) * P],
                         t.bank[t_last(k) % 2][:, :].rearrange("p (k c) -> p k c", k=KT))\
                        .then_inc(t.free[t_last(k) % 2], 1)
                if not last_one:
                    norm.scalar_split(act, i, 1, T_NORM)

            norm.scalar_split(act, 0, 0, -TB)
            with act.Fori(0, B - 1) as i:
                batch(i, False)
            batch(B - 1, True)

        @block.vector
        def _(dve):
            dve.memset(q_stack[:, :, :, :].bitcast(F32), 0.0)
            dve.memset(k_stack[:, :, :, :].bitcast(F32), 0.0)
            dve.memset(v_ones[:, :, :, HD:VW], 1.0)
            if kind == 0:
                dve.memset(thr[:, :, :], NEG / 2)
                dve.memset(flag[:, :], 0.0)
                for r in range(8):
                    dve.memset(ranks[:, r:r + 1], float(r))
                for q in range(NQ):
                    w = (q + 2) * P
                    dve.memset(sign_tab[:, q, 0:1], w - 2 * (KEEP + 0.25))
                    dve.memset(sign_tab[:, q, 1:2], w - 2 * (KEEP - 7.25))
                    dve.memset(sign_tab[:, q, 2:3], w / 2)
            for b in range(2):
                dve.memset(o.bank[b][:, :], 0.0)
            dve.drain().then_inc(stack_free, 2)
            o.prime(dve)
            for b in range(2):
                dve.sem_inc(loaded[b], per_group)
            dve.wait_ge(tables_loaded, 48 + 16 * (kind == 0))

            def rope(i, ahead, step, c, which):
                bank = m.bank[step % 2]
                hi, lo = qk_hi[which], qk_lo[which]
                straight, turned = lo[:, :].bitcast(F32), hi[:, :].bitcast(F32)
                for b in range(2):
                    hold(dve, dve_passed, loaded[b], ((i + ahead) * KT + c + 1) * per_group)
                dve.drain()
                hold(dve, dve_passed, *m.at_ready(i, step))
                dve.tensor_tensor(straight, bank[:, :], cos[:, :], ALU.mult)
                dve.stream_shuffle(turned, bank[:, :], [p ^ (HD // 2) for p in range(32)])\
                   .then_inc(m.free[step % 2], 1)
                dve.drain()
                dve.tensor_tensor(turned, turned, sin[:, :], ALU.mult)
                dve.drain()
                dve.tensor_tensor(straight, straight, turned, ALU.add)
                dve.drain()
                dve.tensor_copy(hi[:, :], straight)
                dve.drain()
                dve.tensor_tensor(lo[:, :], straight, turned, ALU.subtract).then_inc(roped_ready[which], 1)

            def row_max(i, n):
                if kind == 1 and n >= slots:
                    hold(dve, dve_passed, *t.at_ready(i, t_prob(n - slots, TB - 1)))
                for q in range(TB):
                    step, w = n * TB + q, (q + 1) * P
                    hold(dve, dve_passed, *s.at_ready(i, step))
                    dve.tensor_tensor_reduce(sc[:, n % slots, ROW_AT[q]:ROW_AT[q] + w], s.bank[step % 2][:, 0:w],
                                             causal[:, S - w:S], 1.0, 3 * NEG, ALU.add, ALU.max,
                                             top[:, n % slots, q:q + 1]).then_inc(s.free[step % 2], 1)
                dve.drain()
                dve.tensor_scalar(shift[:, n % slots, :], top[:, n % slots, :], -HD ** -0.5, None, ALU.mult)\
                   .then_inc(shift_ready, 1)

            def count(heads):
                for h in heads:
                    for q in range(1, TB):
                        part = slice(ROW_AT[q], ROW_AT[q] + (q + 1) * P)
                        dve.tensor_scalar(above[:, h, part], sc[:, h, part], mid[:, h, q - 1:q], 0.0,
                                          ALU.is_ge, ALU.add, accum_out=cnt[:, h, q - 1:q])

            def narrow(first=False, signed=False, again=False):
                by_count = slice(0, 2 if signed else GH)
                dve.tensor_scalar(is_up[:, by_count, :], cnt[:, by_count, :], KEEP + 0.25, None, ALU.is_gt)
                dve.tensor_scalar(is_down[:, by_count, :], cnt[:, by_count, :], KEEP - 7.25, None, ALU.is_lt)
                if signed:
                    tab = lambda c: sign_tab[:, :, c].unsqueeze(1).broadcast_to([P, 2, NQ])
                    dve.tensor_tensor(is_up[:, 2:GH, :], signs[:, :, :], tab(0), ALU.is_lt)
                    dve.tensor_tensor(is_down[:, 2:GH, :], signs[:, :, :], tab(1), ALU.is_gt)
                    dve.scalar_tensor_tensor(out=cnt[:, 2:GH, :], in0=signs[:, :, :], scalar=-0.5, in1=tab(2),
                                             op0=ALU.mult, op1=ALU.add)
                dve.drain()
                up, down = is_up[:, :, :].bitcast(I32), is_down[:, :, :].bitcast(I32)
                dve.copy_predicated(low[:, :, :], up, mid[:, :, :])
                dve.copy_predicated(high[:, :, :], down, mid[:, :, :])
                dve.copy_predicated(n_low[:, :, :], up, cnt[:, :, :])
                dve.copy_predicated(n_high[:, :, :], down, cnt[:, :, :])
                dve.tensor_tensor(outside[:, :, :], is_up[:, :, :], is_down[:, :, :], ALU.max)
                if first:
                    dve.scalar_tensor_tensor(out=step_a[:, :, :], in0=cnt[:, :, :], scalar=AIM, in1=slope[:, :, :],
                                             op0=ALU.subtract, op1=ALU.mult)
                    dve.drain()
                    dve.tensor_tensor(step_a[:, :, :], step_a[:, :, :], mid[:, :, :], ALU.add)
                else:
                    dve.drain()
                    dve.tensor_tensor(step_b[:, :, :], n_low[:, :, :], n_high[:, :, :], ALU.subtract)
                    dve.tensor_tensor(step_a[:, :, :], high[:, :, :], low[:, :, :], ALU.subtract)
                    dve.drain()
                    dve.reciprocal(step_b[:, :, :], step_b[:, :, :])
                    dve.scalar_tensor_tensor(out=step_a[:, :, :], in0=n_low[:, :, :], scalar=AIM,
                                             in1=step_a[:, :, :], op0=ALU.subtract, op1=ALU.mult)
                    dve.drain()
                    dve.tensor_tensor(step_a[:, :, :], step_a[:, :, :], step_b[:, :, :], ALU.mult)
                    dve.drain()
                    dve.tensor_tensor(step_a[:, :, :], step_a[:, :, :], low[:, :, :], ALU.add)
                dve.drain()
                last = dve.copy_predicated(mid[:, :, :], outside[:, :, :].bitcast(I32), step_a[:, :, :])
                if again:
                    last.then_inc(mid_ready, 1)
                dve.drain()

            def start_search():
                dve.drain()
                for h in range(GH):
                    for q in range(1, TB):
                        dve.bn_stats(bn[:, h, q - 1, :], sc[:, h, ROW_AT[q]:ROW_AT[q] + q * P])
                dve.drain()
                for h in range(GH):
                    for q in range(NQ):
                        dve.bn_aggr(mean_var[:, h, q, :], bn[:, h, q, :])
                dve.tensor_copy(high[:, :, :], top[:, :, 1:TB])
                dve.memset(n_high[:, :, :], 1.0)
                tab = lambda c: sel_tab[:, :, c].unsqueeze(1).broadcast_to([P, GH, NQ])
                dve.tensor_copy(n_low[:, :, :], tab(0))
                dve.drain()
                mean = mean_var[:, :, :, 0]
                sd = step_a
                dve.tensor_scalar(sd[:, :, :].bitcast(I32), mean_var[:, :, :, :].bitcast(I32)[:, :, :, 1], 1, None,
                                  ALU.arith_shift_right)
                dve.scalar_tensor_tensor(out=step_c[:, :, :], in0=mean, scalar=-1.0, in1=mean,
                                         op0=ALU.mult, op1=ALU.max)
                dve.drain()
                dve.tensor_scalar(step_c[:, :, :], step_c[:, :, :], 1e-5, None, ALU.mult)
                dve.tensor_scalar(sd[:, :, :].bitcast(I32), sd[:, :, :].bitcast(I32), float(0x1fbd1df5), None, ALU.add)
                dve.drain()
                dve.tensor_tensor(slope[:, :, :], sd[:, :, :], tab(3), ALU.mult)
                dve.tensor_tensor(mid[:, :, :], sd[:, :, :], tab(1), ALU.mult)
                dve.tensor_tensor(low[:, :, :], sd[:, :, :], tab(2), ALU.mult)
                dve.drain()
                dve.tensor_tensor(mid[:, :, :], mid[:, :, :], mean, ALU.add)
                dve.tensor_tensor(low[:, :, :], low[:, :, :], step_c[:, :, :], ALU.add)
                dve.drain()
                dve.tensor_tensor(low[:, :, :], mean, low[:, :, :], ALU.subtract)
                dve.tensor_tensor(mid[:, :, :], mid[:, :, :], high[:, :, :], ALU.min).then_inc(mid_ready, 1)
                dve.drain()

            def still_open():
                return dve.value_load(flag_int[0:1, 0:1], min_val=0, max_val=2)

            def threshold():
                for h in range(GH):
                    for q in range(1, TB):
                        part = slice(ROW_AT[q], ROW_AT[q] + (q + 1) * P)
                        dve.scalar_tensor_tensor(out=probT[:, h, part], in0=above[:, h, part], scalar=2 * NEG,
                                                 in1=sc[:, h, part], op0=ALU.mult, op1=ALU.add)
                cnt_wide = cnt[:, :, :].rearrange("p h q -> p (h q)").unsqueeze(2).broadcast_to([P, GH * NQ, 8])
                ranks_wide = ranks[:, :].unsqueeze(1).broadcast_to([P, GH * NQ, 8])
                dve.tensor_tensor(hot8[:, :, :], cnt_wide, ranks_wide, ALU.add)
                dve.tensor_scalar(step_b[:, :, :], cnt[:, :, :], KEEP + 0.25, None, ALU.is_gt)
                dve.tensor_scalar(is_down[:, :, :], cnt[:, :, :], KEEP - 7.25, None, ALU.is_lt)
                dve.tensor_scalar(is_up[:, :, :], cnt[:, :, :], float(KEEP), None, ALU.is_equal)
                dve.drain()
                dve.tensor_tensor(outside[:, :, :], step_b[:, :, :], is_down[:, :, :], ALU.max)
                for h in range(GH):
                    for q in range(1, TB):
                        part = slice(ROW_AT[q], ROW_AT[q] + (q + 1) * P)
                        dve.max(next8[:, h * NQ + q - 1, :], probT[:, h, part])
                dve.tensor_scalar(after8[:, :, :], hot8[:, :, :], float(KEEP), None, ALU.is_equal)
                dve.tensor_scalar(hot8[:, :, :], hot8[:, :, :], KEEP - 1.0, None, ALU.is_equal)
                dve.drain()
                dve.tensor_tensor(hot8[:, :, :], hot8[:, :, :], next8[:, :, :], ALU.mult)
                dve.tensor_tensor(after8[:, :, :], after8[:, :, :], next8[:, :, :], ALU.mult)
                dve.drain()
                per_row = lambda b: b[:, :, :].rearrange("p (h q) r -> p h q r", h=GH)
                dve.tensor_reduce(thr[:, :, 1:TB], per_row(hot8), AX.X, ALU.add)
                dve.tensor_reduce(step_a[:, :, :], per_row(after8), AX.X, ALU.add)
                dve.drain()
                dve.copy_predicated(thr[:, :, 1:TB], is_up[:, :, :].bitcast(I32), mid[:, :, :])
                dve.drain()
                dve.tensor_tensor(step_a[:, :, :], step_a[:, :, :], thr[:, :, 1:TB], ALU.is_equal)
                dve.drain()
                dve.scalar_tensor_tensor(out=is_up[:, :, :], in0=outside[:, :, :], scalar=2.0, in1=step_a[:, :, :],
                                         op0=ALU.mult, op1=ALU.max)
                dve.drain()
                dve.tensor_reduce(flag[:, 0:1], is_up[:, :, :], AX.XY, ALU.max)
                dve.drain()
                dve.transpose(flagT[:, :], flag[:, :])
                dve.drain()
                for c in range(P // 32):
                    dve.tensor_copy(flags[0:1, 32 * c:32 * (c + 1)], flagT[32 * c:32 * c + 1, :])
                dve.drain()
                dve.tensor_reduce(flag_int[0:1, :], flags[0:1, :], AX.X, ALU.max)
                dve.drain()
                return still_open()

            def enclose_thr():
                now = thr[:, :, 1:TB]
                dve.scalar_tensor_tensor(out=step_a[:, :, :], in0=now, scalar=-1.0, in1=now,
                                         op0=ALU.mult, op1=ALU.max)
                dve.tensor_copy(low[:, :, :], now)
                dve.drain()
                dve.tensor_scalar(step_a[:, :, :], step_a[:, :, :], 0.512 * 2.0 ** -23, 1e-30, ALU.mult, ALU.add)
                dve.drain()
                dve.tensor_tensor(high[:, :, :], step_a[:, :, :], now, ALU.add)
                dve.drain()
                dve.tensor_copy(mid[:, :, :], high[:, :, :])
                dve.drain()
                count(range(GH))
                dve.drain()
                dve.tensor_scalar(step_a[:, :, :], cnt[:, :, :], -1.0, float(KEEP), ALU.mult, ALU.add)
                dve.drain()

            def search_slowly():
                most = top[:, :, 1:TB]
                dve.scalar_tensor_tensor(out=step_a[:, :, :], in0=most, scalar=-1.0, in1=most,
                                         op0=ALU.mult, op1=ALU.max)
                dve.memset(n_high[:, :, :], 0.0)
                dve.drain()
                dve.tensor_scalar(step_a[:, :, :], step_a[:, :, :], 1e-6, 1e-30, ALU.mult, ALU.add)
                dve.drain()
                dve.tensor_tensor(high[:, :, :], step_a[:, :, :], most, ALU.add)
                dve.drain()
                with dve.Fori(0, BISECT):
                    dve.tensor_tensor(mid[:, :, :], low[:, :, :], high[:, :, :], ALU.add)
                    dve.drain()
                    dve.tensor_scalar(mid[:, :, :], mid[:, :, :], 0.5, None, ALU.mult)
                    dve.drain()
                    count(range(GH))
                    dve.drain()
                    dve.tensor_scalar(is_up[:, :, :], cnt[:, :, :], KEEP - 0.5, None, ALU.is_gt)
                    dve.tensor_scalar(is_down[:, :, :], cnt[:, :, :], KEEP - 0.5, None, ALU.is_lt)
                    dve.drain()
                    dve.copy_predicated(low[:, :, :], is_up[:, :, :].bitcast(I32), mid[:, :, :])
                    dve.copy_predicated(high[:, :, :], is_down[:, :, :].bitcast(I32), mid[:, :, :])
                    dve.copy_predicated(n_high[:, :, :], is_down[:, :, :].bitcast(I32), cnt[:, :, :])
                    dve.drain()
                dve.tensor_copy(thr[:, :, 1:TB], low[:, :, :])
                dve.tensor_scalar(step_a[:, :, :], n_high[:, :, :], -1.0, float(KEEP), ALU.mult, ALU.add)
                dve.drain()

            def drop_ties(h):
                for q in range(1, TB):
                    w = (q + 1) * P
                    scores = sc[:, h, ROW_AT[q]:ROW_AT[q] + w]
                    beyond, tied = probT[:, h, 0:w], probT[:, h, S:S + w]
                    dve.tensor_scalar(beyond, scores, high[:, h, q - 1:q], None, ALU.is_ge)
                    dve.drain()
                    dve.scalar_tensor_tensor(out=tied, in0=scores, scalar=low[:, h, q - 1:q], in1=beyond,
                                             op0=ALU.is_ge, op1=ALU.subtract)
                    dve.drain()
                    dve.tensor_tensor_scan(beyond, tied, tied, 0.0, ALU.add, ALU.max)
                    dve.drain()
                    dve.scalar_tensor_tensor(out=tied, in0=beyond, scalar=step_a[:, h, q - 1:q], in1=tied,
                                             op0=ALU.is_gt, op1=ALU.mult)
                    dve.drain()
                    dve.scalar_tensor_tensor(out=scores, in0=tied, scalar=2 * NEG, in1=scores,
                                             op0=ALU.mult, op1=ALU.add)
                    dve.drain()

            def keep(g, h):
                slot = (g * GH + h) % EX
                for q in range(TB):
                    part = slice(ROW_AT[q], ROW_AT[q] + (q + 1) * P)
                    last = dve.scalar_tensor_tensor(out=ex[:, slot, part], in0=sc[:, h, part],
                                                    scalar=thr[:, h, q:q + 1], in1=ex[:, slot, part],
                                                    op0=ALU.is_ge, op1=ALU.mult)
                last.then_inc(sel_ready, 1)

            def select(i, g):
                start_search()
                for r in range(SHARED):
                    count(range(2))
                    if r == 0 and g >= 1:
                        out_rows(i, g - 1)
                    if r == 1 and g % 2 == 0 and g // 2 + 1 < KT:
                        rope(i, 0, m_q(g // 2 + 1), g // 2 + 1, 0)
                    dve.drain()
                    dve.wait_ge(signs_ready, (i * NG + g) * SHARED + r + 1)
                    narrow(first=r == 0, signed=True, again=r < SHARED - 1)
                count(range(GH))
                dve.drain()
                if g >= 1:
                    dve.wait_ge(*o.at_ready(i, g - 1))
                with dve.If(threshold()):
                    with dve.If(still_open() == 2):
                        for _ in range(2):
                            narrow()
                            count(range(GH))
                            dve.drain()
                        threshold()
                    with dve.If(still_open() == 2):
                        search_slowly()
                    with dve.If(still_open() == 1):
                        enclose_thr()
                    for h in range(GH):
                        hold(dve, dve_passed, exp_ready, i * H + g * GH + h + 1)
                        with dve.If(still_open()):
                            drop_ties(h)
                        keep(g, h)
                with dve.Else():
                    for h in range(GH):
                        dve.wait_ge(exp_ready, i * H + g * GH + h + 1)
                        keep(g, h)
                dve.drain()

            def out_rows(i, g):
                step = t_out(g)
                dve.wait_ge(*t.at_ready(i, step))
                v = t.bank[step % 2][:, :].rearrange("p (q h c) -> p q h c", q=TB, h=GH)
                dve.reciprocal(recip[:, :, :], v[:, :, :, HD])
                dve.drain()
                dve.tensor_tensor(heads[:, :, g * GH * HD:(g + 1) * GH * HD].rearrange("p q (h d) -> p q h d", h=GH),
                                  v[:, :, :, 0:HD], recip[:, :, :].unsqueeze(3).broadcast_to([P, TB, GH, HD]),
                                  ALU.mult).then_inc(t.free[step % 2], 1)

            def start(i, ahead, m_step):
                norm.vector_norm(dve, i, ahead)
                norm.vector_split(dve, i, ahead)
                for k in range(2):
                    rope(i, ahead, m_step + k, 0, firsts[k])

            def batch(i, last_one):
                if kind == 0:
                    for g in range(NG):
                        for h in range(GH):
                            row_max(i, GH * g + h)
                        select(i, g)
                    out_rows(i, NG - 1)
                else:
                    for n in range(H + slots):
                        done = n - slots
                        if done >= 0:
                            move_probs(dve, dve.tensor_copy, i, done, [k for k in range(TB) if k not in on_act])
                        if n < H:
                            row_max(i, n)
                        if done >= 0 and done % GH == GH - 1:
                            out_rows(i, done // GH)
                        if n % 8 == 4 and n < H and n // 8 + 1 < KT:
                            rope(i, 0, m_q(n // 8 + 1), n // 8 + 1, 0)
                            rope(i, 0, m_k(n // 8 + 1), n // 8 + 1, 1)
                if not last_one:
                    start(i, 1, M_FIRST)
                for k in range(TB):
                    dve.wait_ge(*m.at_ready(i, m_last(k, last_one)))
                    dve.tensor_tensor(x[:, TB * i + k, :], m.bank[m_last(k, last_one) % 2][:, :], x[:, TB * i + k, :], ALU.add)\
                       .then_inc(m.free[m_last(k, last_one) % 2], 1)

            start(0, 0, -2)
            with dve.Fori(0, B - 1) as i:
                batch(i, False)
            batch(B - 1, True)


def build(nc, a, out):
    with ExitStack() as ctx:
        sb = lambda name, shape, dt=F32: ctx.enter_context(nc.sbuf_tensor(name, shape, dt))
        x = sb("x", [P, NT, D])
        ident = sb("ident", [P, P])
        ln = sb("mean_var", [P, NT, 2]), sb("inv_dev", [P, NT])
        consts = sb("consts", [P, 2, 16])
        with ExitStack() as c0:
            loaded = nc.alloc_semaphore("start_loaded")
            block = c0.enter_context(nc.Block())

            @block.sync
            def _(sp):
                for b in range(B):
                    sp.dma_start(x[:, TB * b:TB * (b + 1), :],
                                 a["L0_attn_hidden_states"][b].rearrange("(t p) c -> p t c", p=P)).then_inc(loaded, 16)
                sp.dma_start(ident[:, :], a["c_ident"]).then_inc(loaded, 16)
                sp.dma_start(consts[:, :, :], a["c_rows"]).then_inc(loaded, 16)
                sp.wait_ge(loaded, 16 * (B + 2))
        f0 = {k: a["L0_ffn_" + k] for k in ("b", "A", "Bmat", "LiMEs")} | {"W": a["L0_ffn_W"]}
        f1 = {k: a["L1_ffn_" + k] for k in ("lora_A", "lora_B", "router_W", "router_b", "domain_prior", "active")} \
            | {"W": a["L1_ffn_W_base"], "b": a["L1_ffn_b_base"]}
        ffn(nc, "f0a", 0, x, ln, ident, consts, f0, a)
        attention(nc, "at0", 0, x, ln, ident, a)
        ffn(nc, "f0b", 0, x, ln, ident, consts, f0, a)
        ffn(nc, "f1a", 1, x, ln, ident, consts, f1, a)
        attention(nc, "at1", 1, x, ln, ident, a)
        ffn(nc, "f1b", 1, x, ln, ident, consts, f1, a, out)


def ffn(nc, name, kind, x, ln, ident, consts, ins, a, out=None):
    with ExitStack() as ctx:
        sb = lambda n, shape, dt=F32: ctx.enter_context(nc.sbuf_tensor(f"{name}_{n}", shape, dt))
        w_hi, w_lo = sb("w_hi", [P, KT, D], F32R), sb("w_lo", [P, KT, D], F32R)
        small_hi, small_lo = sb("small_hi", [P, KT, SMALL], F32R), sb("small_lo", [P, KT, SMALL], F32R)
        stack = sb("stack", [P, D], F32R)
        extra = {"out": out}
        if kind == 0:
            extra |= {"bias8": sb("bias8", [P, E0]), "limes_bd": sb("limes_bd", [P, NT, RANK]),
                      "tile_mask": sb("tile_mask", [P, NT]), "mask_table": a["c_tile_mask"],
                      "small": sb("small_out", [P, NT, 48])}
        else:
            extra |= {"logit_bias": sb("logit_bias", [P, E_ACT])}
        prepare_weights(nc, name + "w", ident, x, ln, [(ins["W"], D, w_hi, w_lo)])
        ffn_weights(nc, name + "s", ident, consts[:, kind, :], kind, w_hi, w_lo, small_hi, small_lo, stack,
                    extra, ins)
        ffn_loop(nc, name + "l", kind, x, ln, ident, w_hi, w_lo, small_hi, small_lo, stack, extra)
        if kind == 0:
            ffn0_route(nc, name + "r", x, ident, stack, extra)


_INS = ["L0_attn_hidden_states", "L0_attn_Wq", "L0_attn_Wk", "L0_attn_Wv", "L0_attn_Wo", "L0_ffn_W", "L0_ffn_b",
        "L0_ffn_A", "L0_ffn_Bmat", "L0_ffn_LiMEs", "L1_attn_wq", "L1_attn_wk", "L1_attn_wv", "L1_attn_wo",
        "L1_ffn_W_base", "L1_ffn_b_base", "L1_ffn_lora_A", "L1_ffn_lora_B", "L1_ffn_router_W", "L1_ffn_router_b",
        "L1_ffn_domain_prior", "L1_ffn_active"]


def shape_constants():
    p = np.arange(P)
    rows = np.zeros((P, 2, 16), np.float32)
    scale = (0.5, 2.0)
    for kind in range(2):
        rows[:, kind, 0] = np.where(p < ONES_AT, scale[kind], 1.0)
        lo = ((p >= 2 * RANK) & (p < ONES_AT)) | (p == ONES_AT + 1)
        rows[:, kind, 1] = ~lo
        rows[:, kind, 2] = lo
        rows[:, kind, 3] = p
        rows[:, kind, 4] = p // R1
        rows[:, kind, 8:16] = p[:, None] % R1 == np.arange(R1)
    half = HD // 2
    inv = (1.0 / 10000.0 ** (np.arange(0, HD, 2, dtype=np.float32) / np.float32(HD))).astype(np.float32)
    freqs = np.outer(np.arange(S, dtype=np.float32), inv).astype(np.float32)
    d = p % HD
    cos = np.cos(freqs).astype(np.float32)[:, d % half].T
    sin = np.sin(freqs).astype(np.float32)[:, d % half].T * np.where(d < half, -1.0, 1.0)[:, None]
    causal = np.zeros((P, S), np.float32)
    causal[:, S - P:] = np.where(p[:, None] < p[None, :], NEG, 0.0)
    grid = np.linspace(-6, 6, 120001)
    density = np.exp(-grid ** 2 / 2) / (2 * np.pi) ** 0.5
    share_below = np.cumsum(density) * (grid[1] - grid[0])
    select = np.zeros((P, TB - 1, 5), np.float32)
    for q in range(1, TB):
        for r in range(P):
            n = q * P + r + 1
            z = np.interp(1 - AIM / n, share_below, grid)
            select[r, q - 1, :4] = n, z, 1.1 * (q * P) ** 0.5, 1 / (n * np.interp(z, grid, density))
    return {"c_select": select, "c_ident": np.eye(P, dtype=np.float32), "c_rows": rows,
            "c_tile_mask": (p[:, None] // E0 == np.arange(NT)).astype(np.float32),
            "c_cos": np.ascontiguousarray(cos), "c_sin": np.ascontiguousarray(sin.astype(np.float32)),
            "c_causal": causal}


def kernel(**inputs):
    import concourse.bacc as _bacc
    from concourse import mybir as _mybir
    from concourse.bass_utils import run_bass_kernel_spmd as _run

    nc = _bacc.Bacc("TRN2", target_bir_lowering=False, num_devices=1)
    arrays, args = {}, {}
    for name, v in [(n, inputs[n]) for n in _INS] + list(shape_constants().items()):
        v = np.ascontiguousarray(v)
        arrays[f"in_{name}"] = v
        args[name] = nc.dram_tensor(f"in_{name}", v.shape, _mybir.dt.from_np(v.dtype), kind="ExternalInput").ap()
    out = nc.dram_tensor("out_x", (B, S, D), F32, kind="ExternalOutput").ap()
    build(nc, args, out)
    r = _run(nc, [arrays], core_ids=[0])
    return r.results[0]["out_x"]
```
